# Optimizing a Trainium2 kernel written in Bass

```python
import numpy as np
import jax
import jax.numpy as jnp

def _softmax(x, axis=-1):
    return jax.nn.softmax(x, axis=axis)

def _gelu(x):
    return jax.nn.gelu(x, approximate=True)

def _silu(x):
    return jax.nn.silu(x)

def _sigmoid(x):
    return jax.nn.sigmoid(x)

def _layernorm(x, axis=-1, eps=1e-05):
    m = jnp.mean(x, axis=axis, keepdims=True)
    v = jnp.var(x, axis=axis, keepdims=True)
    return (x - m) / jnp.sqrt(v + eps)

def _scatter_add(tgt, idx, src, axis=0):
    return tgt.at[idx].add(src)

def _segment_sum(src, seg, n):
    return jax.ops.segment_sum(src, seg, n)
kernel_name = 'mk_prb_d2_jaxref_r8_5c9521'

def setup_inputs(seed: int=0):
    np.random.seed(seed)
    _w = jnp.asarray

    def _L0_attn_setup():
        import jax, jax.numpy as jnp
        import numpy as np
        from jax import lax
        D_MODEL = 128
        EXPAND = 2
        D_INNER = EXPAND * D_MODEL
        D_STATE = 16
        D_CONV = 4
        DT_RANK = D_MODEL // 16
        B_SZ = 4
        SEQ = 256

        def _mamba_fwd(x, W_in, conv_w, conv_b, W_x, W_dt, b_dt, A_log, D, W_out):
            B, L, _ = x.shape
            xz = jnp.einsum('bld,ed->ble', x, W_in)
            u, z = jnp.split(xz, 2, axis=-1)
            u_nc = u.transpose(0, 2, 1)
            u_c = lax.conv_general_dilated(u_nc, conv_w[:, None, :], window_strides=(1,), padding=[(D_CONV - 1, 0)], feature_group_count=D_INNER, dimension_numbers=('NCH', 'OIH', 'NCH'))
            u_c = (u_c + conv_b[None, :, None]).transpose(0, 2, 1)
            u_c = jax.nn.silu(u_c)
            x_dbl = jnp.einsum('bld,ed->ble', u_c, W_x)
            dt_r, Bm, Cm = jnp.split(x_dbl, [DT_RANK, DT_RANK + D_STATE], axis=-1)
            dt = jax.nn.softplus(jnp.einsum('blr,dr->bld', dt_r, W_dt) + b_dt)
            A = -jnp.exp(A_log)

            def step(h, inp):
                dt_t, u_t, B_t, C_t = inp
                dA = jnp.exp(dt_t[..., None] * A)
                h = dA * h + (dt_t * u_t)[..., None] * B_t[:, None, :]
                y_t = jnp.einsum('bds,bs->bd', h, C_t)
                return (h, y_t)
            xs = (dt.transpose(1, 0, 2), u_c.transpose(1, 0, 2), Bm.transpose(1, 0, 2), Cm.transpose(1, 0, 2))
            h0 = jnp.zeros((B, D_INNER, D_STATE), dtype=x.dtype)
            _, ys = lax.scan(step, h0, xs)
            y = ys.transpose(1, 0, 2)
            y = y + u_c * D
            y = y * jax.nn.silu(z)
            out = jnp.einsum('bld,ed->ble', y, W_out)
            return out

        def _reference_tuple_inner(x, W_in, conv_w, conv_b, W_x, W_dt, b_dt, A_log, D, W_out):
            out = _mamba_fwd(x, W_in, conv_w, conv_b, W_x, W_dt, b_dt, A_log, D, W_out)
            return (out, None)
        key = jax.random.key(seed)
        ks = jax.random.split(key, 10)
        s = lambda k, shape, scale: jax.random.normal(k, shape, dtype=jnp.float32) * scale
        inp = {'x': s(ks[0], (B_SZ, SEQ, D_MODEL), 1.0), 'W_in': s(ks[1], (2 * D_INNER, D_MODEL), D_MODEL ** (-0.5)), 'conv_w': s(ks[2], (D_INNER, D_CONV), D_CONV ** (-0.5)), 'conv_b': s(ks[3], (D_INNER,), 0.02), 'W_x': s(ks[4], (DT_RANK + 2 * D_STATE, D_INNER), D_INNER ** (-0.5)), 'W_dt': s(ks[5], (D_INNER, DT_RANK), DT_RANK ** (-0.5)), 'b_dt': s(ks[6], (D_INNER,), 0.5), 'A_log': jnp.log(jnp.broadcast_to(jnp.arange(1, D_STATE + 1, dtype=jnp.float32), (D_INNER, D_STATE))), 'D': jnp.ones((D_INNER,), dtype=jnp.float32), 'W_out': s(ks[7], (D_MODEL, D_INNER), D_INNER ** (-0.5))}
        return inp
    _L0_attn_in = _L0_attn_setup()

    def _L0_ffn_setup():
        import jax, jax.numpy as jnp
        import numpy as np
        DIM = 128
        DEPTH = 6
        HEADS = 16
        DIM_HEAD = 64
        WINDOW = 32
        INNER = HEADS * DIM_HEAD
        DIM_INNER = int(DIM * 4 * 2 / 3)
        QK_SCALE = 8.0

        def shift_tokens(t):
            a, s = jnp.split(t, 2, -1)
            s = jnp.pad(s, ((0, 0), (1, 0), (0, 0)))[:, :-1]
            return jnp.concatenate([a, s], -1)

        def l2norm(t):
            return t / jnp.maximum(jnp.linalg.norm(t, axis=-1, keepdims=True), 1e-12)

        def rotate_half(x):
            x1, x2 = jnp.split(x, 2, -1)
            return jnp.concatenate([-x2, x1], -1)

        def rotary_tables(n):
            half = jnp.arange(0, DIM_HEAD, 2, dtype=jnp.float32)
            inv_freq = 1.0 / 10000.0 ** (half / DIM_HEAD)
            t = jnp.arange(n, dtype=jnp.float32)
            freqs = t[:, None] * inv_freq[None, :]
            freqs = jnp.concatenate([freqs, freqs], -1)
            base_scale = (half + 0.4 * DIM_HEAD) / (1.4 * DIM_HEAD)
            power = (t - n // 2) / (WINDOW // 2)
            scale = base_scale[None, :] ** power[:, None]
            scale = jnp.concatenate([scale, scale], -1)
            return (freqs, scale)

        def local_attention(q, k, v):
            b, h, n, d = q.shape
            w = WINDOW
            nw = n // w
            bq = q.reshape(b, h, nw, w, d)
            bk = k.reshape(b, h, nw, w, d)
            bv = v.reshape(b, h, nw, w, d)

            def look(t):
                p = jnp.pad(t, ((0, 0), (0, 0), (1, 0), (0, 0), (0, 0)))
                return jnp.concatenate([p[:, :, :nw], p[:, :, 1:]], axis=3)
            bk2, bv2 = (look(bk), look(bv))
            seq = jnp.arange(n).reshape(nw, w)
            seq_p = jnp.pad(seq, ((1, 0), (0, 0)), constant_values=-1)
            jt = jnp.concatenate([seq_p[:nw], seq_p[1:]], axis=1)
            it = seq[:, :, None]
            jb = jt[:, None, :]
            mask = (it < jb) | (it > jb + w) | (jb == -1)
            sim = jnp.einsum('bhwie,bhwje->bhwij', bq, bk2) * QK_SCALE
            sim = jnp.where(mask, -jnp.finfo(sim.dtype).max, sim)
            attn = jax.nn.softmax(sim, -1)
            out = jnp.einsum('bhwij,bhwje->bhwie', attn, bv2)
            return out.reshape(b, h, n, d)

        def attn_layer(x, Wqkv, qs, ksc, Wo):
            b, n, _ = x.shape
            qkv = x @ Wqkv
            q, k, v = jnp.split(qkv, 3, -1)
            sh = lambda t: t.reshape(b, n, HEADS, DIM_HEAD).transpose(0, 2, 1, 3)
            q, k, v = (sh(q), sh(k), sh(v))
            q = l2norm(q) * qs
            k = l2norm(k) * ksc
            freqs, scale = rotary_tables(n)
            cos, sin = (jnp.cos(freqs), jnp.sin(freqs))
            q = q * cos * scale + rotate_half(q) * sin * scale
            inv = 1.0 / scale
            k = k * cos * inv + rotate_half(k) * sin * inv
            out = local_attention(q, k, v)
            out = out.transpose(0, 2, 1, 3).reshape(b, n, INNER)
            return out @ Wo

        def ffn_layer(x, g, bln, W1, b1, W2, b2):
            mu = x.mean(-1, keepdims=True)
            var = ((x - mu) ** 2).mean(-1, keepdims=True)
            xn = (x - mu) / jnp.sqrt(var + 1e-05) * g + bln
            hg = xn @ W1 + b1
            a, gate = jnp.split(hg, 2, -1)
            return a * jax.nn.gelu(gate, approximate=False) @ W2 + b2
        key = jax.random.key(seed)
        ks = jax.random.split(key, 8)
        B, N = (2, 256)
        init = lambda k, shape: jax.random.normal(k, shape, jnp.float32) * 0.02
        return {'x': jax.random.normal(ks[0], (B, N, DIM), jnp.float32), 'Wqkv': init(ks[1], (DEPTH, DIM, 3 * INNER)), 'q_scale': jnp.ones((DEPTH, DIM_HEAD), jnp.float32), 'k_scale': jnp.ones((DEPTH, DIM_HEAD), jnp.float32), 'Wo': init(ks[2], (DEPTH, INNER, DIM)), 'ln_g': jnp.ones((DEPTH, DIM), jnp.float32), 'ln_b': jnp.zeros((DEPTH, DIM), jnp.float32), 'W1': init(ks[3], (DEPTH, DIM, 2 * DIM_INNER)), 'b1': jnp.zeros((DEPTH, 2 * DIM_INNER), jnp.float32), 'W2': init(ks[4], (DEPTH, DIM_INNER, DIM)), 'b2': jnp.zeros((DEPTH, DIM), jnp.float32)}
    _L0_ffn_in = _L0_ffn_setup()

    def _L1_attn_setup():
        import jax, jax.numpy as jnp
        import numpy as np
        B, T, C = (2, 256, 128)
        NH = 16
        HS = C // NH
        BD = max(HS // 4, 16)
        HORIZON = 64
        key = jax.random.key(seed)
        ks = jax.random.split(key, 10)
        s = 0.02
        return {'x': jax.random.normal(ks[0], (B, T, C), dtype=jnp.float32), 'W_disp': jax.random.normal(ks[1], (NH * BD, C), dtype=jnp.float32) * s, 'W_val': jax.random.normal(ks[2], (C, C), dtype=jnp.float32) * s, 'rel_pos_emb': jax.random.normal(ks[3], (HORIZON, BD), dtype=jnp.float32) * s, 'strain_fused_w': jax.random.normal(ks[4], (2 * BD, BD), dtype=jnp.float32) * s, 'strain_fused_b': jnp.zeros((2 * BD,), dtype=jnp.float32), 'pos_proj_w': jax.random.normal(ks[5], (BD, BD), dtype=jnp.float32) * s, 'bond_out_w': jax.random.normal(ks[6], (1, BD), dtype=jnp.float32) * s, 'damage_out_w': jax.random.normal(ks[7], (1, BD), dtype=jnp.float32) * s, 'damage_out_b': jnp.full((1,), -3.0, dtype=jnp.float32), 'c_proj_w': jax.random.normal(ks[8], (C, C), dtype=jnp.float32) * s}
    _L1_attn_in = _L1_attn_setup()

    def _L1_ffn_setup():
        import jax, jax.numpy as jnp
        import numpy as np
        from jax import lax
        HIDDEN = 128
        INTER = 64
        E = 64
        K = 6
        G = 8
        TG = 4
        NSH = 2
        ISH = INTER * NSH

        def _moe_forward(hidden_states, gate_w, gate_bias, eg_w, eu_w, ed_w, sg_w, su_w, sd_w):
            B, S, H = hidden_states.shape
            x = hidden_states.reshape(-1, H)
            T = x.shape[0]
            shared = jax.nn.silu(x @ sg_w.T) * (x @ su_w.T) @ sd_w.T
            logits = x @ gate_w.T
            scores = jax.nn.sigmoid(logits) + gate_bias
            group_scores = scores.reshape(T, G, E // G).max(axis=-1)
            _, sel_groups = lax.top_k(group_scores, TG)
            group_mask = jnp.zeros((T, G), scores.dtype).at[jnp.arange(T)[:, None], sel_groups].set(1.0)
            mask = jnp.repeat(group_mask, E // G, axis=1)
            masked_scores = scores * mask
            topk_w, topk_i = lax.top_k(masked_scores, K)
            topk_w = topk_w / (topk_w.sum(axis=-1, keepdims=True) + 1e-08)
            comb = jnp.zeros((T, E), x.dtype).at[jnp.arange(T)[:, None], topk_i].add(topk_w)
            h = jax.nn.silu(jnp.einsum('th,eih->eti', x, eg_w)) * jnp.einsum('th,eih->eti', x, eu_w)
            routed = jnp.einsum('eti,ehi,te->th', h, ed_w, comb)
            return (shared + routed).reshape(B, S, H)
        key = jax.random.key(seed)
        ks = jax.random.split(key, 9)
        s = 0.02
        return {'hidden_states': jax.random.normal(ks[0], (1, 128, HIDDEN), jnp.float32), 'gate_w': jax.random.normal(ks[1], (E, HIDDEN), jnp.float32) * s, 'gate_bias': jnp.zeros((E,), jnp.float32), 'eg_w': jax.random.normal(ks[2], (E, INTER, HIDDEN), jnp.float32) * s, 'eu_w': jax.random.normal(ks[3], (E, INTER, HIDDEN), jnp.float32) * s, 'ed_w': jax.random.normal(ks[4], (E, HIDDEN, INTER), jnp.float32) * s, 'sg_w': jax.random.normal(ks[5], (ISH, HIDDEN), jnp.float32) * s, 'su_w': jax.random.normal(ks[6], (ISH, HIDDEN), jnp.float32) * s, 'sd_w': jax.random.normal(ks[7], (HIDDEN, ISH), jnp.float32) * s}
    _L1_ffn_in = _L1_ffn_setup()
    _d = {'L0_attn_x': _L0_attn_in['x'], 'L0_attn_W_in': _L0_attn_in['W_in'], 'L0_attn_conv_w': _L0_attn_in['conv_w'], 'L0_attn_conv_b': _L0_attn_in['conv_b'], 'L0_attn_W_x': _L0_attn_in['W_x'], 'L0_attn_W_dt': _L0_attn_in['W_dt'], 'L0_attn_b_dt': _L0_attn_in['b_dt'], 'L0_attn_A_log': _L0_attn_in['A_log'], 'L0_attn_D': _L0_attn_in['D'], 'L0_attn_W_out': _L0_attn_in['W_out'], 'L0_ffn_Wqkv': _L0_ffn_in['Wqkv'], 'L0_ffn_q_scale': _L0_ffn_in['q_scale'], 'L0_ffn_k_scale': _L0_ffn_in['k_scale'], 'L0_ffn_Wo': _L0_ffn_in['Wo'], 'L0_ffn_ln_g': _L0_ffn_in['ln_g'], 'L0_ffn_ln_b': _L0_ffn_in['ln_b'], 'L0_ffn_W1': _L0_ffn_in['W1'], 'L0_ffn_b1': _L0_ffn_in['b1'], 'L0_ffn_W2': _L0_ffn_in['W2'], 'L0_ffn_b2': _L0_ffn_in['b2'], 'L1_attn_W_disp': _L1_attn_in['W_disp'], 'L1_attn_W_val': _L1_attn_in['W_val'], 'L1_attn_rel_pos_emb': _L1_attn_in['rel_pos_emb'], 'L1_attn_strain_fused_w': _L1_attn_in['strain_fused_w'], 'L1_attn_strain_fused_b': _L1_attn_in['strain_fused_b'], 'L1_attn_pos_proj_w': _L1_attn_in['pos_proj_w'], 'L1_attn_bond_out_w': _L1_attn_in['bond_out_w'], 'L1_attn_damage_out_w': _L1_attn_in['damage_out_w'], 'L1_attn_damage_out_b': _L1_attn_in['damage_out_b'], 'L1_attn_c_proj_w': _L1_attn_in['c_proj_w'], 'L1_ffn_gate_w': _L1_ffn_in['gate_w'], 'L1_ffn_gate_bias': _L1_ffn_in['gate_bias'], 'L1_ffn_eg_w': _L1_ffn_in['eg_w'], 'L1_ffn_eu_w': _L1_ffn_in['eu_w'], 'L1_ffn_ed_w': _L1_ffn_in['ed_w'], 'L1_ffn_sg_w': _L1_ffn_in['sg_w'], 'L1_ffn_su_w': _L1_ffn_in['su_w'], 'L1_ffn_sd_w': _L1_ffn_in['sd_w']}
    _x0 = _d['L0_attn_x']
    _d['L0_attn_x'] = jax.random.normal(jax.random.fold_in(jax.random.key(seed), 1), (8, 512, 128), dtype=_x0.dtype)
    del _x0
    return _d

def reference(L0_attn_x, L0_attn_W_in, L0_attn_conv_w, L0_attn_conv_b, L0_attn_W_x, L0_attn_W_dt, L0_attn_b_dt, L0_attn_A_log, L0_attn_D, L0_attn_W_out, L0_ffn_Wqkv, L0_ffn_q_scale, L0_ffn_k_scale, L0_ffn_Wo, L0_ffn_ln_g, L0_ffn_ln_b, L0_ffn_W1, L0_ffn_b1, L0_ffn_W2, L0_ffn_b2, L1_attn_W_disp, L1_attn_W_val, L1_attn_rel_pos_emb, L1_attn_strain_fused_w, L1_attn_strain_fused_b, L1_attn_pos_proj_w, L1_attn_bond_out_w, L1_attn_damage_out_w, L1_attn_damage_out_b, L1_attn_c_proj_w, L1_ffn_gate_w, L1_ffn_gate_bias, L1_ffn_eg_w, L1_ffn_eu_w, L1_ffn_ed_w, L1_ffn_sg_w, L1_ffn_su_w, L1_ffn_sd_w):

    def _L0_attn_ref(x, W_in, conv_w, conv_b, W_x, W_dt, b_dt, A_log, D, W_out):
        import jax, jax.numpy as jnp
        import numpy as np
        from jax import lax
        D_MODEL = 128
        EXPAND = 2
        D_INNER = EXPAND * D_MODEL
        D_STATE = 16
        D_CONV = 4
        DT_RANK = D_MODEL // 16
        B_SZ = 4
        SEQ = 256

        def _mamba_fwd(x, W_in, conv_w, conv_b, W_x, W_dt, b_dt, A_log, D, W_out):
            B, L, _ = x.shape
            xz = jnp.einsum('bld,ed->ble', x, W_in)
            u, z = jnp.split(xz, 2, axis=-1)
            u_nc = u.transpose(0, 2, 1)
            u_c = lax.conv_general_dilated(u_nc, conv_w[:, None, :], window_strides=(1,), padding=[(D_CONV - 1, 0)], feature_group_count=D_INNER, dimension_numbers=('NCH', 'OIH', 'NCH'))
            u_c = (u_c + conv_b[None, :, None]).transpose(0, 2, 1)
            u_c = jax.nn.silu(u_c)
            x_dbl = jnp.einsum('bld,ed->ble', u_c, W_x)
            dt_r, Bm, Cm = jnp.split(x_dbl, [DT_RANK, DT_RANK + D_STATE], axis=-1)
            dt = jax.nn.softplus(jnp.einsum('blr,dr->bld', dt_r, W_dt) + b_dt)
            A = -jnp.exp(A_log)

            def step(h, inp):
                dt_t, u_t, B_t, C_t = inp
                dA = jnp.exp(dt_t[..., None] * A)
                h = dA * h + (dt_t * u_t)[..., None] * B_t[:, None, :]
                y_t = jnp.einsum('bds,bs->bd', h, C_t)
                return (h, y_t)
            xs = (dt.transpose(1, 0, 2), u_c.transpose(1, 0, 2), Bm.transpose(1, 0, 2), Cm.transpose(1, 0, 2))
            h0 = jnp.zeros((B, D_INNER, D_STATE), dtype=x.dtype)
            _, ys = lax.scan(step, h0, xs)
            y = ys.transpose(1, 0, 2)
            y = y + u_c * D
            y = y * jax.nn.silu(z)
            out = jnp.einsum('bld,ed->ble', y, W_out)
            return out

        def _reference_tuple_inner(x, W_in, conv_w, conv_b, W_x, W_dt, b_dt, A_log, D, W_out):
            out = _mamba_fwd(x, W_in, conv_w, conv_b, W_x, W_dt, b_dt, A_log, D, W_out)
            return (out, None)
        return _reference_tuple_inner(x, W_in, conv_w, conv_b, W_x, W_dt, b_dt, A_log, D, W_out)[0]

    def _L0_ffn_ref(x, Wqkv, q_scale, k_scale, Wo, ln_g, ln_b, W1, b1, W2, b2):
        import jax, jax.numpy as jnp
        import numpy as np
        DIM = 128
        DEPTH = 6
        HEADS = 16
        DIM_HEAD = 64
        WINDOW = 32
        INNER = HEADS * DIM_HEAD
        DIM_INNER = int(DIM * 4 * 2 / 3)
        QK_SCALE = 8.0

        def shift_tokens(t):
            a, s = jnp.split(t, 2, -1)
            s = jnp.pad(s, ((0, 0), (1, 0), (0, 0)))[:, :-1]
            return jnp.concatenate([a, s], -1)

        def l2norm(t):
            return t / jnp.maximum(jnp.linalg.norm(t, axis=-1, keepdims=True), 1e-12)

        def rotate_half(x):
            x1, x2 = jnp.split(x, 2, -1)
            return jnp.concatenate([-x2, x1], -1)

        def rotary_tables(n):
            half = jnp.arange(0, DIM_HEAD, 2, dtype=jnp.float32)
            inv_freq = 1.0 / 10000.0 ** (half / DIM_HEAD)
            t = jnp.arange(n, dtype=jnp.float32)
            freqs = t[:, None] * inv_freq[None, :]
            freqs = jnp.concatenate([freqs, freqs], -1)
            base_scale = (half + 0.4 * DIM_HEAD) / (1.4 * DIM_HEAD)
            power = (t - n // 2) / (WINDOW // 2)
            scale = base_scale[None, :] ** power[:, None]
            scale = jnp.concatenate([scale, scale], -1)
            return (freqs, scale)

        def local_attention(q, k, v):
            b, h, n, d = q.shape
            w = WINDOW
            nw = n // w
            bq = q.reshape(b, h, nw, w, d)
            bk = k.reshape(b, h, nw, w, d)
            bv = v.reshape(b, h, nw, w, d)

            def look(t):
                p = jnp.pad(t, ((0, 0), (0, 0), (1, 0), (0, 0), (0, 0)))
                return jnp.concatenate([p[:, :, :nw], p[:, :, 1:]], axis=3)
            bk2, bv2 = (look(bk), look(bv))
            seq = jnp.arange(n).reshape(nw, w)
            seq_p = jnp.pad(seq, ((1, 0), (0, 0)), constant_values=-1)
            jt = jnp.concatenate([seq_p[:nw], seq_p[1:]], axis=1)
            it = seq[:, :, None]
            jb = jt[:, None, :]
            mask = (it < jb) | (it > jb + w) | (jb == -1)
            sim = jnp.einsum('bhwie,bhwje->bhwij', bq, bk2) * QK_SCALE
            sim = jnp.where(mask, -jnp.finfo(sim.dtype).max, sim)
            attn = jax.nn.softmax(sim, -1)
            out = jnp.einsum('bhwij,bhwje->bhwie', attn, bv2)
            return out.reshape(b, h, n, d)

        def attn_layer(x, Wqkv, qs, ksc, Wo):
            b, n, _ = x.shape
            qkv = x @ Wqkv
            q, k, v = jnp.split(qkv, 3, -1)
            sh = lambda t: t.reshape(b, n, HEADS, DIM_HEAD).transpose(0, 2, 1, 3)
            q, k, v = (sh(q), sh(k), sh(v))
            q = l2norm(q) * qs
            k = l2norm(k) * ksc
            freqs, scale = rotary_tables(n)
            cos, sin = (jnp.cos(freqs), jnp.sin(freqs))
            q = q * cos * scale + rotate_half(q) * sin * scale
            inv = 1.0 / scale
            k = k * cos * inv + rotate_half(k) * sin * inv
            out = local_attention(q, k, v)
            out = out.transpose(0, 2, 1, 3).reshape(b, n, INNER)
            return out @ Wo

        def ffn_layer(x, g, bln, W1, b1, W2, b2):
            mu = x.mean(-1, keepdims=True)
            var = ((x - mu) ** 2).mean(-1, keepdims=True)
            xn = (x - mu) / jnp.sqrt(var + 1e-05) * g + bln
            hg = xn @ W1 + b1
            a, gate = jnp.split(hg, 2, -1)
            return a * jax.nn.gelu(gate, approximate=False) @ W2 + b2
        for i in range(DEPTH):
            x = attn_layer(shift_tokens(x), Wqkv[i], q_scale[i], k_scale[i], Wo[i]) + x
            x = ffn_layer(shift_tokens(x), ln_g[i], ln_b[i], W1[i], b1[i], W2[i], b2[i]) + x
        return x

    def _L1_attn_ref(x, W_disp, W_val, rel_pos_emb, strain_fused_w, strain_fused_b, pos_proj_w, bond_out_w, damage_out_w, damage_out_b, c_proj_w):
        import jax, jax.numpy as jnp
        import numpy as np
        B, T, C = (2, 256, 128)
        NH = 16
        HS = C // NH
        BD = max(HS // 4, 16)
        HORIZON = 64
        Bx, Tx, Cx = x.shape
        delta = min(HORIZON, Tx)
        gelu = lambda t: jax.nn.gelu(t, approximate=False)
        disp = (x @ W_disp.T).reshape(Bx, Tx, NH, BD).transpose(0, 2, 1, 3)
        val = (x @ W_val.T).reshape(Bx, Tx, NH, HS).transpose(0, 2, 1, 3)
        pad = ((0, 0), (0, 0), (delta - 1, 0), (0, 0))
        idx = jnp.arange(Tx)[:, None] + jnp.arange(delta)[None, :]
        disp_win = jnp.pad(disp, pad)[:, :, idx, :]
        strain = disp_win - disp[:, :, :, None, :]
        fused = strain @ strain_fused_w.T + strain_fused_b
        bond_feats, damage_feats = (fused[..., :BD], fused[..., BD:])
        pos_feat = rel_pos_emb[:delta] @ pos_proj_w.T
        bond_logits = (gelu(bond_feats + pos_feat) @ bond_out_w.T)[..., 0]
        damage = jax.nn.sigmoid((gelu(damage_feats) @ damage_out_w.T)[..., 0] + damage_out_b)
        logits = bond_logits - damage * 10.0
        cmask = jnp.arange(Tx)[:, None] - delta + 1 + jnp.arange(delta)[None, :] >= 0
        logits = jnp.where(cmask, logits, -jnp.inf)
        weights = jax.nn.softmax(logits, axis=-1)
        val_win = jnp.pad(val, pad)[:, :, idx, :]
        out = jnp.einsum('bhtw,bhtwd->bhtd', weights, val_win)
        out = out.transpose(0, 2, 1, 3).reshape(Bx, Tx, Cx)
        return out @ c_proj_w.T

    def _L1_ffn_ref(hidden_states, gate_w, gate_bias, eg_w, eu_w, ed_w, sg_w, su_w, sd_w):
        import jax, jax.numpy as jnp
        import numpy as np
        from jax import lax
        HIDDEN = 128
        INTER = 64
        E = 64
        K = 6
        G = 8
        TG = 4
        NSH = 2
        ISH = INTER * NSH

        def _moe_forward(hidden_states, gate_w, gate_bias, eg_w, eu_w, ed_w, sg_w, su_w, sd_w):
            B, S, H = hidden_states.shape
            x = hidden_states.reshape(-1, H)
            T = x.shape[0]
            shared = jax.nn.silu(x @ sg_w.T) * (x @ su_w.T) @ sd_w.T
            logits = x @ gate_w.T
            scores = jax.nn.sigmoid(logits) + gate_bias
            group_scores = scores.reshape(T, G, E // G).max(axis=-1)
            _, sel_groups = lax.top_k(group_scores, TG)
            group_mask = jnp.zeros((T, G), scores.dtype).at[jnp.arange(T)[:, None], sel_groups].set(1.0)
            mask = jnp.repeat(group_mask, E // G, axis=1)
            masked_scores = scores * mask
            topk_w, topk_i = lax.top_k(masked_scores, K)
            topk_w = topk_w / (topk_w.sum(axis=-1, keepdims=True) + 1e-08)
            comb = jnp.zeros((T, E), x.dtype).at[jnp.arange(T)[:, None], topk_i].add(topk_w)
            h = jax.nn.silu(jnp.einsum('th,eih->eti', x, eg_w)) * jnp.einsum('th,eih->eti', x, eu_w)
            routed = jnp.einsum('eti,ehi,te->th', h, ed_w, comb)
            return (shared + routed).reshape(B, S, H)
        return _moe_forward(hidden_states, gate_w, gate_bias, eg_w, eu_w, ed_w, sg_w, su_w, sd_w)
    x = L0_attn_x
    xn = _layernorm(x, axis=-1)
    x = x + _L0_attn_ref(xn, L0_attn_W_in, L0_attn_conv_w, L0_attn_conv_b, L0_attn_W_x, L0_attn_W_dt, L0_attn_b_dt, L0_attn_A_log, L0_attn_D, L0_attn_W_out) + _L0_ffn_ref(xn, L0_ffn_Wqkv, L0_ffn_q_scale, L0_ffn_k_scale, L0_ffn_Wo, L0_ffn_ln_g, L0_ffn_ln_b, L0_ffn_W1, L0_ffn_b1, L0_ffn_W2, L0_ffn_b2)
    xn = _layernorm(x, axis=-1)
    x = x + _L1_attn_ref(xn, L1_attn_W_disp, L1_attn_W_val, L1_attn_rel_pos_emb, L1_attn_strain_fused_w, L1_attn_strain_fused_b, L1_attn_pos_proj_w, L1_attn_bond_out_w, L1_attn_damage_out_w, L1_attn_damage_out_b, L1_attn_c_proj_w) + _L1_ffn_ref(xn, L1_ffn_gate_w, L1_ffn_gate_bias, L1_ffn_eg_w, L1_ffn_eu_w, L1_ffn_ed_w, L1_ffn_sg_w, L1_ffn_su_w, L1_ffn_sd_w)
    return x

_drawn_inputs = setup_inputs


def setup_inputs(seed=0):
    import zlib

    import numpy as np

    out = dict(_drawn_inputs(seed))
    spreads = {'L0_attn_D': (1.0, 0.6),
     'L0_ffn_q_scale': (1.0, 0.6),
     'L0_ffn_k_scale': (1.0, 0.6),
     'L0_ffn_ln_g': (1.0, 0.6),
     'L0_ffn_ln_b': (0.0, 0.8),
     'L0_ffn_b1': (0.0, 0.8),
     'L0_ffn_b2': (0.0, 0.1),
     'L1_attn_strain_fused_b': (0.0, 2.0),
     'L1_ffn_gate_bias': (0.0, 0.8)}
    factors = {'L0_attn_conv_b': 15.222,
     'L0_ffn_W1': 3.922,
     'L0_ffn_W2': 3.852,
     'L1_attn_W_disp': 8.0,
     'L1_attn_W_val': 8.0,
     'L1_attn_rel_pos_emb': 64.0,
     'L1_attn_strain_fused_w': 8.0,
     'L1_attn_pos_proj_w': 64.0,
     'L1_attn_bond_out_w': 8.0,
     'L1_attn_damage_out_w': 64.0,
     'L1_attn_c_proj_w': 8.0,
     'L1_ffn_gate_w': 8.0,
     'L1_ffn_eg_w': 8.0,
     'L1_ffn_eu_w': 8.0,
     'L1_ffn_ed_w': 8.0,
     'L1_ffn_sg_w': 8.0,
     'L1_ffn_su_w': 8.0,
     'L1_ffn_sd_w': 8.0,
     'L0_attn_A_log': 2.844}
    for name, (base, spread) in spreads.items():
        noise = np.random.default_rng([zlib.crc32(name.encode()), seed]).standard_normal(out[name].shape)
        drawn = base * np.exp(spread * noise) if base else spread * noise
        out[name] = jnp.asarray(drawn.astype(out[name].dtype))
    for name, factor in factors.items():
        out[name] = (out[name] * factor).astype(out[name].dtype)
    return out
```

```python
from contextlib import ExitStack

import numpy as np

import concourse.bass as bass
from concourse import mybir

F32 = mybir.dt.float32
BF16 = mybir.dt.bfloat16
I32 = mybir.dt.int32
ALU = mybir.AluOpType
ACT = mybir.ActivationFunctionType
AX = mybir.AxisListType.X

P = 128
NB = 8
L = 512
NT = L // P
EPS = 1e-5
BASE = 4
PHASES = ("norm", "mamba", "ffn", "norm", "attn", "moe")


class Chain:

    def __init__(self, eng, sem, per):
        self.eng, self.sem, self.per, self.n, self.base = eng, sem, per, 0, 0

    def start(self, step):
        self.n, self.base = 0, step * self.per

    def tick(self, ins):
        self.n += 1
        ins.then_inc(self.sem, 1)

    def wait(self):
        self.eng.wait_ge(self.sem, BASE + self.base + self.n)

    def link(self, ins):
        self.tick(ins)
        self.wait()

    def end(self):
        assert self.n == self.per, (self.sem, self.n)


def settle(eng, sem):
    eng.sem_inc(sem, 1)


class Stage:

    def __init__(self, nc, ctx, name):
        self.nc, self.ctx, self.name = nc, ctx, name

    def sb(self, name, shape, dt=F32):
        return self.ctx.enter_context(self.nc.sbuf_tensor(f"{self.name}_{name}", shape, dt))

    def banks(self, name, n):
        return self.ctx.enter_context(self.nc.psum_tensor(f"{self.name}_{name}", [P, n, 512], F32))

    def sems(self, names):
        q = {n: self.ctx.enter_context(self.nc.semaphore(f"{self.name}_{n}")) for n in names.split()}
        with self.nc.Block() as block:
            @block.sync
            def _(sp):
                for sem in q.values():
                    sp.sem_inc(sem, BASE)
        return q


RSQRT_LINKS = 12


def rsqrt(dve, chain, out, var, half, tmp):
    chain.link(dve.tensor_scalar(out.bitcast(I32), var.bitcast(I32), 1, None, ALU.logical_shift_right))
    chain.link(dve.tensor_scalar(out.bitcast(I32), out.bitcast(I32), -1.0, float(0x5F3759DF), ALU.mult, ALU.add))
    chain.link(dve.tensor_scalar(half, var, -0.5, None, ALU.mult))
    for _ in range(3):
        chain.link(dve.tensor_tensor(tmp, out, out, ALU.mult))
        chain.link(dve.tensor_tensor(tmp, tmp, half, ALU.mult))
        chain.link(dve.scalar_tensor_tensor(out=out, in0=tmp, scalar=1.5, in1=out, op0=ALU.add, op1=ALU.mult))


def layernorm_stage(nc, g, name):
    acc, xn, ident = g["acc"], g["xn"], g["ident"]
    with ExitStack() as ctx:
        s = Stage(nc, ctx, name)
        xs = s.sb("xs", [P, L])
        stats = s.sb("stats", [P, NT, 6])
        mv = s.sb("mv", [P, NT, 2])
        rstd = s.sb("rstd", [P, NT])
        half = s.sb("half", [P, NT])
        tmp = s.sb("tmp", [P, NT])
        xh = s.sb("xh", [P, NT, P])
        tok = s.banks("tok", 1)
        fea = s.banks("fea", 1)
        q = s.sems("copied turned normed back stored dch")
        copied, turned, normed, back, stored, dch = q.values()
        with nc.Block() as block:
            @block.scalar
            def _(act):
                with act.Fori(0, NB) as b:
                    act.wait_ge(turned, BASE + b)
                    act.activation(xs[:, :], acc[:, b, :], ACT.Copy).then_inc(copied, 1)
                    act.wait_ge(back, BASE + b + 1)
                    act.activation(xn[:, b, :], fea[:, 0, :], ACT.Copy).then_inc(stored, 1)

            @block.tensor
            def _(pe):
                with pe.Fori(0, NB) as b:
                    pe.wait_ge(copied, BASE + b + 1)
                    for k in range(NT):
                        mm = pe.transpose(tok[:, 0, k * P:(k + 1) * P], xs[:, k * P:(k + 1) * P], ident[:, :])
                    mm.then_inc(turned, 1)
                    pe.wait_ge(normed, BASE + b + 1)
                    pe.wait_ge(stored, BASE + b)
                    for k in range(NT):
                        mm = pe.transpose(fea[:, 0, k * P:(k + 1) * P], xh[:, k, :], ident[:, :])
                    mm.then_inc(back, 1)

            @block.vector
            def _(dve):
                c = Chain(dve, dch, 2 * NT + 1 + RSQRT_LINKS)
                with dve.Fori(0, NB) as b:
                    c.start(b)
                    dve.wait_ge(turned, BASE + b + 1)
                    for k in range(NT):
                        c.tick(dve.bn_stats(stats[:, k, :], tok[:, 0, k * P:(k + 1) * P]))
                    c.wait()
                    dve.memset(tmp[:, :], 0.0)
                    for k in range(NT):
                        c.tick(dve.bn_aggr(mv[:, k, :], stats[:, k, :]))
                    c.wait()
                    c.link(dve.tensor_scalar(mv[:, :, 1], mv[:, :, 1], EPS, None, ALU.add))
                    rsqrt(dve, c, rstd[:, :], mv[:, :, 1], half[:, :], tmp[:, :])
                    for k in range(NT):
                        ins = dve.tensor_scalar(xh[:, k, :], tok[:, 0, k * P:(k + 1) * P], mv[:, k, 0:1],
                                                rstd[:, k:k + 1], ALU.subtract, ALU.mult)
                    ins.then_inc(normed, 1)
                    c.end()


DI, DS, DC, DR = 256, 16, 4, 8


def mamba_stage(nc, g, d):
    acc, xn, ident = g["acc"], g["xn"], g["ident"]
    NH = DI // P
    NX = DR + 2 * DS
    with ExitStack() as ctx:
        s = Stage(nc, ctx, "ma")
        w_in = s.sb("w_in", [P, 2 * DI])
        w_x = s.sb("w_x", [P, NH, NX])
        w_dt = s.sb("w_dt", [DR, DI])
        w_out = s.sb("w_out", [P, NH, P])
        par = s.sb("par", [P, NH, DC + 3])
        alog = s.sb("alog", [P, NH, DS])
        aexp = s.sb("aexp", [P, NH, DS])
        u = s.sb("u", [P, NH, DC - 1 + L])
        cv = s.sb("cv", [P, NH, L])
        uc = s.sb("uc", [P, NH, L])
        zg = s.sb("zg", [P, NH, L])
        xd = s.sb("xd", [NX, L])
        v = s.sb("v", [P, NH, L])
        e = s.sb("e", [P, NH, L])
        dt = s.sb("dt", [P, NH, L])
        dtu = s.sb("dtu", [P, NH, L])
        bs = s.sb("bs", [P, 2, L])
        da = s.sb("da", [P, 4, L])
        db = s.sb("db", [P, 4, L])
        h = s.sb("h", [P, 2, L])
        hc = s.sb("hc", [P, 4, L])
        y = s.sb("y", [P, NH, L])
        BC = s.banks("BC", 4)
        Y = s.banks("Y", 2)
        M = s.banks("M", 2)
        q = s.sems("loaded aready acopy uzdone uread zread upad conv ucdone xdone xread dtdone dtread dtready "
                   "dtuready bcdone bcopied bfree cfree daready dafree dbready dbfree hcready hcfree ydone yread outdone "
                   "outread dch ach")
        NS = DS * NH
        with nc.Block() as block:
            @block.sync
            def _(sp):
                for dst, src in ((w_in, "m_w_in"), (w_x, "m_w_x"), (w_dt, "m_w_dt"), (w_out, "m_w_out"),
                                 (par, "m_par"), (alog, "m_alog")):
                    sp.dma_start(dst[:], d[src]).then_inc(q["loaded"], 16)

            @block.scalar
            def _(act):
                act.wait_ge(q["loaded"], BASE + 6 * 16)
                act.activation(aexp[:], alog[:], ACT.Exp).then_inc(q["aready"], 1)
                c = Chain(act, q["ach"], 3)
                with act.Fori(0, NB) as b:
                    c.start(b)
                    act.wait_ge(q["upad"], BASE + 1)
                    act.wait_ge(q["uzdone"], BASE + b + 1)
                    act.wait_ge(q["conv"], BASE + b * NH)
                    act.activation(u[:, :, DC - 1:], BC[:, 0:NH, :], ACT.Copy).then_inc(q["uread"], 1)
                    act.wait_ge(q["yread"], BASE + b)
                    act.activation(zg[:], BC[:, NH:2 * NH, :], ACT.Silu).then_inc(q["zread"], 1)
                    act.wait_ge(q["conv"], BASE + (b + 1) * NH)
                    act.activation(uc[:], cv[:], ACT.Silu).then_inc(q["ucdone"], 1)
                    act.wait_ge(q["xdone"], BASE + b + 1)
                    act.activation(xd[:, :], M[0:NX, 0, :], ACT.Copy).then_inc(q["xread"], 1)
                    act.wait_ge(q["dtdone"], BASE + b + 1)
                    for k in range(NH):
                        ins = act.activation(v[:, k, :], M[:, k, :], ACT.Identity, bias=par[:, k, DC + 1:DC + 2])
                    c.link(ins)
                    c.link(act.activation(e[:], v[:], ACT.Abs))
                    c.link(act.activation(e[:], e[:], ACT.Exp, scale=-1.0))
                    act.activation(e[:], e[:], ACT.Ln, bias=1.0).then_inc(q["dtread"], 1)
                    act.wait_ge(q["dtready"], BASE + b + 1)
                    act.wait_ge(q["acopy"], BASE + 1)
                    for n in range(DS):
                        act.wait_ge(q["bcdone"], BASE + b * DS + n + 1)
                        act.wait_ge(q["bfree"], BASE + b * DS + n)
                        act.activation(bs[:, n % 2, :], BC[:, 2 * (n % 2), :], ACT.Copy).then_inc(q["bcopied"], 1)
                        for k in range(NH):
                            act.wait_ge(q["dafree"], BASE + b * NS + NH * n + k + 1)
                            act.activation(da[:, (NH * n + k) % 4, :], dt[:, k, :], ACT.Exp,
                                           scale=aexp[:, k, n:n + 1]).then_inc(q["daready"], 1)
                    c.end()

            @block.gpsimd
            def _(pool):
                pool.memset(u[:], 0.0).then_inc(q["upad"], 1)
                pool.wait_ge(q["aready"], BASE + 1)
                pool.tensor_scalar(aexp[:], aexp[:], -1.0, None, ALU.mult).then_inc(q["acopy"], 1)
                pool.sem_inc(q["bfree"], 1)
                with pool.Fori(0, NB) as b:
                    pool.wait_ge(q["dtuready"], BASE + b + 1)
                    for n in range(DS):
                        pool.wait_ge(q["bcopied"], BASE + b * DS + n + 1)
                        for k in range(NH):
                            pool.wait_ge(q["dbfree"], BASE + b * NS + NH * n + k + 1)
                            ins = pool.tensor_tensor(db[:, (NH * n + k) % 4, :], dtu[:, k, :], bs[:, n % 2, :], ALU.mult)
                            ins.then_inc(q["dbready"], 1)
                        pool.wait_ge(q["dbready"], BASE + b * NS + NH * (n + 1))
                        pool.sem_inc(q["bfree"], 1)

            @block.tensor
            def _(pe):
                pe.wait_ge(q["loaded"], BASE + 6 * 16)
                with pe.Fori(0, NB) as b:
                    pe.wait_ge(q["cfree"], BASE + b * NS)
                    for k in range(2 * NH):
                        mm = pe.matmul(BC[:, k, :], w_in[:, k * P:(k + 1) * P], xn[:, b, :], start=True, stop=True)
                    mm.then_inc(q["uzdone"], 1)
                    pe.wait_ge(q["ucdone"], BASE + b + 1)
                    pe.wait_ge(q["outread"], BASE + b)
                    for k in range(NH):
                        mm = pe.matmul(M[0:NX, 0, :], w_x[:, k, :], uc[:, k, :], start=(k == 0), stop=(k == NH - 1))
                    mm.then_inc(q["xdone"], 1)
                    pe.wait_ge(q["xread"], BASE + b + 1)
                    for k in range(NH):
                        mm = pe.matmul(M[:, k, :], w_dt[:, k * P:(k + 1) * P], xd[0:DR, :], start=True, stop=True)
                    mm.then_inc(q["dtdone"], 1)
                    pe.wait_ge(q["zread"], BASE + b + 1)

                    def broadcast(n):
                        if n >= 2:
                            pe.wait_ge(q["bcopied"], BASE + b * DS + n - 1)
                            pe.wait_ge(q["cfree"], BASE + b * NS + NH * (n - 1))
                        for j in range(2):
                            col = DR + j * DS + n
                            mm = pe.matmul(BC[:, 2 * (n % 2) + j, :], ident[0:NX, col:col + 1].broadcast_to([NX, P]),
                                           xd[:, :], start=True, stop=True)
                        mm.then_inc(q["bcdone"], 1)

                    broadcast(0)
                    pe.wait_ge(q["yread"], BASE + b)
                    for n in range(DS):
                        if n + 1 < DS:
                            broadcast(n + 1)
                        for k in range(NH):
                            pe.wait_ge(q["hcready"], BASE + b * NS + NH * n + k + 1)
                            pe.matmul(Y[:, k, :], ident[:, :], hc[:, (NH * n + k) % 4, :], start=(n == 0),
                                      stop=(n == DS - 1)).then_inc(q["hcfree"], 1)
                    pe.wait_ge(q["yread"], BASE + b + 1)
                    for k in range(NH):
                        mm = pe.matmul(M[:, 0, :], w_out[:, k, :], y[:, k, :], start=(k == 0), stop=(k == NH - 1))
                    mm.then_inc(q["outdone"], 1)

            @block.vector
            def _(dve):
                c = Chain(dve, q["dch"], (DC - 1) * NH + 2 + NS + 1)
                dve.wait_ge(q["loaded"], BASE + 6 * 16)
                for sem in ("dafree", "dbfree", "hcfree"):
                    dve.sem_inc(q[sem], 4)
                with dve.Fori(0, NB) as b:
                    c.start(b)
                    dve.wait_ge(q["uread"], BASE + b + 1)
                    for k in range(NH):
                        c.link(dve.tensor_scalar(cv[:, k, :], u[:, k, 0:L], par[:, k, 0:1], par[:, k, DC:DC + 1],
                                                 ALU.mult, ALU.add))
                        for t in range(1, DC):
                            ins = dve.scalar_tensor_tensor(out=cv[:, k, :], in0=u[:, k, t:t + L],
                                                           scalar=par[:, k, t:t + 1], in1=cv[:, k, :],
                                                           op0=ALU.mult, op1=ALU.add)
                            if t < DC - 1:
                                c.link(ins)
                        ins.then_inc(q["conv"], 1)
                    dve.wait_ge(q["dtread"], BASE + b + 1)
                    c.link(dve.tensor_scalar(v[:], v[:], 0.0, None, ALU.max))
                    ins = dve.tensor_tensor(dt[:], v[:], e[:], ALU.add)
                    ins.then_inc(q["dtready"], 1)
                    dve.wait_ge(q["dtready"], BASE + b + 1)
                    dve.tensor_tensor(dtu[:], dt[:], uc[:], ALU.mult).then_inc(q["dtuready"], 1)
                    for n in range(DS):
                        for k in range(NH):
                            i = NH * n + k
                            dve.wait_ge(q["daready"], BASE + b * NS + i + 1)
                            dve.wait_ge(q["dbready"], BASE + b * NS + i + 1)
                            ins = dve.tensor_tensor_scan(h[:, i % 2, :], da[:, i % 4, :], db[:, i % 4, :], 0.0,
                                                         ALU.mult, ALU.add)
                            c.link(ins)
                            dve.sem_inc(q["dafree"], 1)
                            dve.sem_inc(q["dbfree"], 1)
                            dve.wait_ge(q["hcfree"], BASE + b * NS + i + 1)
                            dve.wait_ge(q["bcdone"], BASE + b * DS + n + 1)
                            dve.tensor_tensor(hc[:, i % 4, :], h[:, i % 2, :], BC[:, 2 * (n % 2) + 1, :],
                                              ALU.mult).then_inc(q["hcready"], 1)
                            dve.wait_ge(q["hcready"], BASE + b * NS + i + 1)
                            dve.sem_inc(q["cfree"], 1)
                    dve.wait_ge(q["hcfree"], BASE + (b + 1) * NS + 4)
                    for k in range(NH):
                        ins = dve.scalar_tensor_tensor(out=y[:, k, :], in0=uc[:, k, :], scalar=par[:, k, DC + 2:DC + 3],
                                                       in1=Y[:, k, :], op0=ALU.mult, op1=ALU.add)
                    c.link(ins)
                    dve.tensor_tensor(y[:], y[:], zg[:], ALU.mult).then_inc(q["yread"], 1)
                    dve.wait_ge(q["outdone"], BASE + b + 1)
                    ins = dve.tensor_tensor(acc[:, b, :], acc[:, b, :], M[:, 0, :], ALU.add)
                    c.link(ins)
                    dve.sem_inc(q["outread"], 1)
                    c.end()


NLAYER, NHEAD, DH, WIN = 6, 16, 64, 32
NCH = NHEAD // 2
INNER = NHEAD * DH
FF = P * 4 * 2 // 3
FCH = [(c, min(P, FF - c)) for c in range(0, FF, P)]
NQK = 2 * INNER // L
NPC = 3 * INNER // L
NW = L // WIN
WT = P // WIN


def ffn_stage(nc, g, d):
    acc, xn, ident = g["acc"], g["xn"], g["ident"]
    with ExitStack() as ctx:
        s = Stage(nc, ctx, "ff")
        w_qkv = s.sb("w_qkv", [P, 3 * INNER])
        w_o = s.sb("w_o", [P, NCH, P])
        w_1 = s.sb("w_1", [P, 2 * FF])
        w_2 = s.sb("w_2", [P, len(FCH), P])
        par = s.sb("par", [P, 3 + 2 * len(FCH)])
        ctab = s.sb("ctab", [P, 4, NT, DH])
        qk_s = s.sb("qk_s", [P, 4, DH])
        tab = s.sb("tab", [P, 4, NT, DH])
        mask_f = s.sb("mask_f", [P, 2, DH])
        mask = s.sb("mask", [P, 2, NCH, DH], BF16)
        ident_b = s.sb("ident_b", [P, P], BF16)
        xs = s.sb("xs", [P, L])
        raw = s.sb("raw", [P, 2, NQK, L])
        sq = s.sb("sq", [P, NQK * L])
        n2 = s.sb("n2", [P, 2 * NHEAD])
        inv = s.sb("inv", [P, 2 * NHEAD])
        half = s.sb("half", [P, 2 * NHEAD])
        tmp = s.sb("tmp", [P, 2 * NHEAD])
        rc = s.sb("rc", [P, 2, NQK * L])
        qT = s.sb("qT", [P, 2, NCH, P])
        kT = s.sb("kT", [P, NCH, WIN + L])
        v = s.sb("v", [P, 2, INNER])
        v2 = s.sb("v2", [P, NW + 1, NCH * DH])
        mx = s.sb("mx", [P, NHEAD])
        ssum = s.sb("ssum", [P, NHEAD])
        pr = s.sb("pr", [P, 2, NCH, 2, DH])
        pT = s.sb("pT", [P, NCH, P])
        oT = s.sb("oT", [P, NCH, L])
        stats = s.sb("stats", [P, NT, 6])
        mv = s.sb("mv", [P, NT, 2])
        xh = s.sb("xh", [P, NT, P])
        x2 = s.sb("x2", [P, L])
        gg = raw[:, 0, 0:3, :]
        hh = raw[:, 1, 0:3, :]
        QA = s.banks("QA", 2)
        TR = s.banks("TR", 2)
        S = s.banks("S", 2)
        O = s.banks("O", 2)
        q = s.sems("const tabfree w_in masks tabs padded xs_ready qa_fill qa_read0 qa_read1 raw_ready sq_ready "
                   "n2_done rs_ready rc_ready tr_fill tr_read0 tr_read1 qk_turned s_fill s_read p_exp p_sum p_ready "
                   "p_read pt_ready o_fill o_read v_ready v2_in0 v2_in1 x1_ready xh_ready x2_ready g_ready "
                   "h_ready ff_done dch held")
        qa_read, tr_read, v2_in = ([q[f"{n}{k}"] for k in range(2)] for n in ("qa_read", "tr_read", "v2_in"))

        steps = [[(kind, i - lag) for lag, kind in enumerate("XYZ") if 0 <= i - lag < NT] for i in range(NT + 2)]
        order = [x for step in steps for x in step]
        qa = [("X", t, pc) for kind, t in order if kind == "X" for pc in range(NPC)]
        qa += [("Wo",)] + [("W1", c, j) for c in range(len(FCH)) for j in range(2)] + [("W2",)]
        tr = []
        for kind, t in order:
            tr += [(kind, t, j) for j in range({"X": 0, "Y": NQK, "Z": 2}[kind])]
        tr += [("tok",), ("fea",)]
        QN, TN = len(qa), len(tr)
        assert QN % 2 == 0 and TN % 2 == 0
        qa = {key: n for n, key in enumerate(qa)}
        tr = {key: n for n, key in enumerate(tr)}
        NLOAD = 6

        def fill_qa(pe, n, key):
            k = qa[key]
            pe.wait_ge(qa_read[k % 2], BASE + n * (QN // 2) + k // 2)
            return QA[:, k % 2, :]

        def fill_tr(pe, n, key):
            k = tr[key]
            pe.wait_ge(tr_read[k % 2], BASE + n * (TN // 2) + k // 2)
            return TR[:, k % 2, :]

        def filled_qa(eng, n, key):
            k = qa[key]
            eng.wait_ge(q["qa_fill"], BASE + n * QN + k + 1)
            return QA[:, k % 2, :], qa_read[k % 2]

        def filled_tr(eng, n, key):
            k = tr[key]
            eng.wait_ge(q["tr_fill"], BASE + n * TN + k + 1)
            return TR[:, k % 2, :], tr_read[k % 2]

        with nc.Block() as block:
            @block.sync
            def _(sp):
                sp.dma_start(ctab[:], d["f_ctab"]).then_inc(q["const"], 16)
                sp.dma_start(mask_f[:], d["f_mask"]).then_inc(q["const"], 16)
                with sp.Fori(0, NLAYER) as l:
                    sp.wait_ge(q["ff_done"], BASE + l * NB)
                    settle(sp, q["held"])
                    for dst, src in ((w_qkv, "f_w_qkv"), (w_o, "f_w_o"), (w_1, "f_w_1"), (w_2, "f_w_2"),
                                     (par, "f_par"), (qk_s, "f_qk_s")):
                        sp.dma_start(dst[:], d[src][l]).then_inc(q["w_in"], 16)
                    with sp.Fori(0, NB) as b:
                        n = l * NB + b
                        for t in range(NT):
                            sp.wait_ge(q["v_ready"], BASE + n * NT + t + 1)
                            settle(sp, q["held"])
                            sp.wait_ge(q["o_fill"], BASE + n * NT)
                            settle(sp, q["held"])
                            for par_ in range(2):
                                for c in range(2):
                                    r0 = 64 * par_ + WIN * c
                                    for w in range(WT):
                                        sp.dma_start(v2[r0:r0 + WIN, WT * t + w + 1 - c, :],
                                                     v[WIN * w:WIN * w + WIN, t % 2, par_ * L:par_ * L + L]
                                                     ).then_inc(v2_in[t % 2], 16)

            @block.gpsimd
            def _(pool):
                pool.memset(v2[:, 0, :], 0.0)
                pool.memset(kT[:, :, 0:WIN], 0.0)
                pool.memset(xs[:, :], 0.0).then_inc(q["padded"], 1)
                pool.wait_ge(q["const"], BASE + 32)
                pool.tensor_copy(ident_b[:, :], ident[:, :])
                for j in range(2):
                    for c in range(NCH):
                        ins = pool.tensor_copy(mask[:, j, c, :], mask_f[:, j, :])
                ins.then_inc(q["masks"], 1)
                with pool.Fori(0, NLAYER) as l:
                    pool.wait_ge(q["w_in"], BASE + (l + 1) * NLOAD * 16)
                    pool.wait_ge(q["ff_done"], BASE + l * NB)
                    for k in range(4):
                        ins = pool.tensor_tensor(tab[:, k, :, :], ctab[:, k, :, :],
                                                 qk_s[:, k:k + 1, :].broadcast_to([P, NT, DH]), ALU.mult)
                    ins.then_inc(q["tabs"], 1)
                    pool.wait_ge(q["tabs"], BASE + l + 1)
                    settle(pool, q["held"])
                    with pool.Fori(0, NB) as b:
                        n = l * NB + b

                        def rotate(t):
                            pool.wait_ge(q["raw_ready"], BASE + n * NT + t + 1)
                            pool.wait_ge(q["n2_done"], BASE + n * NT + t + 1)
                            for k in range(2):
                                x = raw[:, t % 2, 2 * k:2 * k + 2, :].rearrange("p c (h z e) -> p (c h) z e", z=2, e=DH // 2)
                                y = sq[:, k * INNER:(k + 1) * INNER].rearrange("p (h z e) -> p h z e", z=2, e=DH // 2)
                                for z in range(2):
                                    e0 = z * (DH // 2)
                                    ins = pool.tensor_tensor(
                                        y[:, :, z, :], x[:, :, 1 - z, :],
                                        tab[:, 2 + k, t:t + 1, e0:e0 + DH // 2].broadcast_to([P, NHEAD, DH // 2]), ALU.mult)
                            ins.then_inc(q["rs_ready"], 1)

                        def norm_p(t):
                            pool.wait_ge(q["p_sum"], BASE + n * NT + t + 1)
                            x = pr[:, t % 2, :, :, :].rearrange("p c z e -> p (c z) e")
                            pool.tensor_tensor(x, x, ssum[:, :].unsqueeze(2).broadcast_to([P, NHEAD, DH]),
                                               ALU.mult).then_inc(q["p_ready"], 1)

                        for step in steps:
                            for kind, t in step:
                                if kind == "X":
                                    rotate(t)
                                if kind == "Y":
                                    norm_p(t)

            @block.scalar
            def _(act):
                act.wait_ge(q["padded"], BASE + 1)
                with act.Fori(0, NLAYER) as l:
                    act.wait_ge(q["w_in"], BASE + (l + 1) * NLOAD * 16)
                    with act.Fori(0, NB) as b:
                        n = l * NB + b

                        def shift():
                            settle(act, q["held"])
                            act.activation(xs[0:64, :], xn[0:64, b, :], ACT.Copy)
                            act.activation(xs[64:P, 1:L], xn[64:P, b, 0:L - 1], ACT.Copy).then_inc(q["xs_ready"], 1)

                        def copy_qkv(t):
                            act.wait_ge(q["rc_ready"], BASE + n * NT + max(t - 1, 0))
                            for pc in range(NPC):
                                bank, read = filled_qa(act, n, ("X", t, pc))
                                if pc == NQK and t >= 2:
                                    act.wait_ge(v2_in[t % 2], BASE + (2 * n + t // 2) * 256)
                                dst = raw[:, t % 2, pc, :] if pc < NQK else v[:, t % 2, (pc - NQK) * L:(pc - NQK + 1) * L]
                                act.activation(dst, bank, ACT.Copy).then_inc(read, 1)
                                if pc == NQK - 1:
                                    act.wait_ge(read, BASE + n * (QN // 2) + qa[("X", t, pc)] // 2 + 1)
                                    act.wait_ge(qa_read[1 - qa[("X", t, pc)] % 2],
                                                BASE + n * (QN // 2) + qa[("X", t, pc - 1)] // 2 + 1)
                                    if t >= 1:
                                        act.wait_ge(q["rc_ready"], BASE + n * NT + t)
                                    act.activation(sq[:, :], raw[:, t % 2, :, :], ACT.Square).then_inc(q["sq_ready"], 1)
                            act.wait_ge(q["sq_ready"], BASE + n * NT + t + 1)
                            act.sem_inc(q["raw_ready"], 1)
                            act.wait_ge(read, BASE + n * (QN // 2) + qa[("X", t, NPC - 1)] // 2 + 1)
                            act.sem_inc(q["v_ready"], 1)

                        def turn_qk(t):
                            if t >= 1:
                                act.wait_ge(q["s_fill"], BASE + n * NT + t - 1)
                            for j in range(NQK):
                                bank, read = filled_tr(act, n, ("Y", t, j))
                                src = bank.rearrange("p (c x) -> p c x", x=P)
                                c0 = 4 * (j % 2)
                                dst = (qT[:, t % 2, c0:c0 + 4, :] if j < NQK // 2 else
                                       kT[:, c0:c0 + 4, WIN + t * P:WIN + (t + 1) * P])
                                act.activation(dst, src, ACT.Copy).then_inc(read, 1)
                            for k in range(2):
                                j = NQK - 2 + k
                                i = tr[("Y", t, j)]
                                act.wait_ge(tr_read[i % 2], BASE + n * (TN // 2) + i // 2 + 1)
                            act.sem_inc(q["qk_turned"], 1)

                        def turn_p(t):
                            act.wait_ge(q["o_fill"], BASE + n * NT + t)
                            for j in range(2):
                                bank, read = filled_tr(act, n, ("Z", t, j))
                                act.activation(pT[:, 4 * j:4 * j + 4, :], bank.rearrange("p (c x) -> p c x", x=P),
                                               ACT.Copy).then_inc(read, 1)
                            for j in range(2):
                                i = tr[("Z", t, j)]
                                act.wait_ge(tr_read[i % 2], BASE + n * (TN // 2) + i // 2 + 1)
                            act.sem_inc(q["pt_ready"], 1)
                            act.wait_ge(q["o_fill"], BASE + n * NT + t + 1)
                            act.activation(oT[:, :, t * P:(t + 1) * P],
                                           O[:, :, :].rearrange("p k (c x) -> p (k c) x", x=P),
                                           ACT.Copy).then_inc(q["o_read"], 1)

                        def exp_p(t):
                            act.wait_ge(q["s_read"], BASE + n * NT + t + 1)
                            act.activation(pr[:, t % 2, :, :, :], pr[:, t % 2, :, :, :], ACT.Exp,
                                           scale=8.0).then_inc(q["p_exp"], 1)

                        act.wait_ge(q["ff_done"], BASE + n)
                        shift()
                        for step in steps:
                            for kind, t in step:
                                if kind == "X":
                                    copy_qkv(t)
                                if kind == "Y":
                                    turn_qk(t)
                                if kind == "Z":
                                    turn_p(t)
                            for kind, t in step:
                                if kind == "Y":
                                    exp_p(t)
                        act.wait_ge(q["x1_ready"], BASE + n + 1)
                        shift()
                        bank, read = filled_tr(act, n, ("fea",))
                        act.activation(x2[:, :], bank, ACT.Identity, scale=par[:, 0:1], bias=par[:, 1:2]).then_inc(read, 1)
                        act.wait_ge(read, BASE + n * (TN // 2) + tr[("fea",)] // 2 + 1)
                        act.sem_inc(q["x2_ready"], 1)
                        for c, (_, m) in enumerate(FCH):
                            bank, read = filled_qa(act, n, ("W1", c, 0))
                            act.activation(gg[0:m, c, :], bank[0:m, :], ACT.Gelu, bias=par[0:m, 6 + c:7 + c]).then_inc(read, 1)
                            act.wait_ge(read, BASE + n * (QN // 2) + qa[("W1", c, 0)] // 2 + 1)
                            act.sem_inc(q["g_ready"], 1)

            @block.tensor
            def _(pe):
                pe.wait_ge(q["masks"], BASE + 1)
                with pe.Fori(0, NLAYER) as l:
                    pe.wait_ge(q["w_in"], BASE + (l + 1) * NLOAD * 16)
                    settle(pe, q["held"])
                    with pe.Fori(0, NB) as b:
                        n = l * NB + b

                        def project(t):
                            for pc in range(NPC):
                                bank = fill_qa(pe, n, ("X", t, pc))
                                pe.matmul(bank, xs[:, t * P:(t + 1) * P], w_qkv[:, pc * L:(pc + 1) * L],
                                          start=True, stop=True).then_inc(q["qa_fill"], 1)

                        def scores(t):
                            pe.wait_ge(q["rc_ready"], BASE + n * NT + t + 1)
                            for j in range(NQK):
                                bank = fill_tr(pe, n, ("Y", t, j))
                                for c in range(4):
                                    mm = pe.transpose(bank[:, c * P:(c + 1) * P],
                                                      rc[:, t % 2, j * L + c * P:j * L + (c + 1) * P], ident[:, :])
                                mm.then_inc(q["tr_fill"], 1)
                            pe.wait_ge(q["qk_turned"], BASE + n * NT + t + 1)
                            pe.wait_ge(q["s_read"], BASE + n * NT + t)
                            for z in range(2):
                                pe.matmul(S[:, z, :], ident_b[:, :], mask[:, 0 if t == 0 else 1, :, :], start=True,
                                          stop=False, skip_group_check=True)
                            for c in range(NCH):
                                for z in range(2):
                                    for w in range(WT):
                                        mm = pe.matmul(S[WIN * w:WIN * w + WIN, z, c * DH:(c + 1) * DH],
                                                       qT[64 * z:64 * z + 64, t % 2, c, WIN * w:WIN * w + WIN],
                                                       kT[64 * z:64 * z + 64, c, t * P + WIN * w:t * P + WIN * w + 2 * WIN],
                                                       start=False, stop=(c == NCH - 1), skip_group_check=True)
                            mm.then_inc(q["s_fill"], 1)

                        def attend(t):
                            pe.wait_ge(q["p_ready"], BASE + n * NT + t + 1)
                            for j in range(2):
                                bank = fill_tr(pe, n, ("Z", t, j))
                                for c in range(4):
                                    mm = pe.transpose(bank[:, c * P:(c + 1) * P], pr[:, t % 2, 4 * j + c, :, :], ident[:, :])
                                mm.then_inc(q["tr_fill"], 1)
                            pe.wait_ge(q["pt_ready"], BASE + n * NT + t + 1)
                            pe.wait_ge(v2_in[t % 2], BASE + (2 * n + t // 2 + 1) * 256)
                            pe.wait_ge(q["o_read"], BASE + n * NT + t)
                            settle(pe, q["held"])
                            for c in range(NCH):
                                for w in range(WT):
                                    for z in range(2):
                                        rows = slice(64 * z, 64 * z + 64)
                                        mm = pe.matmul(O[rows, c // 4, (c % 4) * P + WIN * w:(c % 4) * P + WIN * (w + 1)],
                                                       v2[rows, WT * t + w, c * DH:(c + 1) * DH],
                                                       pT[rows, c, WIN * w:WIN * (w + 1)], start=True, stop=True,
                                                       skip_group_check=True)
                            mm.then_inc(q["o_fill"], 1)

                        pe.wait_ge(q["xs_ready"], BASE + 2 * n + 1)
                        for kind, t in order:
                            {"X": project, "Y": scores, "Z": attend}[kind](t)
                        pe.wait_ge(q["o_read"], BASE + (n + 1) * NT)
                        bank = fill_qa(pe, n, ("Wo",))
                        for c in range(NCH):
                            mm = pe.matmul(bank, w_o[:, c, :], oT[:, c, :], start=(c == 0), stop=(c == NCH - 1))
                        mm.then_inc(q["qa_fill"], 1)
                        pe.wait_ge(q["xs_ready"], BASE + 2 * n + 2)
                        bank = fill_tr(pe, n, ("tok",))
                        for t in range(NT):
                            mm = pe.transpose(bank[:, t * P:(t + 1) * P], xs[:, t * P:(t + 1) * P], ident[:, :])
                        mm.then_inc(q["tr_fill"], 1)
                        pe.wait_ge(q["xh_ready"], BASE + n + 1)
                        bank = fill_tr(pe, n, ("fea",))
                        for t in range(NT):
                            mm = pe.transpose(bank[:, t * P:(t + 1) * P], xh[:, t, :], ident[:, :])
                        mm.then_inc(q["tr_fill"], 1)
                        pe.wait_ge(q["x2_ready"], BASE + n + 1)
                        for c, (f0, m) in enumerate(FCH):
                            for j in range(2):
                                bank = fill_qa(pe, n, ("W1", c, j))
                                f = f0 + (1 - j) * FF
                                pe.matmul(bank[0:m, :], w_1[:, f:f + m], x2[:, :], start=True,
                                          stop=True).then_inc(q["qa_fill"], 1)
                        bank = fill_qa(pe, n, ("W2",))
                        for c, (_, m) in enumerate(FCH):
                            pe.wait_ge(q["h_ready"], BASE + n * len(FCH) + c + 1)
                            mm = pe.matmul(bank, w_2[0:m, c, :], hh[0:m, c, :], start=(c == 0), stop=(c == len(FCH) - 1))
                        mm.then_inc(q["qa_fill"], 1)

            @block.vector
            def _(dve):
                ch = Chain(dve, q["dch"], NT * (2 + RSQRT_LINKS + 3 + 4) + 2 * NT + 1 + RSQRT_LINKS)
                with dve.Fori(0, NLAYER) as l:
                    dve.wait_ge(q["tabs"], BASE + l + 1)
                    settle(dve, q["held"])
                    with dve.Fori(0, NB) as b:
                        n = l * NB + b
                        ch.start(n)

                        def rotate(t):
                            dve.wait_ge(q["sq_ready"], BASE + n * NT + t + 1)
                            ch.link(dve.tensor_reduce(n2[:, :], sq[:, :].rearrange("p (h e) -> p h e", e=DH), AX, ALU.add))
                            dve.sem_inc(q["n2_done"], 1)
                            ch.link(dve.tensor_scalar(n2[:, :], n2[:, :], 1e-24, None, ALU.max))
                            rsqrt(dve, ch, inv[:, :], n2[:, :], half[:, :], tmp[:, :])
                            if t >= 2:
                                dve.wait_ge(q["s_fill"], BASE + n * NT + t - 1)
                            for k in range(2):
                                x = raw[:, t % 2, 2 * k:2 * k + 2, :].rearrange("p c (h e) -> p (c h) e", e=DH)
                                y = rc[:, t % 2, k * INNER:(k + 1) * INNER].rearrange("p (h e) -> p h e", e=DH)
                                ins = dve.tensor_tensor(y, x, tab[:, k, t:t + 1, :].broadcast_to([P, NHEAD, DH]), ALU.mult)
                            ch.link(ins)
                            dve.wait_ge(q["rs_ready"], BASE + n * NT + t + 1)
                            ch.link(dve.tensor_tensor(rc[:, t % 2, :], rc[:, t % 2, :], sq[:, :], ALU.add))
                            y = rc[:, t % 2, :].rearrange("p (h e) -> p h e", e=DH)
                            ch.link(dve.tensor_tensor(y, y, inv[:, :].unsqueeze(2).broadcast_to([P, 2 * NHEAD, DH]), ALU.mult))
                            dve.sem_inc(q["rc_ready"], 1)

                        def softmax(t):
                            dve.wait_ge(q["s_fill"], BASE + n * NT + t + 1)
                            x = S[:, :, :].rearrange("p z (c e) -> p z c e", e=DH)
                            m = mx[:, :].rearrange("p (c z) -> p z c", z=2)
                            ch.link(dve.tensor_reduce(m, x, AX, ALU.max))
                            if t >= 2:
                                dve.wait_ge(q["o_fill"], BASE + n * NT + t - 1)
                            for z in range(2):
                                ins = dve.tensor_tensor(pr[:, t % 2, :, z, :], x[:, z, :, :],
                                                        m[:, z, :].unsqueeze(2).broadcast_to([P, NCH, DH]), ALU.subtract)
                            ch.link(ins)
                            dve.sem_inc(q["s_read"], 1)
                            dve.wait_ge(q["p_exp"], BASE + n * NT + t + 1)
                            dve.wait_ge(q["p_ready"], BASE + n * NT + t)
                            ch.link(dve.tensor_reduce(ssum[:, :], pr[:, t % 2, :, :, :].rearrange("p c z e -> p (c z) e"),
                                                      AX, ALU.add))
                            ch.link(dve.reciprocal(ssum[:, :], ssum[:, :]))
                            dve.sem_inc(q["p_sum"], 1)

                        for step in steps:
                            for kind, t in step:
                                if kind == "X":
                                    rotate(t)
                                if kind == "Y":
                                    softmax(t)
                        bank, read = filled_qa(dve, n, ("Wo",))
                        dve.tensor_tensor(xn[:, b, :], xn[:, b, :], bank, ALU.add).then_inc(read, 1)
                        dve.wait_ge(read, BASE + n * (QN // 2) + qa[("Wo",)] // 2 + 1)
                        dve.sem_inc(q["x1_ready"], 1)
                        bank, read = filled_tr(dve, n, ("tok",))
                        for t in range(NT):
                            ch.tick(dve.bn_stats(stats[:, t, :], bank[:, t * P:(t + 1) * P]))
                        ch.wait()
                        dve.memset(tmp[:, :], 0.0)
                        for t in range(NT):
                            ch.tick(dve.bn_aggr(mv[:, t, :], stats[:, t, :]))
                        ch.wait()
                        ch.link(dve.tensor_scalar(mv[:, :, 1], mv[:, :, 1], EPS, None, ALU.add))
                        rsqrt(dve, ch, inv[:, 0:NT], mv[:, :, 1], half[:, 0:NT], tmp[:, 0:NT])
                        for t in range(NT):
                            ins = dve.tensor_scalar(xh[:, t, :], bank[:, t * P:(t + 1) * P], mv[:, t, 0:1],
                                                    inv[:, t:t + 1], ALU.subtract, ALU.mult)
                        ins.then_inc(read, 1)
                        dve.wait_ge(read, BASE + n * (TN // 2) + tr[("tok",)] // 2 + 1)
                        dve.sem_inc(q["xh_ready"], 1)
                        for c, (_, m) in enumerate(FCH):
                            bank, read = filled_qa(dve, n, ("W1", c, 1))
                            dve.wait_ge(q["g_ready"], BASE + n * len(FCH) + c + 1)
                            dve.scalar_tensor_tensor(out=hh[0:m, c, :], in0=bank[0:m, :], scalar=par[0:m, 3 + c:4 + c],
                                                     in1=gg[0:m, c, :], op0=ALU.add, op1=ALU.mult).then_inc(read, 1)
                            dve.wait_ge(read, BASE + n * (QN // 2) + qa[("W1", c, 1)] // 2 + 1)
                            dve.sem_inc(q["h_ready"], 1)
                        bank, read = filled_qa(dve, n, ("W2",))
                        dve.scalar_tensor_tensor(out=xn[:, b, :], in0=bank, scalar=par[:, 2:3], in1=xn[:, b, :],
                                                 op0=ALU.add, op1=ALU.add).then_inc(read, 1)
                        dve.wait_ge(read, BASE + n * (QN // 2) + qa[("W2",)] // 2 + 1)
                        dve.sem_inc(q["ff_done"], 1)
                        ch.end()
                for b in range(NB):
                    dve.tensor_tensor(acc[:, b, :], acc[:, b, :], xn[:, b, :], ALU.add)


BH, BD, HOR = 16, 16, 64
HS = P // BH
NG = BH // 4
WCH = 8
NWC = HOR // WCH
PITCH = HOR + P
DAMAGE = 10.0


def attn_stage(nc, g, d, skew):
    acc, xn, ident = g["acc"], g["xn"], g["ident"]
    with ExitStack() as ctx:
        s = Stage(nc, ctx, "at")
        w_disp = s.sb("w_disp", [P, 2 * P])
        w_val = s.sb("w_val", [P, P])
        w_proj = s.sb("w_proj", [P, P])
        w_fused = s.sb("w_fused", [P, P])
        w_red = s.sb("w_red", [P, 8])
        w_pos = s.sb("w_pos", [BD, P])
        rel = s.sb("rel", [BD, HOR])
        bias = s.sb("bias", [P, 2])
        mask = s.sb("mask", [P, HOR])
        pos = s.sb("pos", [P, HOR])
        xp = s.sb("xp", [P, HOR + L + 1])
        disp = s.sb("disp", [P, 2, L])
        fp = s.sb("fp", [P, NG, HOR + L])
        df = s.sb("df", [P, 2, NG, L])
        ge = s.sb("ge", [P, 2, NG, L])
        th = s.sb("th", [P, NT, BH, WCH])
        lg = s.sb("lg", [P, NT, BH, HOR])
        mx = s.sb("mx", [P, NT, BH])
        rsum = s.sb("rsum", [P, NT, BH])
        va = s.sb("va", [P, NT, P])
        vb = s.sb("vb", [HOR, NT, P])
        band = s.sb("band", [P, 2, BH, PITCH])
        ba = s.sb("ba", [P, BH, P])
        bb = s.sb("bb", [HOR, BH, P])
        o = s.sb("o", [P, NT, P])
        oT = s.sb("oT", [P, L])
        zero = s.sb("zero", [P, 1544])
        LB = s.banks("LB", 4)
        TB = s.banks("TB", 2)
        O = s.banks("O", 1)
        X = s.banks("X", 1)
        q = s.sems("loaded zeroed cleared pos_fill pos_ready dbias xp_ready tb_fill tb_read0 tb_read1 disp_ready f_ready "
                   "d_ready g_ready red_done th_ready lg_part sub_done exp_done sum_done band_free pv_ready pv_done "
                   "o_ready ot_fill ot_ready pr_fill acc_done dch held wr0 wr1 wr2 wr3 rd0 rd1 rd2 rd3 v_ready")
        tb_read = [q["tb_read0"], q["tb_read1"]]
        wr, rd = ([q[f"{n}{t}"] for t in range(NT)] for n in ("wr", "rd"))
        tb = [("disp", k) for k in range(2)] + [("F", k) for k in range(NG)] + [("V", k) for k in range(2)]
        tb += [(k, t, j) for t in range(NT) for j in range(4) for k in ("A", "B")]
        TN = len(tb)
        tb = {key: n for n, key in enumerate(tb)}

        def fill(pe, b, key):
            k = tb[key]
            pe.wait_ge(tb_read[k % 2], BASE + b * (TN // 2) + k // 2)
            if key[0] == "B":
                settle(pe, q["held"])
            return TB[:, k % 2, :]

        def filled(eng, b, key):
            k = tb[key]
            eng.wait_ge(q["tb_fill"], BASE + b * TN + k + 1)
            return TB[:, k % 2, :], tb_read[k % 2]

        def read(eng, b, keys):
            for key in keys:
                eng.wait_ge(tb_read[tb[key] % 2], BASE + b * (TN // 2) + tb[key] // 2 + 1)

        loads = ((w_disp, "a_w_disp"), (w_val, "a_w_val"), (w_proj, "a_w_proj"), (w_fused, "a_w_fused"),
                 (w_red, "a_w_red"), (w_pos, "a_w_pos"), (rel, "a_rel"), (bias, "a_bias"), (mask, "a_mask"))
        flat = skew.rearrange("t h (a n) -> (t h a) n", n=1544)
        with nc.Block() as block:
            @block.sync
            def _(sp):
                for dst, src in loads:
                    sp.dma_start(dst[:], d[src]).then_inc(q["loaded"], 16)
                sp.wait_ge(q["zeroed"], BASE + 1)
                for k in range(flat.shape[0] // P):
                    sp.dma_start(flat[k * P:(k + 1) * P, :], zero[:, :]).then_inc(q["cleared"], 16)
                sp.wait_ge(q["cleared"], BASE + 16 * (flat.shape[0] // P))
                with sp.Fori(0, NB) as b:
                    for t in range(NT):
                        sp.wait_ge(rd[t], BASE + b * 16)
                        settle(sp, q["held"])
                        sp.wait_ge(q["exp_done"], BASE + b * NT + t + 1)
                        settle(sp, q["held"])
                        sp.dma_start(skew[t].rearrange("h (t c) -> t h c", c=PITCH + 1)[:, :, 0:HOR],
                                     lg[:, t, :, :]).then_inc(wr[t], 16)
                        sp.wait_ge(wr[t], BASE + (b + 1) * 16)
                        settle(sp, q["held"])
                        sp.wait_ge(q["band_free"], BASE + b * NT + t - 1)
                        sp.dma_start(band[:, t % 2, :, :],
                                     skew[t][:, 0:P * PITCH].rearrange("h (t c) -> t h c", c=PITCH)).then_inc(rd[t], 16)

            @block.gpsimd
            def _(pool):
                pool.memset(xp[:, :], 0.0)
                pool.memset(fp[:, :, 0:HOR], 0.0)
                pool.memset(zero[:, :], 0.0).then_inc(q["zeroed"], 1)
                pool.wait_ge(q["loaded"], BASE + 16 * len(loads))
                pool.tensor_scalar(bias[:, 1:2], bias[:, 1:2], 0.5, None, ALU.mult).then_inc(q["dbias"], 1)

            @block.scalar
            def _(act):
                act.wait_ge(q["pos_fill"], BASE + 1)
                act.activation(pos[:, :], X[:, 0, 0:HOR], ACT.Identity, bias=bias[:, 0:1]).then_inc(q["pos_ready"], 1)
                act.wait_ge(q["pos_ready"], BASE + 1)
                act.wait_ge(q["dbias"], BASE + 1)
                act.wait_ge(q["zeroed"], BASE + 1)
                with act.Fori(0, NB) as b:
                    act.wait_ge(q["acc_done"], BASE + b)
                    settle(act, q["held"])
                    act.activation(xp[:, HOR:HOR + L], xn[:, b, :], ACT.Copy).then_inc(q["xp_ready"], 1)
                    for k in range(2):
                        bank, r = filled(act, b, ("disp", k))
                        act.activation(disp[:, k, :], bank, ACT.Copy).then_inc(r, 1)
                    read(act, b, [("disp", 0), ("disp", 1)])
                    act.sem_inc(q["disp_ready"], 1)
                    for k in range(NG):
                        bank, r = filled(act, b, ("F", k))
                        act.activation(fp[:, k, HOR:], bank, ACT.Copy).then_inc(r, 1)
                    read(act, b, [("F", NG - 2), ("F", NG - 1)])
                    act.sem_inc(q["f_ready"], 1)
                    for k, dst in enumerate((va[:, :, :], vb[:, :, :])):
                        bank, r = filled(act, b, ("V", k))
                        act.activation(dst, bank[0:dst.shape[0], :].rearrange("p (t n) -> p t n", n=P), ACT.Copy).then_inc(r, 1)
                    read(act, b, [("V", 0), ("V", 1)])
                    act.sem_inc(q["v_ready"], 1)

                    def damage(c):
                        act.wait_ge(q["red_done"], BASE + b * HOR + WCH * (c + 1))
                        act.wait_ge(q["lg_part"], BASE + b * NWC + c)
                        act.activation(th[:].rearrange("p t h w -> p t (h w)"),
                                       LB[:, 2 * (c % 2):2 * (c % 2) + 2, :].rearrange("p k (t y n) -> p (k t) y n", t=2, y=2)[:, :, 1, :],
                                       ACT.Tanh, scale=0.5, bias=bias[:, 1:2]).then_inc(q["th_ready"], 1)

                    for w in range(HOR):
                        act.wait_ge(q["d_ready"], BASE + b * HOR + w + 1)
                        act.wait_ge(q["red_done"], BASE + b * HOR + w - 1)
                        act.activation(ge[:, w % 2, :, :], df[:, w % 2, :, :], ACT.Gelu,
                                       bias=pos[:, w:w + 1]).then_inc(q["g_ready"], 1)
                        if w % WCH == 2 and w > WCH:
                            damage(w // WCH - 1)
                    damage(NWC - 1)
                    for t in range(NT):
                        act.wait_ge(q["sub_done"], BASE + b * NT + t + 1)
                        act.activation(lg[:, t, :, :], lg[:, t, :, :], ACT.Exp).then_inc(q["exp_done"], 1)
                    for t in range(NT):
                        act.wait_ge(q["pv_done"], BASE + b * NT + t)
                        for j in range(4):
                            for k, dst in (("A", ba), ("B", bb)):
                                bank, r = filled(act, b, (k, t, j))
                                act.activation(dst[:, 4 * j:4 * j + 4, :],
                                               bank[0:dst.shape[0], :].rearrange("p (h x) -> p h x", x=P), ACT.Copy).then_inc(r, 1)
                        read(act, b, [("A", t, 3), ("B", t, 3)])
                        act.sem_inc(q["pv_ready"], 1)
                    act.wait_ge(q["ot_fill"], BASE + b + 1)
                    act.activation(oT[:, :], X[:, 0, :], ACT.Copy).then_inc(q["ot_ready"], 1)

            @block.tensor
            def _(pe):
                pe.wait_ge(q["loaded"], BASE + 16 * len(loads))
                pe.matmul(X[:, 0, 0:HOR], w_pos[:, :], rel[:, :], start=True, stop=True).then_inc(q["pos_fill"], 1)
                with pe.Fori(0, NB) as b:
                    pe.wait_ge(q["xp_ready"], BASE + b + 1)
                    for k in range(2):
                        bank = fill(pe, b, ("disp", k))
                        pe.matmul(bank, w_disp[:, k * P:(k + 1) * P], xp[:, HOR:HOR + L], start=True,
                                  stop=True).then_inc(q["tb_fill"], 1)
                    pe.wait_ge(q["disp_ready"], BASE + b + 1)
                    for k in range(NG):
                        bank = fill(pe, b, ("F", k))
                        rows = slice(64 * (k % 2), 64 * (k % 2) + 64)
                        pe.matmul(bank, w_fused[rows, :], disp[rows, k // 2, :], start=True,
                                  stop=True).then_inc(q["tb_fill"], 1)
                    for k, m in enumerate((P, HOR)):
                        bank = fill(pe, b, ("V", k))
                        for t in range(NT):
                            c0 = t * P + 1 + k * P
                            mm = pe.matmul(bank[0:m, t * P:(t + 1) * P], xp[:, c0:c0 + m], w_val[:, :], start=True, stop=True)
                        mm.then_inc(q["tb_fill"], 1)
                    for w in range(HOR):
                        c = w // WCH
                        if w % WCH == 0:
                            pe.wait_ge(q["lg_part"], BASE + b * NWC + c - 1)
                        pe.wait_ge(q["g_ready"], BASE + b * HOR + w + 1)
                        for t in range(NT):
                            bank = LB[:, 2 * (c % 2) + t // 2, (t % 2) * 256:(t % 2) * 256 + 256]
                            bank = bank.rearrange("p (y h w) -> p y h w", y=2, w=WCH)
                            for k in range(NG):
                                mm = pe.matmul(bank[:, :, 4 * k:4 * k + 4, w % WCH], ge[:, w % 2, k, t * P:(t + 1) * P],
                                               w_red[:, :].rearrange("p (y h) -> p y h", y=2), start=True, stop=True,
                                               skip_group_check=True)
                        mm.then_inc(q["red_done"], 1)
                    pe.wait_ge(q["v_ready"], BASE + b + 1)
                    settle(pe, q["held"])
                    for t in range(NT):
                        pe.wait_ge(rd[t], BASE + (b + 1) * 16)
                        for j in range(4):
                            for k, m in (("A", P), ("B", HOR)):
                                bank = fill(pe, b, (k, t, j))
                                c0 = 0 if k == "A" else P
                                for i in range(4):
                                    mm = pe.transpose(bank[0:m, i * P:(i + 1) * P], band[:, t % 2, 4 * j + i, c0:c0 + m], ident[:, :])
                                mm.then_inc(q["tb_fill"], 1)
                        pe.wait_ge(q["tb_fill"], BASE + b * TN + tb[("B", t, 3)] + 1)
                        pe.sem_inc(q["band_free"], 1)
                        pe.wait_ge(q["pv_ready"], BASE + b * NT + t + 1)
                        for h in range(BH):
                            out = O[:, 0, t * P + HS * h:t * P + HS * (h + 1)]
                            pe.matmul(out, ba[:, h, :], va[:, t, HS * h:HS * (h + 1)], start=True, stop=False, skip_group_check=True)
                            mm = pe.matmul(out, bb[:, h, :], vb[:, t, HS * h:HS * (h + 1)], start=False, stop=True, skip_group_check=True)
                        mm.then_inc(q["pv_done"], 1)
                    pe.wait_ge(q["o_ready"], BASE + b + 1)
                    for t in range(NT):
                        mm = pe.transpose(X[:, 0, t * P:(t + 1) * P], o[:, t, :], ident[:, :])
                    mm.then_inc(q["ot_fill"], 1)
                    pe.wait_ge(q["ot_ready"], BASE + b + 1)
                    pe.matmul(X[:, 0, :], w_proj[:, :], oT[:, :], start=True, stop=True).then_inc(q["pr_fill"], 1)

            @block.vector
            def _(dve):
                ch = Chain(dve, q["dch"], 1 + 4 * NT)
                dve.wait_ge(q["loaded"], BASE + 16 * len(loads))
                with dve.Fori(0, NB) as b:
                    ch.start(b)

                    def logits(c):
                        dve.wait_ge(q["th_ready"], BASE + b * NWC + c + 1)
                        dve.wait_ge(rd[NT - 1], BASE + b * 16)
                        dve.scalar_tensor_tensor(
                            out=lg[:, :, :, c * WCH:(c + 1) * WCH].rearrange("p t h w -> p (t h) w"),
                            in0=th[:].rearrange("p t h w -> p (t h w)"), scalar=-DAMAGE / 2,
                            in1=LB[:, 2 * (c % 2):2 * (c % 2) + 2, :].rearrange("p k (t y n) -> p (k t) y n", t=2, y=2)[:, :, 0, :],
                            op0=ALU.mult, op1=ALU.add).then_inc(q["lg_part"], 1)

                    dve.wait_ge(q["f_ready"], BASE + b + 1)
                    for w in range(HOR):
                        dve.wait_ge(q["g_ready"], BASE + b * HOR + w - 1)
                        dve.tensor_tensor(df[:, w % 2, :, :], fp[:, :, w + 1:w + 1 + L], fp[:, :, HOR:],
                                          ALU.subtract).then_inc(q["d_ready"], 1)
                        if w % WCH == 4 and w > WCH:
                            logits(w // WCH - 1)
                    logits(NWC - 1)
                    dve.wait_ge(q["lg_part"], BASE + (b + 1) * NWC)
                    ch.link(dve.tensor_tensor(lg[:, 0, :, :], lg[:, 0, :, :],
                                              mask[:, :].unsqueeze(1).broadcast_to([P, BH, HOR]), ALU.add))
                    for t in range(NT):
                        ch.link(dve.tensor_reduce(mx[:, t, :], lg[:, t, :, :], AX, ALU.max))
                        ch.link(dve.tensor_tensor(lg[:, t, :, :], lg[:, t, :, :],
                                                  mx[:, t, :].unsqueeze(2).broadcast_to([P, BH, HOR]), ALU.subtract))
                        dve.sem_inc(q["sub_done"], 1)
                    for t in range(NT):
                        dve.wait_ge(q["exp_done"], BASE + b * NT + t + 1)
                        ch.link(dve.tensor_reduce(rsum[:, t, :], lg[:, t, :, :], AX, ALU.add))
                        ch.link(dve.reciprocal(rsum[:, t, :], rsum[:, t, :]))
                    dve.wait_ge(q["pv_done"], BASE + (b + 1) * NT)
                    for t in range(NT):
                        ins = dve.tensor_tensor(o[:, t, :].rearrange("p (h e) -> p h e", e=HS),
                                                O[:, 0, t * P:(t + 1) * P].rearrange("p (h e) -> p h e", e=HS),
                                                rsum[:, t, :].unsqueeze(2).broadcast_to([P, BH, HS]), ALU.mult)
                    ins.then_inc(q["o_ready"], 1)
                    dve.wait_ge(q["pr_fill"], BASE + b + 1)
                    dve.tensor_tensor(acc[:, b, :], acc[:, b, :], X[:, 0, :], ALU.add).then_inc(q["acc_done"], 1)
                    ch.end()


NE, NI, NTOP, GROUPS, GTOP = 64, 64, 6, 8, 4
NCK = NE * NI // P
LOW, TAKEN = -1e30, 3e30


def moe_stage(nc, g, d, out):
    acc, xn, ident = g["acc"], g["xn"], g["ident"]
    with ExitStack() as ctx:
        s = Stage(nc, ctx, "mo")
        w_g = s.sb("w_g", [P, NCK + 1, P])
        w_u = s.sb("w_u", [P, NCK + 1, P])
        w_d = s.sb("w_d", [P, NCK + 1, P])
        w_r = s.sb("w_r", [P, NE])
        gb = s.sb("gb", [P, NE])
        comb_t = s.sb("comb_t", [NE, NB, L])
        pick = s.sb("pick", [NE, NE, NI])
        xc = s.sb("xc", [P, L])
        sc = s.sb("sc", [P, NT, NE])
        gv = s.sb("gv", [P, NT, 2 * GROUPS])
        ev = s.sb("ev", [P, NT, NE + 8])
        gsel = s.sb("gsel", [P, NT, 2 * GROUPS])
        esel = s.sb("esel", [P, NT, NE + 8])
        top = s.sb("top", [P, NT, 8])
        comb = s.sb("comb", [P, NT, NE])
        wsum = s.sb("wsum", [P, NT])
        sg = s.sb("sg", [P, 2, L])
        h1 = s.sb("h1", [P, L])
        h2 = s.sb("h2", [P, 2, L])
        G = s.banks("G", 2)
        U = s.banks("U", 2)
        C = s.banks("C", 2)
        R = s.banks("R", 1)
        X = s.banks("X", 1)
        q = s.sems("loaded w_in x_ready lo_fill sc_ready lows comb_ready ct_fill ct_ready xc_ready g_fill uc_fill sg_ready "
                   "h1_ready h_ready d_done r_done saved stored dch held rch")
        with nc.Block() as block:
            @block.sync
            def _(sp):
                for dst, src in ((w_r, "e_w_r"), (gb, "e_gb")):
                    sp.dma_start(dst[:], d[src]).then_inc(q["loaded"], 16)
                for dst, src in ((w_g, "e_w_g"), (w_u, "e_w_u"), (w_d, "e_w_d")):
                    sp.dma_start(dst[:], d[src]).then_inc(q["w_in"], 16)
                with sp.Fori(0, NB) as b:
                    sp.wait_ge(q["saved"], BASE + b + 1)
                    settle(sp, q["held"])
                    sp.dma_start(out[:, b, :], acc[:, b, :]).then_inc(q["stored"], 16)
                sp.wait_ge(q["stored"], BASE + 16 * NB)

            @block.gpsimd
            def _(pool):
                pool.tensor_copy(pick[:], ident[0:NE, 0:NE].unsqueeze(2).broadcast_to([NE, NE, NI]))
                pool.memset(gv[:], LOW)
                pool.memset(ev[:], LOW).then_inc(q["lows"], 1)

            @block.scalar
            def _(act):
                with act.Fori(0, NB) as b:
                    act.wait_ge(q["lo_fill"], BASE + b)
                    settle(act, q["held"])
                    act.activation(xc[:, :], xn[:, b, :], ACT.Copy).then_inc(q["x_ready"], 1)
                    act.wait_ge(q["lo_fill"], BASE + b + 1)
                    act.activation(sc[:], X[:, 0, 0:NT * NE].rearrange("p (t e) -> p t e", e=NE),
                                   ACT.Sigmoid).then_inc(q["sc_ready"], 1)
                    act.wait_ge(q["ct_fill"], BASE + b + 1)
                    settle(act, q["held"])
                    act.activation(comb_t[:, b, :], X[0:NE, 0, :], ACT.Copy).then_inc(q["ct_ready"], 1)
                with act.Fori(0, NB) as b:
                    for c in range(NCK + 1):
                        n = b * (NCK + 1) + c
                        act.wait_ge(q["g_fill"], BASE + n + 1)
                        act.wait_ge(q["h1_ready"], BASE + n - 1)
                        act.activation(sg[:, c % 2, :], G[:, c % 2, :], ACT.Silu).then_inc(q["sg_ready"], 1)
                    act.wait_ge(q["h1_ready"], BASE + (b + 1) * (NCK + 1))

            @block.tensor
            def _(pe):
                pe.wait_ge(q["loaded"], BASE + 32)
                with pe.Fori(0, NB) as b:
                    pe.wait_ge(q["x_ready"], BASE + b + 1)
                    pe.wait_ge(q["ct_ready"], BASE + b)
                    for t in range(NT):
                        mm = pe.matmul(X[:, 0, t * NE:(t + 1) * NE], xc[:, t * P:(t + 1) * P], w_r[:, :], start=True, stop=True)
                    mm.then_inc(q["lo_fill"], 1)
                    pe.wait_ge(q["comb_ready"], BASE + b + 1)
                    settle(pe, q["held"])
                    for t in range(NT):
                        mm = pe.transpose(X[0:NE, 0, t * P:(t + 1) * P], comb[:, t, :], ident[:, :])
                    mm.then_inc(q["ct_fill"], 1)
                pe.wait_ge(q["ct_ready"], BASE + NB)
                pe.wait_ge(q["w_in"], BASE + 48)
                pe.wait_ge(q["lows"], BASE + 1)
                with pe.Fori(0, NB) as b:
                    def up(c):
                        n = b * (NCK + 1) + c
                        pe.wait_ge(q["sg_ready"], BASE + n - 1)
                        pe.matmul(G[:, c % 2, :], w_g[:, c, :], xn[:, b, :], start=True, stop=True).then_inc(q["g_fill"], 1)
                        pe.wait_ge(q["h_ready"], BASE + n - 1)
                        mm = pe.matmul(U[:, c % 2, :], w_u[:, c, :], xn[:, b, :], start=True, stop=True)
                        if c < NCK:
                            mm = pe.matmul(C[:, c % 2, :], pick[:, 2 * c:2 * c + 2, :].rearrange("k e i -> k (e i)"),
                                           comb_t[:, b, :], start=True, stop=True)
                        mm.then_inc(q["uc_fill"], 1)

                    def down(c):
                        n = b * (NCK + 1) + c
                        pe.wait_ge(q["h_ready"], BASE + n + 1)
                        if c == 0:
                            pe.wait_ge(q["saved"], BASE + b)
                        pe.matmul(R[:, 0, :], w_d[:, c, :], h2[:, c % 2, :], start=(c == 0),
                                  stop=(c == NCK)).then_inc(q["d_done"], 1)

                    pe.wait_ge(q["h_ready"], BASE + b * (NCK + 1))
                    settle(pe, q["held"])
                    for c in range(NCK + 1):
                        up(c)
                        if c >= 1:
                            down(c - 1)
                    down(NCK)

            @block.vector
            def _(dve):
                ch = Chain(dve, q["rch"], 12)
                dve.wait_ge(q["loaded"], BASE + 32)
                dve.wait_ge(q["lows"], BASE + 1)
                with dve.Fori(0, NB) as b:
                    ch.start(b)
                    dve.wait_ge(q["sc_ready"], BASE + b + 1)
                    ch.link(dve.tensor_tensor(sc[:], sc[:], gb[:, :].unsqueeze(1).broadcast_to([P, NT, NE]), ALU.add))
                    ch.link(dve.tensor_reduce(gv[:, :, 0:GROUPS], sc[:].rearrange("p t (g e) -> p t g e", g=GROUPS), AX, ALU.max))

                    def taken(values, sel, n):
                        settle(dve, q["held"])
                        for t in range(NT):
                            ins = dve.max(top[:, t, :], values[:, t, :])
                        ch.link(ins)
                        ch.link(dve.memset(top[:, :, n:8], LOW))
                        settle(dve, q["held"])
                        for t in range(NT):
                            ins = dve.match_replace(sel[:, t, :], top[:, t, :], values[:, t, :], TAKEN)
                        ch.link(ins)

                    taken(gv, gsel, GTOP)
                    ch.link(dve.tensor_scalar(gsel[:], gsel[:], -LOW, None, ALU.is_ge))
                    for t in range(NT):
                        ins = dve.tensor_tensor(ev[:, t, 0:NE].rearrange("p (g e) -> p g e", g=GROUPS),
                                                sc[:, t, :].rearrange("p (g e) -> p g e", g=GROUPS),
                                                gsel[:, t, 0:GROUPS].unsqueeze(2).broadcast_to([P, GROUPS, NE // GROUPS]), ALU.mult)
                    ch.link(ins)
                    taken(ev, esel, NTOP)
                    ins = dve.scalar_tensor_tensor(out=comb[:], in0=esel[:, :, 0:NE], scalar=-LOW, in1=ev[:, :, 0:NE],
                                                   op0=ALU.is_ge, op1=ALU.mult)
                    ch.link(ins)
                    dve.tensor_reduce(wsum[:, :], comb[:], AX, ALU.add).then_inc(q["dch"], 1)
                    dve.wait_ge(q["dch"], BASE + 3 * b + 1)
                    dve.tensor_scalar(wsum[:, :], wsum[:, :], 1e-8, None, ALU.add).then_inc(q["dch"], 1)
                    dve.wait_ge(q["dch"], BASE + 3 * b + 2)
                    dve.reciprocal(wsum[:, :], wsum[:, :]).then_inc(q["dch"], 1)
                    dve.wait_ge(q["dch"], BASE + 3 * b + 3)
                    ch.link(dve.tensor_tensor(comb[:], comb[:], wsum[:, :].unsqueeze(2).broadcast_to([P, NT, NE]), ALU.mult))
                    dve.sem_inc(q["comb_ready"], 1)
                    dve.wait_ge(q["ct_fill"], BASE + b + 1)
                    ch.end()
                with dve.Fori(0, NB) as b:
                    for c in range(NCK + 1):
                        n = b * (NCK + 1) + c
                        dve.wait_ge(q["sg_ready"], BASE + n + 1)
                        dve.wait_ge(q["uc_fill"], BASE + n + 1)
                        dve.wait_ge(q["d_done"], BASE + n - 1)
                        if c < NCK:
                            dve.tensor_tensor(h1[:, :], sg[:, c % 2, :], U[:, c % 2, :], ALU.mult).then_inc(q["h1_ready"], 1)
                            dve.wait_ge(q["h1_ready"], BASE + n + 1)
                            dve.tensor_tensor(h2[:, c % 2, :], h1[:, :], C[:, c % 2, :], ALU.mult).then_inc(q["h_ready"], 1)
                            dve.wait_ge(q["h_ready"], BASE + n + 1)
                        else:
                            dve.tensor_tensor(h2[:, c % 2, :], sg[:, c % 2, :], U[:, c % 2, :], ALU.mult).then_inc(q["h1_ready"], 1)
                            dve.wait_ge(q["h1_ready"], BASE + n + 1)
                            dve.sem_inc(q["h_ready"], 1)
                    dve.wait_ge(q["d_done"], BASE + (b + 1) * (NCK + 1))
                    settle(dve, q["held"])
                    dve.tensor_tensor(acc[:, b, :], acc[:, b, :], R[:, 0, :], ALU.add).then_inc(q["saved"], 1)


def rotary_tables():
    f = np.float32
    half = np.arange(0, DH, 2, dtype=f)
    freqs = np.arange(L, dtype=f)[:, None] * (f(1) / f(10000) ** (half / f(DH)))[None, :]
    power = (np.arange(L, dtype=f) - f(L // 2)) / f(WIN // 2)
    scale = ((half + f(0.4 * DH)) / f(1.4 * DH))[None, :] ** power[:, None]
    cos, sin = np.cos(freqs), np.sin(freqs)
    pair = lambda lo, hi: np.concatenate([lo, hi], axis=1)
    k = f(1) / scale
    t = np.stack([pair(cos * scale, cos * scale), pair(cos * k, cos * k),
                  pair(-sin * scale, sin * scale), pair(-sin * k, sin * k)])
    return np.ascontiguousarray(t.reshape(4, NT, P, DH).transpose(2, 0, 1, 3).astype(f))


def window_masks():
    a, key = (np.arange(P) % WIN)[:, None], np.arange(2 * WIN)[None, :]
    seen = (key >= a) & (key <= a + WIN)
    first = seen & ~((np.arange(P)[:, None] < WIN) & (key < WIN))
    return np.ascontiguousarray(np.where(np.stack([first, seen], axis=1), 0.0, -1e30).astype(np.float32))


def program(nc, d, out):
    with ExitStack() as ctx:
        g = {}
        g["acc"] = ctx.enter_context(nc.sbuf_tensor("acc", [P, NB, L], F32))
        g["xn"] = ctx.enter_context(nc.sbuf_tensor("xn", [P, NB, L], F32))
        g["ident"] = ctx.enter_context(nc.sbuf_tensor("ident", [P, P], F32))
        loaded = ctx.enter_context(nc.semaphore("x_loaded"))
        saved = ctx.enter_context(nc.semaphore("out_saved"))
        with nc.Block() as block:
            @block.sync
            def _(sp):
                sp.dma_start(g["ident"][:, :], d["ident"]).then_inc(loaded, 16)
                sp.dma_start(g["acc"][:, :, :], d["x"]).then_inc(loaded, 16)
                sp.wait_ge(loaded, 32)
        n = 0
        for phase in PHASES:
            if phase == "norm":
                layernorm_stage(nc, g, f"ln{n}")
                n += 1
            if phase == "mamba":
                mamba_stage(nc, g, d)
            if phase == "ffn":
                ffn_stage(nc, g, d)
            if phase == "attn":
                attn_stage(nc, g, d, nc.dram_tensor("skew", (NT, BH, P * (PITCH + 1)), F32).ap())
            if phase == "moe":
                moe_stage(nc, g, d, out)
        if PHASES[-1] == "moe":
            return
        src = g["acc"] if PHASES[-1] != "norm" else g["xn"]
        with nc.Block() as block:
            @block.sync
            def _(sp):
                sp.dma_start(out, src[:, :, :]).then_inc(saved, 16)
                sp.wait_ge(saved, 16)


def layouts(i):
    T = np.ascontiguousarray
    a = {}
    a["ident"] = np.eye(P, dtype=np.float32)
    a["x"] = T(i["L0_attn_x"].reshape(NB, L, P).transpose(2, 0, 1))
    halves = lambda w: T(w.reshape(2, P, -1).transpose(1, 0, 2))
    a["m_w_in"] = T(i["L0_attn_W_in"].T)
    a["m_w_x"] = halves(T(i["L0_attn_W_x"].T))
    a["m_w_dt"] = T(i["L0_attn_W_dt"].T)
    a["m_w_out"] = halves(T(i["L0_attn_W_out"].T))
    a["m_par"] = halves(np.concatenate([i["L0_attn_conv_w"], i["L0_attn_conv_b"][:, None],
                                        i["L0_attn_b_dt"][:, None], i["L0_attn_D"][:, None]], axis=1))
    a["m_alog"] = halves(i["L0_attn_A_log"])
    a["f_w_qkv"] = i["L0_ffn_Wqkv"].copy()
    a["f_w_qkv"][:, :, 2 * INNER:] = (i["L0_ffn_Wqkv"][:, :, 2 * INNER:].reshape(NLAYER, P, NCH, 2, DH)
                                      .transpose(0, 1, 3, 2, 4).reshape(NLAYER, P, INNER))
    a["f_w_o"] = T(i["L0_ffn_Wo"].reshape(NLAYER, NCH, P, P).transpose(0, 2, 1, 3))
    a["f_w_1"] = i["L0_ffn_W1"]
    a["f_w_2"] = np.zeros((NLAYER, P, len(FCH), P), np.float32)
    a["f_par"] = np.zeros((NLAYER, P, 3 + 2 * len(FCH)), np.float32)
    for k, name in enumerate(("ln_g", "ln_b", "b2")):
        a["f_par"][:, :, k] = i[f"L0_ffn_{name}"]
    for c, (f0, m) in enumerate(FCH):
        a["f_w_2"][:, 0:m, c, :] = i["L0_ffn_W2"][:, f0:f0 + m, :]
        a["f_par"][:, 0:m, 3 + c] = i["L0_ffn_b1"][:, f0:f0 + m]
        a["f_par"][:, 0:m, 6 + c] = i["L0_ffn_b1"][:, FF + f0:FF + f0 + m]
    qs, ks = i["L0_ffn_q_scale"], i["L0_ffn_k_scale"]
    swap = lambda w: np.concatenate([w[:, DH // 2:], w[:, :DH // 2]], axis=1)
    a["f_qk_s"] = T(np.broadcast_to(np.stack([qs, ks, swap(qs), swap(ks)], axis=1)[:, None], (NLAYER, P, 4, DH)))
    a["f_ctab"], a["f_mask"] = rotary_tables(), window_masks()
    a["a_w_disp"] = T(i["L1_attn_W_disp"].T)
    a["a_w_val"] = T(i["L1_attn_W_val"].T)
    a["a_w_proj"] = T(i["L1_attn_c_proj_w"].T)
    a["a_w_fused"] = np.zeros((2, 4, BD, 4, 2 * BD), np.float32)
    a["a_w_red"] = np.zeros((4, 2, BD, 2, 4), np.float32)
    a["a_w_pos"] = np.zeros((BD, 4, 2, BD), np.float32)
    for h in range(4):
        a["a_w_fused"][:, h, :, h, :] = i["L1_attn_strain_fused_w"].T
        a["a_w_red"][h, 0, :, 0, h] = i["L1_attn_bond_out_w"][0]
        a["a_w_red"][h, 1, :, 1, h] = i["L1_attn_damage_out_w"][0]
        a["a_w_pos"][:, h, 0, :] = i["L1_attn_pos_proj_w"].T
    a["a_w_fused"] = a["a_w_fused"].reshape(P, P)
    a["a_w_red"] = a["a_w_red"].reshape(P, 8)
    a["a_w_pos"] = a["a_w_pos"].reshape(BD, P)
    a["a_rel"] = T(i["L1_attn_rel_pos_emb"].T)
    a["a_bias"] = T(np.stack([np.tile(i["L1_attn_strain_fused_b"], 4),
                              np.tile(i["L1_attn_damage_out_b"], P)], axis=1))
    t, w = np.arange(P)[:, None], np.arange(HOR)[None, :]
    a["a_mask"] = np.where(t + w >= HOR - 1, 0.0, -1e30).astype(np.float32)
    chunks = lambda w, sh: T(np.concatenate([w.reshape(NE * NI, P), sh]).reshape(NCK + 1, P, P))
    a["e_w_g"] = T(chunks(i["L1_ffn_eg_w"], i["L1_ffn_sg_w"]).transpose(2, 0, 1))
    a["e_w_u"] = T(chunks(i["L1_ffn_eu_w"], i["L1_ffn_su_w"]).transpose(2, 0, 1))
    a["e_w_d"] = T(chunks(T(i["L1_ffn_ed_w"].transpose(0, 2, 1)), i["L1_ffn_sd_w"].T).transpose(1, 0, 2))
    a["e_w_r"] = T(i["L1_ffn_gate_w"].T)
    a["e_gb"] = T(np.broadcast_to(i["L1_ffn_gate_bias"], (P, NE)))
    return a


def kernel(**inputs):
    import concourse.bacc as _bacc
    from concourse.bass_utils import run_bass_kernel_spmd as _run

    nc = _bacc.Bacc("TRN2", target_bir_lowering=False, num_devices=1)
    arrays, d = {}, {}
    for name, a in layouts({k: np.asarray(v) for k, v in inputs.items()}).items():
        arrays[f"in_{name}_dram"] = a
        d[name] = nc.dram_tensor(f"in_{name}_dram", a.shape, mybir.dt.from_np(a.dtype), kind="ExternalInput").ap()
    out = nc.dram_tensor("out_0_dram", (P, NB, L), F32, kind="ExternalOutput").ap()
    program(nc, d, out)
    r = _run(nc, [arrays], core_ids=[0])
    return np.ascontiguousarray(r.results[0]["out_0_dram"].transpose(1, 2, 0))
```

```python
from contextlib import ExitStack

import numpy as np

import concourse.bass as bass
from concourse import mybir

F32 = mybir.dt.float32
BF16 = mybir.dt.bfloat16
I32 = mybir.dt.int32
ALU = mybir.AluOpType
ACT = mybir.ActivationFunctionType
AX = mybir.AxisListType.X

P = 128
NB = 8
L = 512
NT = L // P
EPS = 1e-5
BASE = 16
PHASES = ("norm", "mamba", "ffn", "norm", "attn", "moe")


class Chain:

    def __init__(self, eng, sem, per):
        self.eng, self.sem, self.per, self.n, self.base = eng, sem, per, 0, 0

    def start(self, step):
        self.n, self.base = 0, BASE + step * self.per

    def tick(self, ins):
        self.n += 1
        ins.then_inc(self.sem, 1)

    def wait(self):
        self.eng.wait_ge(self.sem, self.base + self.n)

    def link(self, ins):
        self.tick(ins)
        self.wait()

    def end(self):
        assert self.n == self.per, (self.sem, self.n)


def settle(eng, sem):
    eng.sem_inc(sem, 1)


class Stage:

    def __init__(self, nc, ctx, name):
        self.nc, self.ctx, self.name = nc, ctx, name

    def sb(self, name, shape, dt=F32):
        return self.ctx.enter_context(self.nc.sbuf_tensor(f"{self.name}_{name}", shape, dt))

    def banks(self, name, n):
        return self.ctx.enter_context(self.nc.psum_tensor(f"{self.name}_{name}", [P, n, 512], F32))

    def sems(self, names):
        q = {n: self.ctx.enter_context(self.nc.semaphore(f"{self.name}_{n}")) for n in names.split()}
        with self.nc.Block() as block:
            @block.sync
            def _(sp):
                for sem in q.values():
                    sp.sem_inc(sem, BASE)
        return q


RSQRT_LINKS = 12


def rsqrt(dve, chain, out, var, half, tmp):
    chain.link(dve.tensor_scalar(out.bitcast(I32), var.bitcast(I32), 1, None, ALU.logical_shift_right))
    chain.link(dve.tensor_scalar(out.bitcast(I32), out.bitcast(I32), -1.0, float(0x5F3759DF), ALU.mult, ALU.add))
    chain.link(dve.tensor_scalar(half, var, -0.5, None, ALU.mult))
    for _ in range(3):
        chain.link(dve.tensor_tensor(tmp, out, out, ALU.mult))
        chain.link(dve.tensor_tensor(tmp, tmp, half, ALU.mult))
        chain.link(dve.scalar_tensor_tensor(out=out, in0=tmp, scalar=1.5, in1=out, op0=ALU.add, op1=ALU.mult))


def layernorm_stage(nc, g, name):
    acc, xn, ident = g["acc"], g["xn"], g["ident"]
    with ExitStack() as ctx:
        s = Stage(nc, ctx, name)
        xs = s.sb("xs", [P, L])
        stats = s.sb("stats", [P, NT, 6])
        mv = s.sb("mv", [P, NT, 2])
        rstd = s.sb("rstd", [P, NT])
        half = s.sb("half", [P, NT])
        tmp = s.sb("tmp", [P, NT])
        xh = s.sb("xh", [P, NT, P])
        tok = s.banks("tok", 1)
        fea = s.banks("fea", 1)
        q = s.sems("copied turned normed back stored dch")
        copied, turned, normed, back, stored, dch = q.values()
        with nc.Block() as block:
            @block.scalar
            def _(act):
                with act.Fori(0, NB) as b:
                    act.wait_ge(turned, BASE + b)
                    act.activation(xs[:, :], acc[:, b, :], ACT.Copy).then_inc(copied, 1)
                    act.wait_ge(back, BASE + b + 1)
                    act.activation(xn[:, b, :], fea[:, 0, :], ACT.Copy).then_inc(stored, 1)

            @block.tensor
            def _(pe):
                with pe.Fori(0, NB) as b:
                    pe.wait_ge(copied, BASE + b + 1)
                    for k in range(NT):
                        mm = pe.transpose(tok[:, 0, k * P:(k + 1) * P], xs[:, k * P:(k + 1) * P], ident[:, :])
                    mm.then_inc(turned, 1)
                    pe.wait_ge(normed, BASE + b + 1)
                    pe.wait_ge(stored, BASE + b)
                    for k in range(NT):
                        mm = pe.transpose(fea[:, 0, k * P:(k + 1) * P], xh[:, k, :], ident[:, :])
                    mm.then_inc(back, 1)

            @block.vector
            def _(dve):
                c = Chain(dve, dch, 2 * NT + 1 + RSQRT_LINKS)
                with dve.Fori(0, NB) as b:
                    c.start(b)
                    dve.wait_ge(turned, BASE + b + 1)
                    for k in range(NT):
                        c.tick(dve.bn_stats(stats[:, k, :], tok[:, 0, k * P:(k + 1) * P]))
                    c.wait()
                    dve.memset(tmp[:, :], 0.0)
                    for k in range(NT):
                        c.tick(dve.bn_aggr(mv[:, k, :], stats[:, k, :]))
                    c.wait()
                    c.link(dve.tensor_scalar(mv[:, :, 1], mv[:, :, 1], EPS, None, ALU.add))
                    rsqrt(dve, c, rstd[:, :], mv[:, :, 1], half[:, :], tmp[:, :])
                    for k in range(NT):
                        ins = dve.tensor_scalar(xh[:, k, :], tok[:, 0, k * P:(k + 1) * P], mv[:, k, 0:1],
                                                rstd[:, k:k + 1], ALU.subtract, ALU.mult)
                    ins.then_inc(normed, 1)
                    c.end()


DI, DS, DC, DR = 256, 16, 4, 8


def mamba_stage(nc, g, d):
    acc, xn, ident = g["acc"], g["xn"], g["ident"]
    NH = DI // P
    NX = DR + 2 * DS
    with ExitStack() as ctx:
        s = Stage(nc, ctx, "ma")
        w_in = s.sb("w_in", [P, 2 * DI])
        w_x = s.sb("w_x", [P, NH, NX])
        w_dt = s.sb("w_dt", [DR, DI])
        w_out = s.sb("w_out", [P, NH, P])
        par = s.sb("par", [P, NH, DC + 3])
        alog = s.sb("alog", [P, NH, DS])
        aexp = s.sb("aexp", [P, NH, DS])
        u = s.sb("u", [P, NH, DC - 1 + L])
        cv = s.sb("cv", [P, NH, L])
        uc = s.sb("uc", [P, NH, L])
        zg = s.sb("zg", [P, NH, L])
        xd = s.sb("xd", [NX, L])
        v = s.sb("v", [P, NH, L])
        e = s.sb("e", [P, NH, L])
        dt = s.sb("dt", [P, NH, L])
        dtu = s.sb("dtu", [P, NH, L])
        bs = s.sb("bs", [P, 2, L])
        da = s.sb("da", [P, 4, L])
        db = s.sb("db", [P, 4, L])
        h = s.sb("h", [P, 2, L])
        hc = s.sb("hc", [P, 4, L])
        y = s.sb("y", [P, NH, L])
        BC = s.banks("BC", 4)
        Y = s.banks("Y", 2)
        M = s.banks("M", 2)
        q = s.sems("loaded aready acopy uzdone uread zread upad conv ucdone xdone xread dtdone dtread dtready "
                   "dtuready bcdone bcopied bfree cfree daready dafree dbready dbfree hcready hcfree ydone yread outdone "
                   "outread dch ach")
        NS = DS * NH
        with nc.Block() as block:
            @block.sync
            def _(sp):
                for dst, src in ((w_in, "m_w_in"), (w_x, "m_w_x"), (w_dt, "m_w_dt"), (w_out, "m_w_out"),
                                 (par, "m_par"), (alog, "m_alog")):
                    sp.dma_start(dst[:], d[src]).then_inc(q["loaded"], 16)

            @block.scalar
            def _(act):
                act.wait_ge(q["loaded"], BASE + 6 * 16)
                act.activation(aexp[:], alog[:], ACT.Exp).then_inc(q["aready"], 1)
                c = Chain(act, q["ach"], 3)
                with act.Fori(0, NB) as b:
                    c.start(b)
                    act.wait_ge(q["upad"], BASE + 1)
                    act.wait_ge(q["uzdone"], BASE + b + 1)
                    act.wait_ge(q["conv"], BASE + b * NH)
                    act.activation(u[:, :, DC - 1:], BC[:, 0:NH, :], ACT.Copy).then_inc(q["uread"], 1)
                    act.wait_ge(q["yread"], BASE + b)
                    act.activation(zg[:], BC[:, NH:2 * NH, :], ACT.Silu).then_inc(q["zread"], 1)
                    act.wait_ge(q["conv"], BASE + (b + 1) * NH)
                    act.activation(uc[:], cv[:], ACT.Silu).then_inc(q["ucdone"], 1)
                    act.wait_ge(q["xdone"], BASE + b + 1)
                    act.activation(xd[:, :], M[0:NX, 0, :], ACT.Copy).then_inc(q["xread"], 1)
                    act.wait_ge(q["dtdone"], BASE + b + 1)
                    for k in range(NH):
                        ins = act.activation(v[:, k, :], M[:, k, :], ACT.Identity, bias=par[:, k, DC + 1:DC + 2])
                    c.link(ins)
                    c.link(act.activation(e[:], v[:], ACT.Abs))
                    c.link(act.activation(e[:], e[:], ACT.Exp, scale=-1.0))
                    act.activation(e[:], e[:], ACT.Ln, bias=1.0).then_inc(q["dtread"], 1)
                    act.wait_ge(q["dtready"], BASE + b + 1)
                    act.wait_ge(q["acopy"], BASE + 1)
                    for n in range(DS):
                        act.wait_ge(q["bcdone"], BASE + b * DS + n + 1)
                        act.wait_ge(q["bfree"], BASE + b * DS + n)
                        act.activation(bs[:, n % 2, :], BC[:, 2 * (n % 2), :], ACT.Copy).then_inc(q["bcopied"], 1)
                        for k in range(NH):
                            act.wait_ge(q["dafree"], BASE + b * NS + NH * n + k + 1)
                            act.activation(da[:, (NH * n + k) % 4, :], dt[:, k, :], ACT.Exp,
                                           scale=aexp[:, k, n:n + 1]).then_inc(q["daready"], 1)
                    c.end()

            @block.gpsimd
            def _(pool):
                pool.memset(u[:], 0.0).then_inc(q["upad"], 1)
                pool.wait_ge(q["aready"], BASE + 1)
                pool.tensor_scalar(aexp[:], aexp[:], -1.0, None, ALU.mult).then_inc(q["acopy"], 1)
                pool.sem_inc(q["bfree"], 1)
                with pool.Fori(0, NB) as b:
                    pool.wait_ge(q["dtuready"], BASE + b + 1)
                    for n in range(DS):
                        pool.wait_ge(q["bcopied"], BASE + b * DS + n + 1)
                        for k in range(NH):
                            pool.wait_ge(q["dbfree"], BASE + b * NS + NH * n + k + 1)
                            ins = pool.tensor_tensor(db[:, (NH * n + k) % 4, :], dtu[:, k, :], bs[:, n % 2, :], ALU.mult)
                            ins.then_inc(q["dbready"], 1)
                        pool.wait_ge(q["dbready"], BASE + b * NS + NH * (n + 1))
                        pool.sem_inc(q["bfree"], 1)

            @block.tensor
            def _(pe):
                pe.wait_ge(q["loaded"], BASE + 6 * 16)
                with pe.Fori(0, NB) as b:
                    pe.wait_ge(q["cfree"], BASE + b * NS)
                    for k in range(2 * NH):
                        mm = pe.matmul(BC[:, k, :], w_in[:, k * P:(k + 1) * P], xn[:, b, :], start=True, stop=True)
                    mm.then_inc(q["uzdone"], 1)
                    pe.wait_ge(q["ucdone"], BASE + b + 1)
                    pe.wait_ge(q["outread"], BASE + b)
                    for k in range(NH):
                        mm = pe.matmul(M[0:NX, 0, :], w_x[:, k, :], uc[:, k, :], start=(k == 0), stop=(k == NH - 1))
                    mm.then_inc(q["xdone"], 1)
                    pe.wait_ge(q["xread"], BASE + b + 1)
                    for k in range(NH):
                        mm = pe.matmul(M[:, k, :], w_dt[:, k * P:(k + 1) * P], xd[0:DR, :], start=True, stop=True)
                    mm.then_inc(q["dtdone"], 1)
                    pe.wait_ge(q["zread"], BASE + b + 1)

                    def broadcast(n):
                        if n >= 2:
                            pe.wait_ge(q["bcopied"], BASE + b * DS + n - 1)
                            pe.wait_ge(q["cfree"], BASE + b * NS + NH * (n - 1))
                        for j in range(2):
                            col = DR + j * DS + n
                            mm = pe.matmul(BC[:, 2 * (n % 2) + j, :], ident[0:NX, col:col + 1].broadcast_to([NX, P]),
                                           xd[:, :], start=True, stop=True)
                        mm.then_inc(q["bcdone"], 1)

                    broadcast(0)
                    pe.wait_ge(q["yread"], BASE + b)
                    for n in range(DS):
                        if n + 1 < DS:
                            broadcast(n + 1)
                        for k in range(NH):
                            pe.wait_ge(q["hcready"], BASE + b * NS + NH * n + k + 1)
                            pe.matmul(Y[:, k, :], ident[:, :], hc[:, (NH * n + k) % 4, :], start=(n == 0),
                                      stop=(n == DS - 1)).then_inc(q["hcfree"], 1)
                    pe.wait_ge(q["yread"], BASE + b + 1)
                    for k in range(NH):
                        mm = pe.matmul(M[:, 0, :], w_out[:, k, :], y[:, k, :], start=(k == 0), stop=(k == NH - 1))
                    mm.then_inc(q["outdone"], 1)

            @block.vector
            def _(dve):
                c = Chain(dve, q["dch"], (DC - 1) * NH + 2 + NS + 1)
                dve.wait_ge(q["loaded"], BASE + 6 * 16)
                for sem in ("dafree", "dbfree", "hcfree"):
                    dve.sem_inc(q[sem], 4)
                with dve.Fori(0, NB) as b:
                    c.start(b)
                    dve.wait_ge(q["uread"], BASE + b + 1)
                    for k in range(NH):
                        c.link(dve.tensor_scalar(cv[:, k, :], u[:, k, 0:L], par[:, k, 0:1], par[:, k, DC:DC + 1],
                                                 ALU.mult, ALU.add))
                        for t in range(1, DC):
                            ins = dve.scalar_tensor_tensor(out=cv[:, k, :], in0=u[:, k, t:t + L],
                                                           scalar=par[:, k, t:t + 1], in1=cv[:, k, :],
                                                           op0=ALU.mult, op1=ALU.add)
                            if t < DC - 1:
                                c.link(ins)
                        ins.then_inc(q["conv"], 1)
                    dve.wait_ge(q["dtread"], BASE + b + 1)
                    c.link(dve.tensor_scalar(v[:], v[:], 0.0, None, ALU.max))
                    ins = dve.tensor_tensor(dt[:], v[:], e[:], ALU.add)
                    ins.then_inc(q["dtready"], 1)
                    dve.wait_ge(q["dtready"], BASE + b + 1)
                    dve.tensor_tensor(dtu[:], dt[:], uc[:], ALU.mult).then_inc(q["dtuready"], 1)
                    for n in range(DS):
                        for k in range(NH):
                            i = NH * n + k
                            dve.wait_ge(q["daready"], BASE + b * NS + i + 1)
                            dve.wait_ge(q["dbready"], BASE + b * NS + i + 1)
                            ins = dve.tensor_tensor_scan(h[:, i % 2, :], da[:, i % 4, :], db[:, i % 4, :], 0.0,
                                                         ALU.mult, ALU.add)
                            c.link(ins)
                            dve.sem_inc(q["dafree"], 1)
                            dve.sem_inc(q["dbfree"], 1)
                            dve.wait_ge(q["hcfree"], BASE + b * NS + i + 1)
                            dve.wait_ge(q["bcdone"], BASE + b * DS + n + 1)
                            dve.tensor_tensor(hc[:, i % 4, :], h[:, i % 2, :], BC[:, 2 * (n % 2) + 1, :],
                                              ALU.mult).then_inc(q["hcready"], 1)
                            dve.wait_ge(q["hcready"], BASE + b * NS + i + 1)
                            dve.sem_inc(q["cfree"], 1)
                    dve.wait_ge(q["hcfree"], BASE + (b + 1) * NS + 4)
                    for k in range(NH):
                        ins = dve.scalar_tensor_tensor(out=y[:, k, :], in0=uc[:, k, :], scalar=par[:, k, DC + 2:DC + 3],
                                                       in1=Y[:, k, :], op0=ALU.mult, op1=ALU.add)
                    c.link(ins)
                    dve.tensor_tensor(y[:], y[:], zg[:], ALU.mult).then_inc(q["yread"], 1)
                    dve.wait_ge(q["outdone"], BASE + b + 1)
                    ins = dve.tensor_tensor(acc[:, b, :], acc[:, b, :], M[:, 0, :], ALU.add)
                    c.link(ins)
                    dve.sem_inc(q["outread"], 1)
                    c.end()


NLAYER, NHEAD, DH, WIN = 6, 16, 64, 32
NCH = NHEAD // 2
INNER = NHEAD * DH
FF = P * 4 * 2 // 3
FCH = [(c, min(P, FF - c)) for c in range(0, FF, P)]
NQK = 2 * INNER // L
NPC = 3 * INNER // L
NW = L // WIN
WT = P // WIN


def ffn_stage(nc, g, d, park):
    acc, xn, ident = g["acc"], g["xn"], g["ident"]
    with ExitStack() as ctx:
        s = Stage(nc, ctx, "ff")
        w_qkv = s.sb("w_qkv", [P, 3 * INNER])
        w_o = s.sb("w_o", [P, NCH, P])
        w_1 = s.sb("w_1", [P, 2 * FF])
        w_2 = s.sb("w_2", [P, len(FCH), P])
        par = s.sb("par", [P, 3 + 2 * len(FCH)])
        qk_s = s.sb("qk_s", [P, 4, DH])
        tab = s.sb("tab", [P, 4, NT, DH])
        mask_f = s.sb("mask_f", [P, 2, DH])
        mask = s.sb("mask", [P, 2, NCH, DH], BF16)
        ident_b = s.sb("ident_b", [P, P], BF16)
        xs = s.sb("xs", [P, L])
        xs1 = s.sb("xs1", [P, L])
        raw = s.sb("raw", [P, 2, NQK, L])
        sq = s.sb("sq", [P, NQK * L])
        n2 = s.sb("n2", [P, 2 * NHEAD])
        inv = s.sb("inv", [P, 2 * NHEAD])
        half = s.sb("half", [P, 2 * NHEAD])
        tmp = s.sb("tmp", [P, 2 * NHEAD])
        rc = s.sb("rc", [P, 2, NQK * L])
        qT = s.sb("qT", [P, 2, NCH, P])
        kT = s.sb("kT", [P, NCH, WIN + L])
        v = s.sb("v", [P, 2, INNER])
        v2 = s.sb("v2", [P, NW + 1, NCH * DH])
        mx = s.sb("mx", [P, NHEAD])
        ssum = s.sb("ssum", [P, NHEAD])
        pr = s.sb("pr", [P, 2, NCH, 2, DH])
        pT = s.sb("pT", [P, NCH, P])
        oT = acc
        stats = s.sb("stats", [P, NT, 6])
        mv = s.sb("mv", [P, NT, 2])
        xh = s.sb("xh", [P, NT, P])
        x2 = s.sb("x2", [P, L])
        gg = s.sb("gg", [P, L])
        hh = s.sb("hh", [P, 2, L])
        QA = s.banks("QA", 2)
        TR = s.banks("TR", 2)
        S = s.banks("S", 2)
        O = s.banks("O", 2)
        q = s.sems("const tabfree w_in masks tabs padded xs_ready qa_fill qa_read0 qa_read1 raw_ready sq_ready "
                   "n2_done rs_ready rc_ready tr_fill tr_read0 tr_read1 qk_turned s_fill s_read p_exp p_sum p_ready "
                   "p_read pt_ready o_fill o_read v_ready v2_in0 v2_in1 x1_ready xh_ready x2_ready g_ready "
                   "h_ready h_used ff_done wo_done xs1_ready parked back dch held")
        qa_read, tr_read, v2_in = ([q[f"{n}{k}"] for k in range(2)] for n in ("qa_read", "tr_read", "v2_in"))

        FFS = {2: [("Wo", 0, 1)], 3: [("tok", 0, 1), ("fea", 0, 1), ("W", 0, 1)]}
        TLINKS = {"X": 2 + RSQRT_LINKS + 3, "Y": 4, "tok": 2 * NT + 1 + RSQRT_LINKS}

        def a_pass(steps):
            order = []
            for x, ff in steps:
                f = {k[0]: k for k in ff}
                names = {k[0]: k for k in x}
                for key in ("tok", "X", "Wo", "fea", "Y", "Z", "W"):
                    order += [e for e in (f.get(key), names.get(key)) if e]
            qa, tr = [], []
            for kind, t, back in order:
                if kind == "X":
                    qa += [("X", t, pc) for pc in range(NPC)]
                if kind == "Wo":
                    qa += [("Wo",)]
                if kind == "W":
                    qa += [("W1", c, j) for c in range(len(FCH)) for j in range(2)] + [("W2",)]
                tr += [(kind, t, j) for j in range({"Y": NQK, "Z": 2, "tok": 1, "fea": 1}.get(kind, 0))]
            links = sum(TLINKS.get(kind, 0) for kind, _, _ in order)
            return {"steps": steps, "order": order, "qa": {k: n for n, k in enumerate(qa)},
                    "tr": {k: n for n, k in enumerate(tr)}, "links": links}

        def xyz(i, lo, hi):
            return [("XYZ"[lag], (i - lag) % NT, 0 if i >= lag else 1) for lag in range(3) if lo <= i - lag < hi]

        first = a_pass([(xyz(i, 0, NT), []) for i in range(NT)])
        loop = a_pass([(xyz(i, -NT, NT), FFS.get(i, [])) for i in range(NT)])
        last = a_pass([(xyz(i, -NT, 0), FFS.get(i, [])) for i in range(NT)])
        QN, TN, LINKS = len(loop["qa"]), len(loop["tr"]), loop["links"]
        first["before"] = (0, 0, 0)
        loop["before"] = last["before"] = tuple(-len(x) if not isinstance(x, int) else -x
                                                for x in (last["qa"], last["tr"], last["links"]))
        assert all(len(p[r]) % 2 == 0 for p in (first, loop, last) for r in ("qa", "tr"))
        assert len(first["qa"]) + len(last["qa"]) == QN and len(first["tr"]) + len(last["tr"]) == TN
        NLOAD = 7

        def batches(eng, body, l):
            body(first, l * NB, 0)
            with eng.Fori(1, NB) as b:
                body(loop, l * NB + b, b)
            body(last, l * NB + NB, NB)

        def ring(p, n, name, key):
            N, before, k = (QN, p["before"][0], p["qa"][key]) if name == "qa" else (TN, p["before"][1], p["tr"][key])
            return k % 2, n * (N // 2) + (before // 2 + k // 2), n * N + (before + k)

        def fill_qa(pe, p, n, key):
            k, bank_fills, _ = ring(p, n, "qa", key)
            pe.wait_ge(qa_read[k], BASE + bank_fills)
            return QA[:, k, :]

        def fill_tr(pe, p, n, key):
            k, bank_fills, _ = ring(p, n, "tr", key)
            pe.wait_ge(tr_read[k], BASE + bank_fills)
            return TR[:, k, :]

        def filled_qa(eng, p, n, key):
            k, _, fills = ring(p, n, "qa", key)
            eng.wait_ge(q["qa_fill"], BASE + 1 + fills)
            return QA[:, k, :], qa_read[k]

        def filled_tr(eng, p, n, key):
            k, _, fills = ring(p, n, "tr", key)
            eng.wait_ge(q["tr_fill"], BASE + 1 + fills)
            return TR[:, k, :], tr_read[k]

        def is_read(eng, p, n, name, key):
            k, bank_fills, _ = ring(p, n, name, key)
            eng.wait_ge((qa_read if name == "qa" else tr_read)[k], BASE + 1 + bank_fills)

        with nc.Block() as block:
            @block.sync
            def _(sp):
                sp.dma_start(mask_f[:], d["f_mask"]).then_inc(q["const"], 16)
                sp.dma_start(park, acc[:, :, :]).then_inc(q["parked"], 16)
                with sp.Fori(0, NLAYER) as l:
                    sp.wait_ge(q["ff_done"], BASE + l * NB)
                    settle(sp, q["held"])
                    for dst, src in ((w_qkv, "f_w_qkv"), (w_o, "f_w_o"), (w_1, "f_w_1"), (w_2, "f_w_2"),
                                     (par, "f_par"), (qk_s, "f_qk_s")):
                        sp.dma_start(dst[:], d[src][l]).then_inc(q["w_in"], 16)
                    sp.dma_start(tab[:], d["f_ctab"]).then_inc(q["w_in"], 16)
                    with sp.Fori(0, NB) as b:
                        n = l * NB + b
                        for t in range(NT):
                            sp.wait_ge(q["v_ready"], BASE + n * NT + t + 1)
                            settle(sp, q["held"])
                            sp.wait_ge(q["o_fill"], BASE + n * NT + min(t - 2, 0))
                            settle(sp, q["held"])
                            for z in range(2):
                                for c in range(2):
                                    r0 = 64 * z + WIN * c
                                    for w in range(WT):
                                        sp.dma_start(v2[r0:r0 + WIN, WT * t + w + 1 - c, :],
                                                     v[WIN * w:WIN * w + WIN, t % 2, z * L:z * L + L]
                                                     ).then_inc(v2_in[t % 2], 16)
                sp.wait_ge(q["wo_done"], BASE + NLAYER * NB)
                sp.dma_start(acc[:, :, :], park).then_inc(q["back"], 16)

            @block.gpsimd
            def _(pool):
                pool.memset(v2[:, 0, :], 0.0)
                pool.memset(kT[:, :, 0:WIN], 0.0)
                pool.memset(xs1[:, :], 0.0)
                pool.memset(xs[:, :], 0.0).then_inc(q["padded"], 1)
                pool.wait_ge(q["const"], BASE + 16)
                pool.tensor_copy(ident_b[:, :], ident[:, :])
                for j in range(2):
                    for c in range(NCH):
                        ins = pool.tensor_copy(mask[:, j, c, :], mask_f[:, j, :])
                ins.then_inc(q["masks"], 1)
                with pool.Fori(0, NLAYER) as l:
                    pool.wait_ge(q["w_in"], BASE + (l + 1) * NLOAD * 16)
                    for k in range(4):
                        ins = pool.tensor_tensor(tab[:, k, :, :], tab[:, k, :, :],
                                                 qk_s[:, k:k + 1, :].broadcast_to([P, NT, DH]), ALU.mult)
                    ins.then_inc(q["tabs"], 1)
                    pool.wait_ge(q["tabs"], BASE + l + 1)
                    settle(pool, q["held"])

                    def body(p, n, b):
                        def rotate(t):
                            pool.wait_ge(q["raw_ready"], BASE + n * NT + t + 1)
                            pool.wait_ge(q["n2_done"], BASE + n * NT + t + 1)
                            for k in range(2):
                                x = raw[:, t % 2, 2 * k:2 * k + 2, :].rearrange("p c (h z e) -> p (c h) z e", z=2, e=DH // 2)
                                y = sq[:, k * INNER:(k + 1) * INNER].rearrange("p (h z e) -> p h z e", z=2, e=DH // 2)
                                for z in range(2):
                                    e0 = z * (DH // 2)
                                    ins = pool.tensor_tensor(
                                        y[:, :, z, :], x[:, :, 1 - z, :],
                                        tab[:, 2 + k, t:t + 1, e0:e0 + DH // 2].broadcast_to([P, NHEAD, DH // 2]), ALU.mult)
                            ins.then_inc(q["rs_ready"], 1)

                        def norm_p(t, n):
                            pool.wait_ge(q["p_sum"], BASE + n * NT + t + 1)
                            x = pr[:, t % 2, :, :, :].rearrange("p c z e -> p (c z) e")
                            pool.tensor_tensor(x, x, ssum[:, :].unsqueeze(2).broadcast_to([P, NHEAD, DH]),
                                               ALU.mult).then_inc(q["p_ready"], 1)

                        for step, _ in p["steps"]:
                            for kind, t, back in step:
                                if kind == "X":
                                    rotate(t)
                                if kind == "Y":
                                    norm_p(t, n - back)

                    batches(pool, body, l)

            @block.scalar
            def _(act):
                act.wait_ge(q["padded"], BASE + 1)
                act.wait_ge(q["parked"], BASE + 16)
                with act.Fori(0, NLAYER) as l:
                    act.wait_ge(q["w_in"], BASE + (l + 1) * NLOAD * 16)

                    def body(p, n, b):
                        def shift(dst, b, done):
                            settle(act, q["held"])
                            act.activation(dst[0:64, :], xn[0:64, b, :], ACT.Copy)
                            act.activation(dst[64:P, 1:L], xn[64:P, b, 0:L - 1], ACT.Copy).then_inc(done, 1)

                        def copy_qkv(t):
                            act.wait_ge(q["rc_ready"], BASE + n * NT + (t - 1))
                            for pc in range(NPC):
                                bank, read = filled_qa(act, p, n, ("X", t, pc))
                                if pc == NQK:
                                    act.wait_ge(v2_in[t % 2], BASE + (2 * n + t // 2) * 256)
                                dst = raw[:, t % 2, pc, :] if pc < NQK else v[:, t % 2, (pc - NQK) * L:(pc - NQK + 1) * L]
                                act.activation(dst, bank, ACT.Copy).then_inc(read, 1)
                                if pc == NQK - 1:
                                    is_read(act, p, n, "qa", ("X", t, pc - 1))
                                    is_read(act, p, n, "qa", ("X", t, pc))
                                    act.wait_ge(q["rc_ready"], BASE + n * NT + t)
                                    act.activation(sq[:, :], raw[:, t % 2, :, :], ACT.Square).then_inc(q["sq_ready"], 1)
                            act.wait_ge(q["sq_ready"], BASE + n * NT + t + 1)
                            act.sem_inc(q["raw_ready"], 1)
                            is_read(act, p, n, "qa", ("X", t, NPC - 2))
                            is_read(act, p, n, "qa", ("X", t, NPC - 1))
                            act.sem_inc(q["v_ready"], 1)

                        def turn_qk(t, m):
                            act.wait_ge(q["s_fill"], BASE + m * NT + (t - 1))
                            for j in range(NQK):
                                bank, read = filled_tr(act, p, n, ("Y", t, j))
                                src = bank.rearrange("p (c x) -> p c x", x=P)
                                c0 = 4 * (j % 2)
                                dst = (qT[:, t % 2, c0:c0 + 4, :] if j < NQK // 2 else
                                       kT[:, c0:c0 + 4, WIN + t * P:WIN + (t + 1) * P])
                                act.activation(dst, src, ACT.Copy).then_inc(read, 1)
                            for j in (NQK - 2, NQK - 1):
                                is_read(act, p, n, "tr", ("Y", t, j))
                            act.sem_inc(q["qk_turned"], 1)

                        def turn_p(t, m):
                            act.wait_ge(q["o_fill"], BASE + m * NT + t)
                            for j in range(2):
                                bank, read = filled_tr(act, p, n, ("Z", t, j))
                                act.activation(pT[:, 4 * j:4 * j + 4, :], bank.rearrange("p (c x) -> p c x", x=P),
                                               ACT.Copy).then_inc(read, 1)
                            for j in range(2):
                                is_read(act, p, n, "tr", ("Z", t, j))
                            act.sem_inc(q["pt_ready"], 1)
                            if t == 0:
                                act.wait_ge(q["wo_done"], BASE + m)
                            act.wait_ge(q["o_fill"], BASE + m * NT + t + 1)
                            act.activation(oT[:, :, t * P:(t + 1) * P],
                                           O[:, :, :].rearrange("p k (c x) -> p (k c) x", x=P),
                                           ACT.Copy).then_inc(q["o_read"], 1)

                        def exp_p(t, m):
                            act.wait_ge(q["s_read"], BASE + m * NT + t + 1)
                            act.activation(pr[:, t % 2, :, :, :], pr[:, t % 2, :, :, :], ACT.Exp,
                                           scale=8.0).then_inc(q["p_exp"], 1)

                        for step, ff in p["steps"]:
                            ff = {k for k, _, _ in ff}
                            for kind, t, back in step:
                                if kind == "X":
                                    if t == 0:
                                        act.wait_ge(q["ff_done"], BASE + n - NB)
                                        shift(xs, b, q["xs_ready"])
                                    copy_qkv(t)
                            if "fea" in ff:
                                bank, read = filled_tr(act, p, n, ("fea", 0, 0))
                                act.activation(x2[:, :], bank, ACT.Identity, scale=par[:, 0:1],
                                               bias=par[:, 1:2]).then_inc(read, 1)
                                is_read(act, p, n, "tr", ("fea", 0, 0))
                                act.sem_inc(q["x2_ready"], 1)
                            for kind, t, back in step:
                                if kind == "Y":
                                    turn_qk(t, n - back)
                                if kind == "Z":
                                    turn_p(t, n - back)
                            for kind, t, back in step:
                                if kind == "Y":
                                    exp_p(t, n - back)
                            if "Wo" in ff:
                                act.wait_ge(q["x1_ready"], BASE + n)
                                shift(xs1, b - 1, q["xs1_ready"])
                            if "W" in ff:
                                for c, (_, m) in enumerate(FCH):
                                    bank, read = filled_qa(act, p, n, ("W1", c, 0))
                                    act.wait_ge(q["h_ready"], BASE + (n - 1) * len(FCH) + c)
                                    act.activation(gg[0:m, :], bank[0:m, :], ACT.Gelu, bias=par[0:m, 6 + c:7 + c]).then_inc(read, 1)
                                    is_read(act, p, n, "qa", ("W1", c, 0))
                                    act.sem_inc(q["g_ready"], 1)

                    batches(act, body, l)

            @block.tensor
            def _(pe):
                pe.wait_ge(q["masks"], BASE + 1)
                with pe.Fori(0, NLAYER) as l:
                    pe.wait_ge(q["w_in"], BASE + (l + 1) * NLOAD * 16)
                    settle(pe, q["held"])

                    def body(p, n, b):
                        def project(t, _):
                            if t == 0:
                                pe.wait_ge(q["xs_ready"], BASE + n + 1)
                            for pc in range(NPC):
                                bank = fill_qa(pe, p, n, ("X", t, pc))
                                pe.matmul(bank, xs[:, t * P:(t + 1) * P], w_qkv[:, pc * L:(pc + 1) * L],
                                          start=True, stop=True).then_inc(q["qa_fill"], 1)

                        def scores(t, m):
                            pe.wait_ge(q["rc_ready"], BASE + m * NT + t + 1)
                            for j in range(NQK):
                                bank = fill_tr(pe, p, n, ("Y", t, j))
                                for c in range(4):
                                    mm = pe.transpose(bank[:, c * P:(c + 1) * P],
                                                      rc[:, t % 2, j * L + c * P:j * L + (c + 1) * P], ident[:, :])
                                mm.then_inc(q["tr_fill"], 1)
                            pe.wait_ge(q["qk_turned"], BASE + m * NT + t + 1)
                            pe.wait_ge(q["s_read"], BASE + m * NT + t)
                            for z in range(2):
                                pe.matmul(S[:, z, :], ident_b[:, :], mask[:, 0 if t == 0 else 1, :, :], start=True,
                                          stop=False, skip_group_check=True)
                            for c in range(NCH):
                                for z in range(2):
                                    for w in range(WT):
                                        mm = pe.matmul(S[WIN * w:WIN * w + WIN, z, c * DH:(c + 1) * DH],
                                                       qT[64 * z:64 * z + 64, t % 2, c, WIN * w:WIN * w + WIN],
                                                       kT[64 * z:64 * z + 64, c, t * P + WIN * w:t * P + WIN * w + 2 * WIN],
                                                       start=False, stop=(c == NCH - 1), skip_group_check=True)
                            mm.then_inc(q["s_fill"], 1)

                        def attend(t, m):
                            pe.wait_ge(q["p_ready"], BASE + m * NT + t + 1)
                            for j in range(2):
                                bank = fill_tr(pe, p, n, ("Z", t, j))
                                for c in range(4):
                                    mm = pe.transpose(bank[:, c * P:(c + 1) * P], pr[:, t % 2, 4 * j + c, :, :], ident[:, :])
                                mm.then_inc(q["tr_fill"], 1)
                            pe.wait_ge(q["pt_ready"], BASE + m * NT + t + 1)
                            pe.wait_ge(v2_in[t % 2], BASE + (2 * m + (t // 2 + 1)) * 256)
                            pe.wait_ge(q["o_read"], BASE + m * NT + t)
                            settle(pe, q["held"])
                            for c in range(NCH):
                                for w in range(WT):
                                    for z in range(2):
                                        rows = slice(64 * z, 64 * z + 64)
                                        mm = pe.matmul(O[rows, c // 4, (c % 4) * P + WIN * w:(c % 4) * P + WIN * (w + 1)],
                                                       v2[rows, WT * t + w, c * DH:(c + 1) * DH],
                                                       pT[rows, c, WIN * w:WIN * (w + 1)], start=True, stop=True,
                                                       skip_group_check=True)
                            mm.then_inc(q["o_fill"], 1)

                        def output(_, m):
                            pe.wait_ge(q["o_read"], BASE + (m + 1) * NT)
                            bank = fill_qa(pe, p, n, ("Wo",))
                            for c in range(NCH):
                                mm = pe.matmul(bank, w_o[:, c, :], oT[:, c, :], start=(c == 0), stop=(c == NCH - 1))
                            mm.then_inc(q["qa_fill"], 1)
                            pe.wait_ge(q["qa_fill"], BASE + 1 + ring(p, n, "qa", ("Wo",))[2])
                            pe.sem_inc(q["wo_done"], 1)

                        def token_major(_, m):
                            pe.wait_ge(q["xs1_ready"], BASE + m + 1)
                            bank = fill_tr(pe, p, n, ("tok", 0, 0))
                            for t in range(NT):
                                mm = pe.transpose(bank[:, t * P:(t + 1) * P], xs1[:, t * P:(t + 1) * P], ident[:, :])
                            mm.then_inc(q["tr_fill"], 1)

                        def feature_major(_, m):
                            pe.wait_ge(q["xh_ready"], BASE + m + 1)
                            bank = fill_tr(pe, p, n, ("fea", 0, 0))
                            for t in range(NT):
                                mm = pe.transpose(bank[:, t * P:(t + 1) * P], xh[:, t, :], ident[:, :])
                            mm.then_inc(q["tr_fill"], 1)

                        def feed_forward(_, m):
                            pe.wait_ge(q["x2_ready"], BASE + m + 1)
                            for c, (f0, f) in enumerate(FCH):
                                for j in range(2):
                                    bank = fill_qa(pe, p, n, ("W1", c, j))
                                    c0 = f0 + (1 - j) * FF
                                    pe.matmul(bank[0:f, :], w_1[:, c0:c0 + f], x2[:, :], start=True,
                                              stop=True).then_inc(q["qa_fill"], 1)
                            bank = fill_qa(pe, p, n, ("W2",))
                            for c, (_, f) in enumerate(FCH):
                                pe.wait_ge(q["h_ready"], BASE + m * len(FCH) + c + 1)
                                mm = pe.matmul(bank, w_2[0:f, c, :], hh[0:f, c % 2, :], start=(c == 0), stop=(c == len(FCH) - 1))
                                if c < len(FCH) - 1:
                                    mm.then_inc(q["h_used"], 1)
                            mm.then_inc(q["qa_fill"], 1)

                        run = {"X": project, "Y": scores, "Z": attend, "Wo": output, "tok": token_major,
                               "fea": feature_major, "W": feed_forward}
                        for kind, t, back in p["order"]:
                            run[kind](t, n - back)

                    batches(pe, body, l)

            @block.vector
            def _(dve):
                with dve.Fori(0, NLAYER) as l:
                    dve.wait_ge(q["tabs"], BASE + l + 1)
                    settle(dve, q["held"])

                    def body(p, n, b):
                        ch = Chain(dve, q["dch"], p["links"])
                        ch.base = BASE + n * LINKS + p["before"][2]

                        def rotate(t):
                            dve.wait_ge(q["sq_ready"], BASE + n * NT + t + 1)
                            ch.link(dve.tensor_reduce(n2[:, :], sq[:, :].rearrange("p (h e) -> p h e", e=DH), AX, ALU.add))
                            dve.sem_inc(q["n2_done"], 1)
                            ch.link(dve.tensor_scalar(n2[:, :], n2[:, :], 1e-24, None, ALU.max))
                            rsqrt(dve, ch, inv[:, :], n2[:, :], half[:, :], tmp[:, :])
                            dve.wait_ge(q["s_fill"], BASE + n * NT + (t - 1))
                            for k in range(2):
                                x = raw[:, t % 2, 2 * k:2 * k + 2, :].rearrange("p c (h e) -> p (c h) e", e=DH)
                                y = rc[:, t % 2, k * INNER:(k + 1) * INNER].rearrange("p (h e) -> p h e", e=DH)
                                ins = dve.tensor_tensor(y, x, tab[:, k, t:t + 1, :].broadcast_to([P, NHEAD, DH]), ALU.mult)
                            ch.link(ins)
                            dve.wait_ge(q["rs_ready"], BASE + n * NT + t + 1)
                            ch.link(dve.tensor_tensor(rc[:, t % 2, :], rc[:, t % 2, :], sq[:, :], ALU.add))
                            y = rc[:, t % 2, :].rearrange("p (h e) -> p h e", e=DH)
                            ch.link(dve.tensor_tensor(y, y, inv[:, :].unsqueeze(2).broadcast_to([P, 2 * NHEAD, DH]), ALU.mult))
                            dve.sem_inc(q["rc_ready"], 1)

                        def softmax(t, m):
                            tile = m * NT + t
                            dve.wait_ge(q["s_fill"], BASE + tile + 1)
                            x = S[:, :, :].rearrange("p z (c e) -> p z c e", e=DH)
                            top = mx[:, :].rearrange("p (c z) -> p z c", z=2)
                            ch.link(dve.tensor_reduce(top, x, AX, ALU.max))
                            dve.wait_ge(q["o_fill"], BASE + tile - 1)
                            for z in range(2):
                                ins = dve.tensor_tensor(pr[:, t % 2, :, z, :], x[:, z, :, :],
                                                        top[:, z, :].unsqueeze(2).broadcast_to([P, NCH, DH]), ALU.subtract)
                            ch.link(ins)
                            dve.sem_inc(q["s_read"], 1)
                            dve.wait_ge(q["p_exp"], BASE + tile + 1)
                            dve.wait_ge(q["p_ready"], BASE + tile)
                            ch.link(dve.tensor_reduce(ssum[:, :], pr[:, t % 2, :, :, :].rearrange("p c z e -> p (c z) e"),
                                                      AX, ALU.add))
                            ch.link(dve.reciprocal(ssum[:, :], ssum[:, :]))
                            dve.sem_inc(q["p_sum"], 1)

                        def add_attention():
                            bank, read = filled_qa(dve, p, n, ("Wo",))
                            dve.tensor_tensor(xn[:, b - 1, :], xn[:, b - 1, :], bank, ALU.add).then_inc(read, 1)
                            is_read(dve, p, n, "qa", ("Wo",))
                            dve.sem_inc(q["x1_ready"], 1)

                        def normalise():
                            bank, read = filled_tr(dve, p, n, ("tok", 0, 0))
                            for t in range(NT):
                                ch.tick(dve.bn_stats(stats[:, t, :], bank[:, t * P:(t + 1) * P]))
                            ch.wait()
                            dve.memset(tmp[:, :], 0.0)
                            for t in range(NT):
                                ch.tick(dve.bn_aggr(mv[:, t, :], stats[:, t, :]))
                            ch.wait()
                            ch.link(dve.tensor_scalar(mv[:, :, 1], mv[:, :, 1], EPS, None, ALU.add))
                            rsqrt(dve, ch, inv[:, 0:NT], mv[:, :, 1], half[:, 0:NT], tmp[:, 0:NT])
                            dve.wait_ge(q["x2_ready"], BASE + n - 1)
                            for t in range(NT):
                                ins = dve.tensor_scalar(xh[:, t, :], bank[:, t * P:(t + 1) * P], mv[:, t, 0:1],
                                                        inv[:, t:t + 1], ALU.subtract, ALU.mult)
                            ins.then_inc(read, 1)
                            is_read(dve, p, n, "tr", ("tok", 0, 0))
                            dve.sem_inc(q["xh_ready"], 1)

                        def feed_forward():
                            for c, (_, m) in enumerate(FCH):
                                bank, read = filled_qa(dve, p, n, ("W1", c, 1))
                                dve.wait_ge(q["g_ready"], BASE + (n - 1) * len(FCH) + c + 1)
                                if c >= 2:
                                    dve.wait_ge(q["h_used"], BASE + (n - 1) * (len(FCH) - 1) + c - 1)
                                dve.scalar_tensor_tensor(out=hh[0:m, c % 2, :], in0=bank[0:m, :], scalar=par[0:m, 3 + c:4 + c],
                                                         in1=gg[0:m, :], op0=ALU.add, op1=ALU.mult).then_inc(read, 1)
                                is_read(dve, p, n, "qa", ("W1", c, 1))
                                dve.sem_inc(q["h_ready"], 1)
                            bank, read = filled_qa(dve, p, n, ("W2",))
                            dve.scalar_tensor_tensor(out=xn[:, b - 1, :], in0=bank, scalar=par[:, 2:3], in1=xn[:, b - 1, :],
                                                     op0=ALU.add, op1=ALU.add).then_inc(read, 1)
                            is_read(dve, p, n, "qa", ("W2",))
                            dve.sem_inc(q["ff_done"], 1)

                        for step, ff in p["steps"]:
                            ff = {k for k, _, _ in ff}
                            if "tok" in ff:
                                normalise()
                            for kind, t, _ in step:
                                if kind == "X":
                                    rotate(t)
                            if "Wo" in ff:
                                add_attention()
                            for kind, t, back in step:
                                if kind == "Y":
                                    softmax(t, n - back)
                            if "W" in ff:
                                feed_forward()
                        ch.end()

                    batches(dve, body, l)
                dve.wait_ge(q["back"], BASE + 16)
                for b in range(NB):
                    dve.tensor_tensor(acc[:, b, :], acc[:, b, :], xn[:, b, :], ALU.add)


BH, BD, HOR = 16, 16, 64
HS = P // BH
NG = BH // 4
NQ = HOR // 4
GR = 4
PITCH = HOR + P
DAMAGE = 10.0


def attn_stage(nc, g, d, skew):
    acc, xn, ident = g["acc"], g["xn"], g["ident"]
    with ExitStack() as ctx:
        s = Stage(nc, ctx, "at")
        w_disp = s.sb("w_disp", [P, 2 * P])
        w_val = s.sb("w_val", [P, P])
        w_proj = s.sb("w_proj", [P, P])
        w_fused = s.sb("w_fused", [P, P])
        w_red = s.sb("w_red", [P, NG, 32])
        w_pos = s.sb("w_pos", [BD, P])
        rel = s.sb("rel", [BD, HOR])
        bias = s.sb("bias", [P, 2])
        mask = s.sb("mask", [P, HOR])
        pos = s.sb("pos", [P, HOR])
        xp = s.sb("xp", [P, HOR + L + 1])
        disp = s.sb("disp", [P, 2, L])
        fp = s.sb("fp", [P, NG, HOR + L])
        df = s.sb("df", [P, 2, NG, L])
        ge = s.sb("ge", [P, GR, NG, L])
        lt = s.sb("lt", [P, 2, L])
        th = s.sb("th", [P, NT, 4, BH])
        lg = s.sb("lg", [P, NT, BH, HOR])
        mx = s.sb("mx", [P, NT, BH])
        rsum = s.sb("rsum", [P, NT, BH])
        va = s.sb("va", [P, NT, 4, 4, 32])
        vb = s.sb("vb", [HOR, NT, 4, 4, 32])
        band = s.sb("band", [P, 2, BH, PITCH])
        ba = s.sb("ba", [P, BH, P])
        bb = s.sb("bb", [HOR, BH, P])
        oT = s.sb("oT", [P, L])
        zero = s.sb("zero", [P, 1544])
        LT = s.banks("LT", 2)
        TK = s.banks("TK", 2)
        TB = s.banks("TB", 2)
        O = s.banks("O", 1)
        X = s.banks("X", 1)
        q = s.sems("loaded zeroed cleared pos_fill pos_ready dbias xp_ready tb_fill tb_read0 tb_read1 disp_ready f_ready "
                   "d_ready g_ready red_done lt_ready tk_fill th_ready lg_part sub_done exp_done sum_done norm_done band_free pv_ready "
                   "pv_done ot_ready pr_fill acc_done dch held wr0 wr1 wr2 wr3 rd0 rd1 rd2 rd3 v_ready")
        tb_read = [q["tb_read0"], q["tb_read1"]]
        wr, rd = ([q[f"{n}{t}"] for t in range(NT)] for n in ("wr", "rd"))
        tb = [("disp", k) for k in range(2)] + [("F", k) for k in range(NG)] + [("V", k) for k in range(2)]
        tb += [(k, t, j) for t in range(NT) for j in range(4) for k in ("A", "B")]
        TN = len(tb)
        tb = {key: n for n, key in enumerate(tb)}

        def fill(pe, b, key):
            k = tb[key]
            pe.wait_ge(tb_read[k % 2], BASE + b * (TN // 2) + k // 2)
            if key[0] == "B":
                settle(pe, q["held"])
            return TB[:, k % 2, :]

        def filled(eng, b, key):
            k = tb[key]
            eng.wait_ge(q["tb_fill"], BASE + b * TN + k + 1)
            return TB[:, k % 2, :], tb_read[k % 2]

        def read(eng, b, keys):
            for key in keys:
                eng.wait_ge(tb_read[tb[key] % 2], BASE + b * (TN // 2) + tb[key] // 2 + 1)

        loads = ((w_disp, "a_w_disp"), (w_val, "a_w_val"), (w_proj, "a_w_proj"), (w_fused, "a_w_fused"),
                 (w_red, "a_w_red"), (w_pos, "a_w_pos"), (rel, "a_rel"), (bias, "a_bias"), (mask, "a_mask"))
        flat = skew.rearrange("t h (a n) -> (t h a) n", n=1544)
        with nc.Block() as block:
            @block.sync
            def _(sp):
                for dst, src in loads:
                    sp.dma_start(dst[:], d[src]).then_inc(q["loaded"], 16)
                sp.wait_ge(q["zeroed"], BASE + 1)
                for k in range(flat.shape[0] // P):
                    sp.dma_start(flat[k * P:(k + 1) * P, :], zero[:, :]).then_inc(q["cleared"], 16)
                sp.wait_ge(q["cleared"], BASE + 16 * (flat.shape[0] // P))
                with sp.Fori(0, NB) as b:
                    for t in range(NT):
                        sp.wait_ge(rd[t], BASE + b * 16)
                        settle(sp, q["held"])
                        sp.wait_ge(q["norm_done"], BASE + b * NT + t + 1)
                        settle(sp, q["held"])
                        sp.dma_start(skew[t].rearrange("h (t c) -> t h c", c=PITCH + 1)[:, :, 0:HOR],
                                     lg[:, t, :, :]).then_inc(wr[t], 16)
                        sp.wait_ge(wr[t], BASE + (b + 1) * 16)
                        settle(sp, q["held"])
                        sp.wait_ge(q["band_free"], BASE + b * NT + t - 1)
                        sp.dma_start(band[:, t % 2, :, :],
                                     skew[t][:, 0:P * PITCH].rearrange("h (t c) -> t h c", c=PITCH)).then_inc(rd[t], 16)

            @block.gpsimd
            def _(pool):
                pool.memset(xp[:, :], 0.0)
                pool.memset(va[:], 0.0)
                pool.memset(vb[:], 0.0)
                pool.memset(fp[:, :, 0:HOR], 0.0)
                pool.memset(zero[:, :], 0.0).then_inc(q["zeroed"], 1)
                pool.wait_ge(q["loaded"], BASE + 16 * len(loads))
                pool.tensor_scalar(bias[:, 1:2], bias[:, 1:2], 0.5, None, ALU.mult).then_inc(q["dbias"], 1)
                with pool.Fori(0, NB) as b:
                    for t in range(NT):
                        pool.wait_ge(q["sum_done"], BASE + b * NT + t + 1)
                        pool.tensor_tensor(lg[:, t, :, :], lg[:, t, :, :],
                                           rsum[:, t, :].unsqueeze(2).broadcast_to([P, BH, HOR]), ALU.mult).then_inc(q["norm_done"], 1)

            @block.scalar
            def _(act):
                act.wait_ge(q["pos_fill"], BASE + 1)
                act.activation(pos[:, :], X[:, 0, 0:HOR], ACT.Identity, bias=bias[:, 0:1]).then_inc(q["pos_ready"], 1)
                act.wait_ge(q["pos_ready"], BASE + 1)
                act.wait_ge(q["dbias"], BASE + 1)
                act.wait_ge(q["zeroed"], BASE + 1)
                with act.Fori(0, NB) as b:
                    act.wait_ge(q["acc_done"], BASE + b)
                    settle(act, q["held"])
                    act.activation(xp[:, HOR:HOR + L], xn[:, b, :], ACT.Copy).then_inc(q["xp_ready"], 1)
                    for k in range(2):
                        bank, r = filled(act, b, ("disp", k))
                        act.activation(disp[:, k, :], bank, ACT.Copy).then_inc(r, 1)
                    read(act, b, [("disp", 0), ("disp", 1)])
                    act.sem_inc(q["disp_ready"], 1)
                    for k in range(NG):
                        bank, r = filled(act, b, ("F", k))
                        act.activation(fp[:, k, HOR:], bank, ACT.Copy).then_inc(r, 1)
                    read(act, b, [("F", NG - 2), ("F", NG - 1)])
                    act.sem_inc(q["f_ready"], 1)
                    for k, dst in enumerate((va, vb)):
                        bank, r = filled(act, b, ("V", k))
                        for m in range(4):
                            ins = act.activation(dst[:, :, :, m, HS * m:HS * (m + 1)],
                                                 bank[0:dst.shape[0], :].rearrange("p (t h m e) -> p t h m e", t=NT, m=4, e=HS)[:, :, :, m, :],
                                                 ACT.Copy)
                        ins.then_inc(r, 1)
                    read(act, b, [("V", 0), ("V", 1)])
                    act.sem_inc(q["v_ready"], 1)

                    def keep(c):
                        act.wait_ge(q["red_done"], BASE + b * (HOR // 2) + 2 * (c + 1))
                        act.wait_ge(q["tk_fill"], BASE + b * NQ + c - 1)
                        act.activation(lt[:, c % 2, :], LT[:, c % 2, :], ACT.Copy).then_inc(q["lt_ready"], 1)

                    def damage(c):
                        act.wait_ge(q["tk_fill"], BASE + b * NQ + c + 1)
                        act.wait_ge(q["lg_part"], BASE + b * NQ + c)
                        act.activation(th[:].rearrange("p t w (g h) -> p (t w g) h", h=4),
                                       TK[:, c % 2, :].rearrange("p (n y h) -> p n y h", y=2, h=4)[:, :, 1, :],
                                       ACT.Tanh, scale=0.5, bias=bias[:, 1:2]).then_inc(q["th_ready"], 1)

                    for w in range(HOR):
                        act.wait_ge(q["d_ready"], BASE + b * HOR + w + 1)
                        act.wait_ge(q["red_done"], BASE + b * (HOR // 2) + w // 2 - 1)
                        act.activation(ge[:, w % GR, :, :], df[:, w % 2, :, :], ACT.Gelu,
                                       bias=pos[:, w:w + 1]).then_inc(q["g_ready"], 1)
                        if w >= 4 and w % 4 == 1:
                            keep(w // 4 - 1)
                        if w >= 4 and w % 4 == 3:
                            damage(w // 4 - 1)
                    keep(NQ - 1)
                    damage(NQ - 1)
                    for t in range(NT):
                        act.wait_ge(q["sub_done"], BASE + b * NT + t + 1)
                        act.activation(lg[:, t, :, :], lg[:, t, :, :], ACT.Exp).then_inc(q["exp_done"], 1)
                    for t in range(NT):
                        act.wait_ge(q["pv_done"], BASE + b * NT + t)
                        for j in range(4):
                            for k, dst in (("A", ba), ("B", bb)):
                                bank, r = filled(act, b, (k, t, j))
                                act.activation(dst[:, 4 * j:4 * j + 4, :],
                                               bank[0:dst.shape[0], :].rearrange("p (h x) -> p h x", x=P), ACT.Copy).then_inc(r, 1)
                        read(act, b, [("A", t, 3), ("B", t, 3)])
                        act.sem_inc(q["pv_ready"], 1)
                    act.wait_ge(q["pv_done"], BASE + (b + 1) * NT)
                    act.activation(oT[:, :], O[:, 0, :], ACT.Copy).then_inc(q["ot_ready"], 1)

            @block.tensor
            def _(pe):
                pe.wait_ge(q["loaded"], BASE + 16 * len(loads))
                pe.matmul(X[:, 0, 0:HOR], w_pos[:, :], rel[:, :], start=True, stop=True).then_inc(q["pos_fill"], 1)
                with pe.Fori(0, NB) as b:
                    pe.wait_ge(q["xp_ready"], BASE + b + 1)
                    for k in range(2):
                        bank = fill(pe, b, ("disp", k))
                        pe.matmul(bank, w_disp[:, k * P:(k + 1) * P], xp[:, HOR:HOR + L], start=True,
                                  stop=True).then_inc(q["tb_fill"], 1)
                    pe.wait_ge(q["disp_ready"], BASE + b + 1)
                    for k in range(NG):
                        bank = fill(pe, b, ("F", k))
                        rows = slice(64 * (k % 2), 64 * (k % 2) + 64)
                        pe.matmul(bank, w_fused[rows, :], disp[rows, k // 2, :], start=True,
                                  stop=True).then_inc(q["tb_fill"], 1)
                    for k, m in enumerate((P, HOR)):
                        bank = fill(pe, b, ("V", k))
                        for t in range(NT):
                            c0 = t * P + 1 + k * P
                            mm = pe.matmul(bank[0:m, t * P:(t + 1) * P], xp[:, c0:c0 + m], w_val[:, :], start=True, stop=True)
                        mm.then_inc(q["tb_fill"], 1)
                    def turn(c):
                        pe.wait_ge(q["lt_ready"], BASE + b * NQ + c + 1)
                        pe.wait_ge(q["lg_part"], BASE + b * NQ + c - 1)
                        for t in range(NT):
                            mm = pe.transpose(TK[:, c % 2, t * P:(t + 1) * P], lt[:, c % 2, t * P:(t + 1) * P], ident[:, :])
                        mm.then_inc(q["tk_fill"], 1)

                    for w in range(0, HOR, 2):
                        c = w // 4
                        pe.wait_ge(q["lt_ready"], BASE + b * NQ + c - 1)
                        pe.wait_ge(q["g_ready"], BASE + b * HOR + w + 2)
                        for k in range(NG):
                            for i in (w, w + 1):
                                r0 = 32 * (i % 4)
                                mm = pe.matmul(LT[r0:r0 + 32, c % 2, :], w_red[:, k, :], ge[:, i % GR, k, :],
                                               start=(k == 0), stop=(k == NG - 1), skip_group_check=True)
                        mm.then_inc(q["red_done"], 1)
                        if w >= 4 and w % 4 == 2:
                            turn(c - 1)
                    turn(NQ - 1)
                    pe.wait_ge(q["v_ready"], BASE + b + 1)
                    settle(pe, q["held"])
                    for t in range(NT):
                        pe.wait_ge(rd[t], BASE + (b + 1) * 16)
                        for j in range(4):
                            for k, m in (("A", P), ("B", HOR)):
                                bank = fill(pe, b, (k, t, j))
                                c0 = 0 if k == "A" else P
                                for i in range(4):
                                    mm = pe.transpose(bank[0:m, i * P:(i + 1) * P], band[:, t % 2, 4 * j + i, c0:c0 + m], ident[:, :])
                                mm.then_inc(q["tb_fill"], 1)
                        pe.wait_ge(q["tb_fill"], BASE + b * TN + tb[("B", t, 3)] + 1)
                        pe.sem_inc(q["band_free"], 1)
                        pe.wait_ge(q["pv_ready"], BASE + b * NT + t + 1)
                        for m in range(4):
                            for k, (val, bnd) in enumerate(((va, ba), (vb, bb))):
                                for h in range(4):
                                    mm = pe.matmul(O[32 * h:32 * h + 32, 0, t * P:(t + 1) * P], val[:, t, h, m, :],
                                                   bnd[:, 4 * h + m, :], start=(m == 0 and k == 0),
                                                   stop=(m == 3 and k == 1), skip_group_check=True)
                        mm.then_inc(q["pv_done"], 1)
                    pe.wait_ge(q["ot_ready"], BASE + b + 1)
                    pe.matmul(X[:, 0, :], w_proj[:, :], oT[:, :], start=True, stop=True).then_inc(q["pr_fill"], 1)

            @block.vector
            def _(dve):
                ch = Chain(dve, q["dch"], 1 + 4 * NT)
                dve.wait_ge(q["loaded"], BASE + 16 * len(loads))
                with dve.Fori(0, NB) as b:
                    ch.start(b)

                    def logits(c):
                        dve.wait_ge(q["th_ready"], BASE + b * NQ + c + 1)
                        dve.wait_ge(rd[NT - 1], BASE + b * 16)
                        for t in range(NT):
                            ins = dve.scalar_tensor_tensor(
                                out=lg[:, t, :, 4 * c:4 * c + 4].rearrange("p (g h) w -> p w g h", h=4),
                                in0=th[:, t, :, :].rearrange("p w (g h) -> p w g h", h=4), scalar=-DAMAGE / 2,
                                in1=TK[:, c % 2, t * P:(t + 1) * P].rearrange("p (w g y h) -> p w g y h", w=4, y=2, h=4)[:, :, :, 0, :],
                                op0=ALU.mult, op1=ALU.add)
                        ins.then_inc(q["lg_part"], 1)

                    dve.wait_ge(q["f_ready"], BASE + b + 1)
                    for w in range(HOR):
                        dve.wait_ge(q["g_ready"], BASE + b * HOR + w - 1)
                        dve.tensor_tensor(df[:, w % 2, :, :], fp[:, :, w + 1:w + 1 + L], fp[:, :, HOR:],
                                          ALU.subtract).then_inc(q["d_ready"], 1)
                        if w >= 8 and w % 4 == 1:
                            logits(w // 4 - 2)
                    logits(NQ - 2)
                    logits(NQ - 1)
                    dve.wait_ge(q["lg_part"], BASE + (b + 1) * NQ)
                    ch.link(dve.tensor_tensor(lg[:, 0, :, :], lg[:, 0, :, :],
                                              mask[:, :].unsqueeze(1).broadcast_to([P, BH, HOR]), ALU.add))
                    for t in range(NT):
                        ch.link(dve.tensor_reduce(mx[:, t, :], lg[:, t, :, :], AX, ALU.max))
                        ch.link(dve.tensor_tensor(lg[:, t, :, :], lg[:, t, :, :],
                                                  mx[:, t, :].unsqueeze(2).broadcast_to([P, BH, HOR]), ALU.subtract))
                        dve.sem_inc(q["sub_done"], 1)
                    for t in range(NT):
                        dve.wait_ge(q["exp_done"], BASE + b * NT + t + 1)
                        ch.link(dve.tensor_reduce(rsum[:, t, :], lg[:, t, :, :], AX, ALU.add))
                        ch.link(dve.reciprocal(rsum[:, t, :], rsum[:, t, :]))
                        dve.sem_inc(q["sum_done"], 1)
                    dve.wait_ge(q["pr_fill"], BASE + b + 1)
                    dve.tensor_tensor(acc[:, b, :], acc[:, b, :], X[:, 0, :], ALU.add).then_inc(q["acc_done"], 1)
                    ch.end()


NE, NI, NTOP, GROUPS, GTOP = 64, 64, 6, 8, 4
NCK = NE * NI // P
LOW, TAKEN = -1e30, 3e30


def moe_stage(nc, g, d, out):
    acc, xn, ident = g["acc"], g["xn"], g["ident"]
    with ExitStack() as ctx:
        s = Stage(nc, ctx, "mo")
        w_g = s.sb("w_g", [P, NCK + 1, P])
        w_u = s.sb("w_u", [P, NCK + 1, P])
        w_d = s.sb("w_d", [P, NCK + 1, P])
        w_r = s.sb("w_r", [P, NE])
        gb = s.sb("gb", [P, NE])
        comb_t = s.sb("comb_t", [NE, NB, L])
        pick = s.sb("pick", [NE, NE, NI])
        xc = s.sb("xc", [P, L])
        sc = s.sb("sc", [P, NT, NE])
        gv = s.sb("gv", [P, NT, 2 * GROUPS])
        ev = s.sb("ev", [P, NT, NE + 8])
        gsel = s.sb("gsel", [P, NT, 2 * GROUPS])
        esel = s.sb("esel", [P, NT, NE + 8])
        top = s.sb("top", [P, NT, 8])
        comb = s.sb("comb", [P, NT, NE])
        wsum = s.sb("wsum", [P, NT])
        sg = s.sb("sg", [P, 2, L])
        h1 = s.sb("h1", [P, L])
        h2 = s.sb("h2", [P, 2, L])
        G = s.banks("G", 2)
        U = s.banks("U", 2)
        C = s.banks("C", 2)
        R = s.banks("R", 1)
        X = s.banks("X", 1)
        q = s.sems("loaded w_in x_ready lo_fill sc_ready lows comb_ready ct_fill ct_ready xc_ready g_fill uc_fill sg_ready "
                   "h1_ready h_ready d_done r_done saved stored dch held rch")
        with nc.Block() as block:
            @block.sync
            def _(sp):
                for dst, src in ((w_r, "e_w_r"), (gb, "e_gb")):
                    sp.dma_start(dst[:], d[src]).then_inc(q["loaded"], 16)
                for dst, src in ((w_g, "e_w_g"), (w_u, "e_w_u"), (w_d, "e_w_d")):
                    sp.dma_start(dst[:], d[src]).then_inc(q["w_in"], 16)
                with sp.Fori(0, NB) as b:
                    sp.wait_ge(q["saved"], BASE + b + 1)
                    settle(sp, q["held"])
                    sp.dma_start(out[:, b, :], acc[:, b, :]).then_inc(q["stored"], 16)
                sp.wait_ge(q["stored"], BASE + 16 * NB)

            @block.gpsimd
            def _(pool):
                pool.tensor_copy(pick[:], ident[0:NE, 0:NE].unsqueeze(2).broadcast_to([NE, NE, NI]))
                pool.memset(gv[:], LOW)
                pool.memset(ev[:], LOW).then_inc(q["lows"], 1)

            @block.scalar
            def _(act):
                with act.Fori(0, NB) as b:
                    act.wait_ge(q["lo_fill"], BASE + b)
                    settle(act, q["held"])
                    act.activation(xc[:, :], xn[:, b, :], ACT.Copy).then_inc(q["x_ready"], 1)
                    act.wait_ge(q["lo_fill"], BASE + b + 1)
                    act.activation(sc[:], X[:, 0, 0:NT * NE].rearrange("p (t e) -> p t e", e=NE),
                                   ACT.Sigmoid).then_inc(q["sc_ready"], 1)
                    act.wait_ge(q["ct_fill"], BASE + b + 1)
                    settle(act, q["held"])
                    act.activation(comb_t[:, b, :], X[0:NE, 0, :], ACT.Copy).then_inc(q["ct_ready"], 1)
                with act.Fori(0, NB) as b:
                    for c in range(NCK + 1):
                        n = b * (NCK + 1) + c
                        act.wait_ge(q["g_fill"], BASE + n + 1)
                        act.wait_ge(q["h1_ready"], BASE + n - 1)
                        act.activation(sg[:, c % 2, :], G[:, c % 2, :], ACT.Silu).then_inc(q["sg_ready"], 1)
                    act.wait_ge(q["h1_ready"], BASE + (b + 1) * (NCK + 1))

            @block.tensor
            def _(pe):
                pe.wait_ge(q["loaded"], BASE + 32)
                with pe.Fori(0, NB) as b:
                    pe.wait_ge(q["x_ready"], BASE + b + 1)
                    pe.wait_ge(q["ct_ready"], BASE + b)
                    for t in range(NT):
                        mm = pe.matmul(X[:, 0, t * NE:(t + 1) * NE], xc[:, t * P:(t + 1) * P], w_r[:, :], start=True, stop=True)
                    mm.then_inc(q["lo_fill"], 1)
                    pe.wait_ge(q["comb_ready"], BASE + b + 1)
                    settle(pe, q["held"])
                    for t in range(NT):
                        mm = pe.transpose(X[0:NE, 0, t * P:(t + 1) * P], comb[:, t, :], ident[:, :])
                    mm.then_inc(q["ct_fill"], 1)
                pe.wait_ge(q["ct_ready"], BASE + NB)
                pe.wait_ge(q["w_in"], BASE + 48)
                pe.wait_ge(q["lows"], BASE + 1)
                with pe.Fori(0, NB) as b:
                    def up(c):
                        n = b * (NCK + 1) + c
                        pe.wait_ge(q["sg_ready"], BASE + n - 1)
                        pe.matmul(G[:, c % 2, :], w_g[:, c, :], xn[:, b, :], start=True, stop=True).then_inc(q["g_fill"], 1)
                        pe.wait_ge(q["h_ready"], BASE + n - 1)
                        mm = pe.matmul(U[:, c % 2, :], w_u[:, c, :], xn[:, b, :], start=True, stop=True)
                        if c < NCK:
                            mm = pe.matmul(C[:, c % 2, :], pick[:, 2 * c:2 * c + 2, :].rearrange("k e i -> k (e i)"),
                                           comb_t[:, b, :], start=True, stop=True)
                        mm.then_inc(q["uc_fill"], 1)

                    def down(c):
                        n = b * (NCK + 1) + c
                        pe.wait_ge(q["h_ready"], BASE + n + 1)
                        if c == 0:
                            pe.wait_ge(q["saved"], BASE + b)
                        pe.matmul(R[:, 0, :], w_d[:, c, :], h2[:, c % 2, :], start=(c == 0),
                                  stop=(c == NCK)).then_inc(q["d_done"], 1)

                    pe.wait_ge(q["h_ready"], BASE + b * (NCK + 1))
                    settle(pe, q["held"])
                    for c in range(NCK + 1):
                        up(c)
                        if c >= 1:
                            down(c - 1)
                    down(NCK)

            @block.vector
            def _(dve):
                ch = Chain(dve, q["rch"], 12)
                dve.wait_ge(q["loaded"], BASE + 32)
                dve.wait_ge(q["lows"], BASE + 1)
                with dve.Fori(0, NB) as b:
                    ch.start(b)
                    dve.wait_ge(q["sc_ready"], BASE + b + 1)
                    ch.link(dve.tensor_tensor(sc[:], sc[:], gb[:, :].unsqueeze(1).broadcast_to([P, NT, NE]), ALU.add))
                    ch.link(dve.tensor_reduce(gv[:, :, 0:GROUPS], sc[:].rearrange("p t (g e) -> p t g e", g=GROUPS), AX, ALU.max))

                    def taken(values, sel, n):
                        settle(dve, q["held"])
                        for t in range(NT):
                            ins = dve.max(top[:, t, :], values[:, t, :])
                        ch.link(ins)
                        ch.link(dve.memset(top[:, :, n:8], LOW))
                        settle(dve, q["held"])
                        for t in range(NT):
                            ins = dve.match_replace(sel[:, t, :], top[:, t, :], values[:, t, :], TAKEN)
                        ch.link(ins)

                    taken(gv, gsel, GTOP)
                    ch.link(dve.tensor_scalar(gsel[:], gsel[:], -LOW, None, ALU.is_ge))
                    for t in range(NT):
                        ins = dve.tensor_tensor(ev[:, t, 0:NE].rearrange("p (g e) -> p g e", g=GROUPS),
                                                sc[:, t, :].rearrange("p (g e) -> p g e", g=GROUPS),
                                                gsel[:, t, 0:GROUPS].unsqueeze(2).broadcast_to([P, GROUPS, NE // GROUPS]), ALU.mult)
                    ch.link(ins)
                    taken(ev, esel, NTOP)
                    ins = dve.scalar_tensor_tensor(out=comb[:], in0=esel[:, :, 0:NE], scalar=-LOW, in1=ev[:, :, 0:NE],
                                                   op0=ALU.is_ge, op1=ALU.mult)
                    ch.link(ins)
                    dve.tensor_reduce(wsum[:, :], comb[:], AX, ALU.add).then_inc(q["dch"], 1)
                    dve.wait_ge(q["dch"], BASE + 3 * b + 1)
                    dve.tensor_scalar(wsum[:, :], wsum[:, :], 1e-8, None, ALU.add).then_inc(q["dch"], 1)
                    dve.wait_ge(q["dch"], BASE + 3 * b + 2)
                    dve.reciprocal(wsum[:, :], wsum[:, :]).then_inc(q["dch"], 1)
                    dve.wait_ge(q["dch"], BASE + 3 * b + 3)
                    ch.link(dve.tensor_tensor(comb[:], comb[:], wsum[:, :].unsqueeze(2).broadcast_to([P, NT, NE]), ALU.mult))
                    dve.sem_inc(q["comb_ready"], 1)
                    dve.wait_ge(q["ct_fill"], BASE + b + 1)
                    ch.end()
                with dve.Fori(0, NB) as b:
                    for c in range(NCK + 1):
                        n = b * (NCK + 1) + c
                        dve.wait_ge(q["sg_ready"], BASE + n + 1)
                        dve.wait_ge(q["uc_fill"], BASE + n + 1)
                        dve.wait_ge(q["d_done"], BASE + n - 1)
                        if c < NCK:
                            dve.tensor_tensor(h1[:, :], sg[:, c % 2, :], U[:, c % 2, :], ALU.mult).then_inc(q["h1_ready"], 1)
                            dve.wait_ge(q["h1_ready"], BASE + n + 1)
                            dve.tensor_tensor(h2[:, c % 2, :], h1[:, :], C[:, c % 2, :], ALU.mult).then_inc(q["h_ready"], 1)
                            dve.wait_ge(q["h_ready"], BASE + n + 1)
                        else:
                            dve.tensor_tensor(h2[:, c % 2, :], sg[:, c % 2, :], U[:, c % 2, :], ALU.mult).then_inc(q["h1_ready"], 1)
                            dve.wait_ge(q["h1_ready"], BASE + n + 1)
                            dve.sem_inc(q["h_ready"], 1)
                    dve.wait_ge(q["d_done"], BASE + (b + 1) * (NCK + 1))
                    settle(dve, q["held"])
                    dve.tensor_tensor(acc[:, b, :], acc[:, b, :], R[:, 0, :], ALU.add).then_inc(q["saved"], 1)


def rotary_tables():
    f = np.float32
    half = np.arange(0, DH, 2, dtype=f)
    freqs = np.arange(L, dtype=f)[:, None] * (f(1) / f(10000) ** (half / f(DH)))[None, :]
    power = (np.arange(L, dtype=f) - f(L // 2)) / f(WIN // 2)
    scale = ((half + f(0.4 * DH)) / f(1.4 * DH))[None, :] ** power[:, None]
    cos, sin = np.cos(freqs), np.sin(freqs)
    pair = lambda lo, hi: np.concatenate([lo, hi], axis=1)
    k = f(1) / scale
    t = np.stack([pair(cos * scale, cos * scale), pair(cos * k, cos * k),
                  pair(-sin * scale, sin * scale), pair(-sin * k, sin * k)])
    return np.ascontiguousarray(t.reshape(4, NT, P, DH).transpose(2, 0, 1, 3).astype(f))


def window_masks():
    a, key = (np.arange(P) % WIN)[:, None], np.arange(2 * WIN)[None, :]
    seen = (key >= a) & (key <= a + WIN)
    first = seen & ~((np.arange(P)[:, None] < WIN) & (key < WIN))
    return np.ascontiguousarray(np.where(np.stack([first, seen], axis=1), 0.0, -1e30).astype(np.float32))


def program(nc, d, out):
    with ExitStack() as ctx:
        g = {}
        g["acc"] = ctx.enter_context(nc.sbuf_tensor("acc", [P, NB, L], F32))
        g["xn"] = ctx.enter_context(nc.sbuf_tensor("xn", [P, NB, L], F32))
        g["ident"] = ctx.enter_context(nc.sbuf_tensor("ident", [P, P], F32))
        loaded = ctx.enter_context(nc.semaphore("x_loaded"))
        saved = ctx.enter_context(nc.semaphore("out_saved"))
        with nc.Block() as block:
            @block.sync
            def _(sp):
                sp.dma_start(g["ident"][:, :], d["ident"]).then_inc(loaded, 16)
                sp.dma_start(g["acc"][:, :, :], d["x"]).then_inc(loaded, 16)
                sp.wait_ge(loaded, 32)
        n = 0
        for phase in PHASES:
            if phase == "norm":
                layernorm_stage(nc, g, f"ln{n}")
                n += 1
            if phase == "mamba":
                mamba_stage(nc, g, d)
            if phase == "ffn":
                ffn_stage(nc, g, d, nc.dram_tensor("park", (P, NB, L), F32).ap())
            if phase == "attn":
                attn_stage(nc, g, d, nc.dram_tensor("skew", (NT, BH, P * (PITCH + 1)), F32).ap())
            if phase == "moe":
                moe_stage(nc, g, d, out)
        if PHASES[-1] == "moe":
            return
        src = g["acc"] if PHASES[-1] != "norm" else g["xn"]
        with nc.Block() as block:
            @block.sync
            def _(sp):
                sp.dma_start(out, src[:, :, :]).then_inc(saved, 16)
                sp.wait_ge(saved, 16)


def layouts(i):
    T = np.ascontiguousarray
    a = {}
    a["ident"] = np.eye(P, dtype=np.float32)
    a["x"] = T(i["L0_attn_x"].reshape(NB, L, P).transpose(2, 0, 1))
    halves = lambda w: T(w.reshape(2, P, -1).transpose(1, 0, 2))
    a["m_w_in"] = T(i["L0_attn_W_in"].T)
    a["m_w_x"] = halves(T(i["L0_attn_W_x"].T))
    a["m_w_dt"] = T(i["L0_attn_W_dt"].T)
    a["m_w_out"] = halves(T(i["L0_attn_W_out"].T))
    a["m_par"] = halves(np.concatenate([i["L0_attn_conv_w"], i["L0_attn_conv_b"][:, None],
                                        i["L0_attn_b_dt"][:, None], i["L0_attn_D"][:, None]], axis=1))
    a["m_alog"] = halves(i["L0_attn_A_log"])
    a["f_w_qkv"] = i["L0_ffn_Wqkv"].copy()
    a["f_w_qkv"][:, :, 2 * INNER:] = (i["L0_ffn_Wqkv"][:, :, 2 * INNER:].reshape(NLAYER, P, NCH, 2, DH)
                                      .transpose(0, 1, 3, 2, 4).reshape(NLAYER, P, INNER))
    a["f_w_o"] = T(i["L0_ffn_Wo"].reshape(NLAYER, NCH, P, P).transpose(0, 2, 1, 3))
    a["f_w_1"] = i["L0_ffn_W1"]
    a["f_w_2"] = np.zeros((NLAYER, P, len(FCH), P), np.float32)
    a["f_par"] = np.zeros((NLAYER, P, 3 + 2 * len(FCH)), np.float32)
    for k, name in enumerate(("ln_g", "ln_b", "b2")):
        a["f_par"][:, :, k] = i[f"L0_ffn_{name}"]
    for c, (f0, m) in enumerate(FCH):
        a["f_w_2"][:, 0:m, c, :] = i["L0_ffn_W2"][:, f0:f0 + m, :]
        a["f_par"][:, 0:m, 3 + c] = i["L0_ffn_b1"][:, f0:f0 + m]
        a["f_par"][:, 0:m, 6 + c] = i["L0_ffn_b1"][:, FF + f0:FF + f0 + m]
    qs, ks = i["L0_ffn_q_scale"], i["L0_ffn_k_scale"]
    swap = lambda w: np.concatenate([w[:, DH // 2:], w[:, :DH // 2]], axis=1)
    a["f_qk_s"] = T(np.broadcast_to(np.stack([qs, ks, swap(qs), swap(ks)], axis=1)[:, None], (NLAYER, P, 4, DH)))
    a["f_ctab"], a["f_mask"] = rotary_tables(), window_masks()
    a["a_w_disp"] = T(i["L1_attn_W_disp"].T)
    a["a_w_val"] = T(i["L1_attn_W_val"].T)
    a["a_w_proj"] = T(i["L1_attn_c_proj_w"].T)
    a["a_w_fused"] = np.zeros((2, 4, BD, 4, 2 * BD), np.float32)
    a["a_w_red"] = np.zeros((4, 2, BD, NG, NG, 2, 4), np.float32)
    a["a_w_pos"] = np.zeros((BD, 4, 2, BD), np.float32)
    for h in range(4):
        a["a_w_fused"][:, h, :, h, :] = i["L1_attn_strain_fused_w"].T
        for k in range(NG):
            a["a_w_red"][h, 0, :, k, k, 0, h] = i["L1_attn_bond_out_w"][0]
            a["a_w_red"][h, 1, :, k, k, 1, h] = i["L1_attn_damage_out_w"][0]
        a["a_w_pos"][:, h, 0, :] = i["L1_attn_pos_proj_w"].T
    a["a_w_fused"] = a["a_w_fused"].reshape(P, P)
    a["a_w_red"] = a["a_w_red"].reshape(P, NG, 32)
    a["a_w_pos"] = a["a_w_pos"].reshape(BD, P)
    a["a_rel"] = T(i["L1_attn_rel_pos_emb"].T)
    a["a_bias"] = T(np.stack([np.tile(i["L1_attn_strain_fused_b"], 4),
                              np.tile(i["L1_attn_damage_out_b"], P)], axis=1))
    t, w = np.arange(P)[:, None], np.arange(HOR)[None, :]
    a["a_mask"] = np.where(t + w >= HOR - 1, 0.0, -1e30).astype(np.float32)
    chunks = lambda w, sh: T(np.concatenate([w.reshape(NE * NI, P), sh]).reshape(NCK + 1, P, P))
    a["e_w_g"] = T(chunks(i["L1_ffn_eg_w"], i["L1_ffn_sg_w"]).transpose(2, 0, 1))
    a["e_w_u"] = T(chunks(i["L1_ffn_eu_w"], i["L1_ffn_su_w"]).transpose(2, 0, 1))
    a["e_w_d"] = T(chunks(T(i["L1_ffn_ed_w"].transpose(0, 2, 1)), i["L1_ffn_sd_w"].T).transpose(1, 0, 2))
    a["e_w_r"] = T(i["L1_ffn_gate_w"].T)
    a["e_gb"] = T(np.broadcast_to(i["L1_ffn_gate_bias"], (P, NE)))
    return a


def kernel(**inputs):
    import concourse.bacc as _bacc
    from concourse.bass_utils import run_bass_kernel_spmd as _run

    nc = _bacc.Bacc("TRN2", target_bir_lowering=False, num_devices=1)
    arrays, d = {}, {}
    for name, a in layouts({k: np.asarray(v) for k, v in inputs.items()}).items():
        arrays[f"in_{name}_dram"] = a
        d[name] = nc.dram_tensor(f"in_{name}_dram", a.shape, mybir.dt.from_np(a.dtype), kind="ExternalInput").ap()
    out = nc.dram_tensor("out_0_dram", (P, NB, L), F32, kind="ExternalOutput").ap()
    program(nc, d, out)
    r = _run(nc, [arrays], core_ids=[0])
    return np.ascontiguousarray(r.results[0]["out_0_dram"].transpose(1, 2, 0))
```

```python
from contextlib import ExitStack

import numpy as np

import concourse.bass as bass
from concourse import mybir

F32 = mybir.dt.float32
BF16 = mybir.dt.bfloat16
I32 = mybir.dt.int32
ALU = mybir.AluOpType
ACT = mybir.ActivationFunctionType
AX = mybir.AxisListType.X

P = 128
NB = 8
L = 512
NT = L // P
EPS = 1e-5
BASE = 16


class Chain:

    def __init__(self, eng, sem, per):
        self.eng, self.sem, self.per, self.n, self.base = eng, sem, per, 0, 0

    def start(self, step):
        self.n, self.base = 0, BASE + step * self.per

    def tick(self, ins):
        self.n += 1
        ins.then_inc(self.sem, 1)

    def wait(self):
        self.eng.wait_ge(self.sem, self.base + self.n)

    def link(self, ins):
        self.tick(ins)
        self.wait()

    def end(self):
        assert self.n == self.per, (self.sem, self.n)


def settle(eng, sem):
    eng.sem_inc(sem, 1)


class Stage:

    def __init__(self, nc, ctx, name):
        self.nc, self.ctx, self.name = nc, ctx, name

    def sb(self, name, shape, dt=F32):
        return self.ctx.enter_context(self.nc.sbuf_tensor(f"{self.name}_{name}", shape, dt))

    def banks(self, name, n):
        return self.ctx.enter_context(self.nc.psum_tensor(f"{self.name}_{name}", [P, n, 512], F32))

    def sems(self, names):
        q = {n: self.ctx.enter_context(self.nc.semaphore(f"{self.name}_{n}")) for n in names.split()}
        with self.nc.Block() as block:
            @block.sync
            def _(sp):
                for sem in q.values():
                    sp.sem_inc(sem, BASE)
        return q


RSQRT_LINKS = 12


def rsqrt(dve, chain, out, var, half, tmp):
    chain.link(dve.tensor_scalar(out.bitcast(I32), var.bitcast(I32), 1, None, ALU.logical_shift_right))
    chain.link(dve.tensor_scalar(out.bitcast(I32), out.bitcast(I32), -1.0, float(0x5F3759DF), ALU.mult, ALU.add))
    chain.link(dve.tensor_scalar(half, var, -0.5, None, ALU.mult))
    for _ in range(3):
        chain.link(dve.tensor_tensor(tmp, out, out, ALU.mult))
        chain.link(dve.tensor_tensor(tmp, tmp, half, ALU.mult))
        chain.link(dve.scalar_tensor_tensor(out=out, in0=tmp, scalar=1.5, in1=out, op0=ALU.add, op1=ALU.mult))


def layernorm_stage(nc, g, name):
    acc, xn, ident = g["acc"], g["xn"], g["ident"]
    with ExitStack() as ctx:
        s = Stage(nc, ctx, name)
        xs = s.sb("xs", [P, 2, L])
        stats = s.sb("stats", [P, NT, 6])
        mv = s.sb("mv", [P, NT, 2])
        rstd = s.sb("rstd", [P, NT])
        half = s.sb("half", [P, NT])
        tmp = s.sb("tmp", [P, NT])
        xh = s.sb("xh", [P, 2, NT, P])
        tok = s.banks("tok", 2)
        fea = s.banks("fea", 2)
        q = s.sems("copied turned normed back stored dch")
        copied, turned, normed, back, stored, dch = q.values()

        def pairs(eng, body):
            body(0, 0)
            with eng.Fori(0, NB // 2 - 1) as i:
                body(i * 2 + 1, 1)
                body(i * 2 + 2, 0)
            body(NB - 1, 1)

        with nc.Block() as block:
            @block.scalar
            def _(act):
                def store(b, k):
                    act.wait_ge(back, BASE + b + 1)
                    act.activation(xn[:, b, :], fea[:, k, :], ACT.Copy).then_inc(stored, 1)

                def body(b, k):
                    act.wait_ge(turned, BASE + b - 1)
                    act.activation(xs[:, k, :], acc[:, b, :], ACT.Copy).then_inc(copied, 1)
                    if not isinstance(b, int) or b > 0:
                        store(b - 1, 1 - k)

                pairs(act, body)
                store(NB - 1, 1)

            @block.tensor
            def _(pe):
                def turn_back(b, k):
                    pe.wait_ge(normed, BASE + b + 1)
                    pe.wait_ge(stored, BASE + b - 1)
                    for t in range(NT):
                        mm = pe.transpose(fea[:, k, t * P:(t + 1) * P], xh[:, k, t, :], ident[:, :])
                    mm.then_inc(back, 1)

                def body(b, k):
                    pe.wait_ge(copied, BASE + b + 1)
                    pe.wait_ge(normed, BASE + b - 1)
                    for t in range(NT):
                        mm = pe.transpose(tok[:, k, t * P:(t + 1) * P], xs[:, k, t * P:(t + 1) * P], ident[:, :])
                    mm.then_inc(turned, 1)
                    if not isinstance(b, int) or b > 0:
                        turn_back(b - 1, 1 - k)

                pairs(pe, body)
                turn_back(NB - 1, 1)

            @block.vector
            def _(dve):
                c = Chain(dve, dch, 2 * NT + 1 + RSQRT_LINKS)

                def body(b, k):
                    c.start(b)
                    dve.wait_ge(turned, BASE + b + 1)
                    for t in range(NT):
                        c.tick(dve.bn_stats(stats[:, t, :], tok[:, k, t * P:(t + 1) * P]))
                    c.wait()
                    dve.memset(tmp[:, :], 0.0)
                    for t in range(NT):
                        c.tick(dve.bn_aggr(mv[:, t, :], stats[:, t, :]))
                    c.wait()
                    c.link(dve.tensor_scalar(mv[:, :, 1], mv[:, :, 1], EPS, None, ALU.add))
                    rsqrt(dve, c, rstd[:, :], mv[:, :, 1], half[:, :], tmp[:, :])
                    dve.wait_ge(back, BASE + b - 1)
                    for t in range(NT):
                        ins = dve.tensor_scalar(xh[:, k, t, :], tok[:, k, t * P:(t + 1) * P], mv[:, t, 0:1],
                                                rstd[:, t:t + 1], ALU.subtract, ALU.mult)
                    ins.then_inc(normed, 1)
                    c.end()

                pairs(dve, body)


DI, DS, DC, DR = 256, 16, 4, 8


def mamba_stage(nc, g, d):
    acc, xn, ident = g["acc"], g["xn"], g["ident"]
    NH = DI // P
    NX = 2 * DS + DR
    with ExitStack() as ctx:
        s = Stage(nc, ctx, "ma")
        w_in = s.sb("w_in", [P, 2 * DI])
        w_x = s.sb("w_x", [P, NH, NX])
        w_dt = s.sb("w_dt", [DR, DI])
        w_out = s.sb("w_out", [P, NH, P])
        par = s.sb("par", [P, NH, DC + 3])
        alog = s.sb("alog", [P, NH, DS])
        aexp = s.sb("aexp", [P, NH, DS])
        u = s.sb("u", [P, NH, DC - 1 + L])
        cv = s.sb("cv", [P, NH, L])
        uc = s.sb("uc", [P, 2, NH, L])
        zg = s.sb("zg", [P, 2, NH, L])
        xd = s.sb("xd", [DR, L])
        bc = s.sb("bc", [2 * DS, L])
        rest = s.sb("rest", [2 * DS, L])
        mid = s.sb("mid", [2 * DS, L], BF16)
        parts = s.sb("parts", [3 * 2 * DS, 2, L], BF16)
        sel = s.sb("sel", [3 * 2 * DS, 2 * DS], BF16)
        v = s.sb("v", [P, NH, L])
        e = s.sb("e", [P, NH, L])
        dt = s.sb("dt", [P, 2, NH, L])
        dtu = s.sb("dtu", [P, 2, NH, L])
        bs = s.sb("bs", [P, 2, L])
        da = s.sb("da", [P, 4, L])
        db = s.sb("db", [P, 4, L])
        h = s.sb("h", [P, 2, L])
        hc = s.sb("hc", [P, 4, L])
        y = s.sb("y", [P, NH, L])
        BC = s.banks("BC", 4)
        Y = s.banks("Y", 2)
        M = s.banks("M", 2)
        q = s.sems("loaded selready split aready acopy udone uread zdone zread upad conv ucdone xdone xread dtdone vread "
                   "eready dtready dtuready bdone cdone bcopied bfree daready dbready scanned hcready hcfree yread "
                   "outdone outread dch ych ach held")
        NS = DS * NH

        with nc.Block() as block:
            @block.sync
            def _(sp):
                for dst, src in ((w_in, "m_w_in"), (w_x, "m_w_x"), (w_dt, "m_w_dt"), (w_out, "m_w_out"),
                                 (par, "m_par"), (alog, "m_alog")):
                    sp.dma_start(dst[:], d[src]).then_inc(q["loaded"], 16)

            def batches(eng, prepare, scan):
                for n in range(DS):
                    prepare(0, 0, n)
                scan(0, 0, prepare)
                with eng.Fori(0, NB // 2 - 1) as i:
                    scan(i * 2 + 1, 1, prepare)
                    scan(i * 2 + 2, 0, prepare)
                scan(NB - 1, 1, lambda b, k, n: None)

            @block.scalar
            def _(act):
                act.wait_ge(q["loaded"], BASE + 6 * 16)
                act.activation(aexp[:], alog[:], ACT.Exp).then_inc(q["aready"], 1)
                act.wait_ge(q["acopy"], BASE + 1)
                act.wait_ge(q["upad"], BASE + 1)
                c = Chain(act, q["ach"], 3)

                def prepare(b, k, n):
                    if n == 4:
                        act.wait_ge(q["udone"], BASE + b + 1)
                        act.wait_ge(q["conv"], BASE + b * NH)
                        act.activation(u[:, :, DC - 1:], M[:, :, :], ACT.Copy).then_inc(q["uread"], 1)
                    if n == 8:
                        act.wait_ge(q["zdone"], BASE + b + 1)
                        act.wait_ge(q["yread"], BASE + b - 1)
                        act.activation(zg[:, k], M[:, :, :], ACT.Silu).then_inc(q["zread"], 1)
                        act.wait_ge(q["conv"], BASE + (b + 1) * NH)
                        act.activation(uc[:, k], cv[:], ACT.Silu).then_inc(q["ucdone"], 1)
                    if n == 11:
                        act.wait_ge(q["xdone"], BASE + b + 1)
                        act.wait_ge(q["dtdone"], BASE + b)
                        act.wait_ge(q["split"], BASE + b)
                        act.activation(xd[:, :], M[2 * DS:NX, 0, :], ACT.Copy)
                        act.activation(bc[:, :], M[0:2 * DS, 0, :], ACT.Copy).then_inc(q["xread"], 1)
                    if n == 13:
                        c.start(b)
                        act.wait_ge(q["dtdone"], BASE + b + 1)
                        act.wait_ge(q["dtready"], BASE + b)
                        for i in range(NH):
                            ins = act.activation(v[:, i, :], M[:, i, :], ACT.Identity, bias=par[:, i, DC + 1:DC + 2])
                        c.link(ins)
                        act.sem_inc(q["vread"], 1)
                        c.link(act.activation(e[:], v[:], ACT.Abs))
                    if n == 14:
                        c.link(act.activation(e[:], e[:], ACT.Exp, scale=-1.0))
                        act.activation(e[:], e[:], ACT.Ln, bias=1.0).then_inc(q["eready"], 1)
                        c.end()

                def scan(b, kb, prepare):
                    act.wait_ge(q["dtready"], BASE + b + 1)
                    for n in range(DS):
                        act.wait_ge(q["bdone"], BASE + b * DS + n + 1)
                        act.wait_ge(q["bfree"], BASE + b * DS + n)
                        act.activation(bs[:, n % 2, :], BC[:, 2 * (n % 2), :], ACT.Copy).then_inc(q["bcopied"], 1)
                        for k in range(NH):
                            act.wait_ge(q["scanned"], BASE + b * NS + (NH * n + k - 3))
                            act.activation(da[:, (NH * n + k) % 4, :], dt[:, kb, k, :], ACT.Exp,
                                           scale=aexp[:, k, n:n + 1]).then_inc(q["daready"], 1)
                        prepare(b + 1, 1 - kb, n)

                batches(act, prepare, scan)

            @block.gpsimd
            def _(pool):
                pool.memset(u[:], 0.0).then_inc(q["upad"], 1)
                for k in range(3):
                    rows = slice(k * 2 * DS, (k + 1) * 2 * DS)
                    pool.tensor_copy(sel[rows, :], ident[rows, rows]).then_inc(q["selready"], 1)
                    pool.wait_ge(q["selready"], BASE + k + 1)
                pool.wait_ge(q["aready"], BASE + 1)
                pool.tensor_scalar(aexp[:], aexp[:], -1.0, None, ALU.mult).then_inc(q["acopy"], 1)
                pool.sem_inc(q["bfree"], 1)

                def scan(b, kb):
                    pool.wait_ge(q["dtuready"], BASE + b + 1)
                    for n in range(DS):
                        pool.wait_ge(q["bcopied"], BASE + b * DS + n + 1)
                        for k in range(NH):
                            pool.wait_ge(q["scanned"], BASE + b * NS + (NH * n + k - 3))
                            ins = pool.tensor_tensor(db[:, (NH * n + k) % 4, :], dtu[:, kb, k, :], bs[:, n % 2, :], ALU.mult)
                            ins.then_inc(q["dbready"], 1)
                        pool.wait_ge(q["dbready"], BASE + b * NS + NH * (n + 1))
                        pool.sem_inc(q["bfree"], 1)

                with pool.Fori(0, NB // 2) as i:
                    scan(i * 2, 0)
                    scan(i * 2 + 1, 1)

            @block.tensor
            def _(pe):
                pe.wait_ge(q["loaded"], BASE + 6 * 16)
                pe.wait_ge(q["selready"], BASE + 3)

                def prepare(b, k, n):
                    if n == 2:
                        pe.wait_ge(q["vread"], BASE + b)
                        pe.wait_ge(q["outread"], BASE + b - 1)
                        settle(pe, q["held"])
                    if n in (2, 3):
                        mm = pe.matmul(M[:, n - 2, :], w_in[:, (n - 2) * P:(n - 1) * P], xn[:, b, :], start=True, stop=True)
                        if n == 3:
                            mm.then_inc(q["udone"], 1)
                    if n == 5:
                        pe.wait_ge(q["uread"], BASE + b + 1)
                        settle(pe, q["held"])
                    if n in (5, 6):
                        i = n - 5
                        mm = pe.matmul(M[:, i, :], w_in[:, (NH + i) * P:(NH + i + 1) * P], xn[:, b, :], start=True, stop=True)
                        if n == 6:
                            mm.then_inc(q["zdone"], 1)
                    if n == 8:
                        pe.wait_ge(q["zread"], BASE + b + 1)
                        pe.wait_ge(q["ucdone"], BASE + b + 1)
                    if n in (8, 9):
                        i = n - 8
                        mm = pe.matmul(M[0:NX, 0, :], w_x[:, i, :], uc[:, k, i, :], start=(i == 0), stop=(i == NH - 1))
                        if n == 9:
                            mm.then_inc(q["xdone"], 1)
                    if n == 11:
                        pe.wait_ge(q["xread"], BASE + b + 1)
                    if n in (11, 12):
                        i = n - 11
                        mm = pe.matmul(M[:, i, :], w_dt[:, i * P:(i + 1) * P], xd[:, :], start=True, stop=True)
                        if n == 12:
                            mm.then_inc(q["dtdone"], 1)

                def output(b, k):
                    if k == 0:
                        pe.wait_ge(q["yread"], BASE + b + 1)
                    mm = pe.matmul(M[:, 0, :], w_out[:, k, :], y[:, k, :], start=(k == 0), stop=(k == NH - 1))
                    if k == NH - 1:
                        mm.then_inc(q["outdone"], 1)

                def scan(b, kb, prepare):
                    def spread(j, n):
                        mm = pe.matmul(BC[:, 2 * (n % 2) + j, :],
                                       sel[:, j * DS + n:j * DS + n + 1].broadcast_to([3 * 2 * DS, P]), parts[:, kb, :],
                                       start=True, stop=True)
                        mm.then_inc(q["bdone"] if j == 0 else q["cdone"], 1)

                    def spread_b(n):
                        pe.wait_ge(q["bcopied"], BASE + b * DS + n - 1)
                        spread(0, n)

                    def spread_c(n):
                        pe.wait_ge(q["hcready"], BASE + b * NS + NH * (n - 1))
                        spread(1, n)

                    pe.wait_ge(q["split"], BASE + b + 1)
                    settle(pe, q["held"])
                    spread_b(0)
                    spread_b(1)
                    spread_c(0)
                    pe.wait_ge(q["yread"], BASE + b)
                    settle(pe, q["held"])
                    for n in range(DS):
                        if n + 2 < DS:
                            spread_b(n + 2)
                        if n + 1 < DS:
                            spread_c(n + 1)
                        for k in range(NH):
                            pe.wait_ge(q["hcready"], BASE + b * NS + NH * n + k + 1)
                            pe.matmul(Y[:, k, :], ident[:, :], hc[:, (NH * n + k) % 4, :], start=(n == 0),
                                      stop=(n == DS - 1)).then_inc(q["hcfree"], 1)
                        if n < NH and not (isinstance(b, int) and b == 0):
                            if n == 0:
                                pe.wait_ge(q["vread"], BASE + b + 1)
                                settle(pe, q["held"])
                            output(b - 1, n)
                        prepare(b + 1, 1 - kb, n)

                batches(pe, prepare, scan)
                for k in range(NH):
                    output(NB - 1, k)

            @block.vector
            def _(dve):
                c = Chain(dve, q["dch"], (DC - 1) * NH + 5 + 1)
                dve.wait_ge(q["loaded"], BASE + 6 * 16)
                dve.sem_inc(q["hcfree"], 4)

                def prepare(b, k, n):
                    if n in (5, 6):
                        if n == 5:
                            c.start(b)
                            dve.wait_ge(q["uread"], BASE + b + 1)
                            dve.wait_ge(q["ucdone"], BASE + b)
                        i = n - 5
                        c.link(dve.tensor_scalar(cv[:, i, :], u[:, i, 0:L], par[:, i, 0:1], par[:, i, DC:DC + 1],
                                                 ALU.mult, ALU.add))
                        for tap in range(1, DC):
                            ins = dve.scalar_tensor_tensor(out=cv[:, i, :], in0=u[:, i, tap:tap + L],
                                                           scalar=par[:, i, tap:tap + 1], in1=cv[:, i, :],
                                                           op0=ALU.mult, op1=ALU.add)
                            if tap < DC - 1:
                                c.link(ins)
                        ins.then_inc(q["conv"], 1)
                    if n == 11:
                        dve.wait_ge(q["xread"], BASE + b + 1)
                        if not (isinstance(b, int) and b == 0):
                            dve.wait_ge(q["bdone"], BASE + (b - 1) * DS)
                            dve.wait_ge(q["cdone"], BASE + (b - 1) * DS)
                        w = 2 * DS
                        c.link(dve.tensor_copy(parts[0:w, k, :], bc[:, :]))
                        c.link(dve.tensor_tensor(rest[:, :], bc[:, :], parts[0:w, k, :], ALU.subtract))
                        c.link(dve.tensor_copy(mid[:, :], rest[:, :]))
                        c.link(dve.tensor_copy(parts[w:2 * w, k, :], mid[:, :]))
                        c.link(dve.tensor_tensor(parts[2 * w:3 * w, k, :], rest[:, :], mid[:, :], ALU.subtract))
                        dve.sem_inc(q["split"], 1)
                    if n == 15:
                        dve.wait_ge(q["eready"], BASE + b + 1)
                        if not (isinstance(b, int) and b == 0):
                            dve.wait_ge(q["daready"], BASE + (b - 1) * NS)
                        c.link(dve.tensor_scalar(v[:], v[:], 0.0, None, ALU.max))
                        dve.tensor_tensor(dt[:, k], v[:], e[:], ALU.add).then_inc(q["dtready"], 1)
                        c.end()
                    if n == 15:
                        dve.wait_ge(q["dtready"], BASE + b + 1)
                        if not (isinstance(b, int) and b == 0):
                            dve.wait_ge(q["dbready"], BASE + (b - 1) * NS)
                        dve.tensor_tensor(dtu[:, k], dt[:, k], uc[:, k], ALU.mult).then_inc(q["dtuready"], 1)

                def add_output(b):
                    dve.wait_ge(q["outdone"], BASE + b + 1)
                    dve.tensor_tensor(acc[:, b, :], acc[:, b, :], M[:, 0, :], ALU.add).then_inc(q["outread"], 1)

                def finish(b, kb):
                    dve.wait_ge(q["hcfree"], BASE + (b + 1) * NS + 4)
                    dve.wait_ge(q["outdone"], BASE + b)
                    for k in range(NH):
                        ins = dve.scalar_tensor_tensor(out=y[:, k, :], in0=uc[:, kb, k, :], scalar=par[:, k, DC + 2:DC + 3],
                                                       in1=Y[:, k, :], op0=ALU.mult, op1=ALU.add)
                    ins.then_inc(q["ych"], 1)
                    dve.wait_ge(q["ych"], BASE + b + 1)
                    dve.tensor_tensor(y[:], y[:], zg[:, kb], ALU.mult).then_inc(q["yread"], 1)

                def scan(b, kb, prepare):
                    for n in range(DS):
                        for k in range(NH):
                            i = NH * n + k
                            dve.wait_ge(q["daready"], BASE + b * NS + i + 1)
                            dve.wait_ge(q["dbready"], BASE + b * NS + i + 1)
                            dve.wait_ge(q["hcready"], BASE + b * NS + i - 1)
                            dve.tensor_tensor_scan(h[:, k, :], da[:, i % 4, :], db[:, i % 4, :], 0.0,
                                                   ALU.mult, ALU.add).then_inc(q["scanned"], 1)
                        for k in range(NH):
                            i = NH * n + k
                            dve.wait_ge(q["scanned"], BASE + b * NS + i + 1)
                            dve.wait_ge(q["hcfree"], BASE + b * NS + i + 1)
                            dve.wait_ge(q["cdone"], BASE + b * DS + n + 1)
                            dve.tensor_tensor(hc[:, i % 4, :], h[:, k, :], BC[:, 2 * (n % 2) + 1, :],
                                              ALU.mult).then_inc(q["hcready"], 1)
                        if n == 0 and not (isinstance(b, int) and b == 0):
                            finish(b - 1, 1 - kb)
                        if n == 2 and not (isinstance(b, int) and b == 0):
                            add_output(b - 1)
                        prepare(b + 1, 1 - kb, n)

                batches(dve, prepare, scan)
                finish(NB - 1, 1)
                add_output(NB - 1)


NLAYER, NHEAD, DH, WIN = 6, 16, 64, 32
NCH = NHEAD // 2
INNER = NHEAD * DH
FF = P * 4 * 2 // 3
FCH = [(c, min(P, FF - c)) for c in range(0, FF, P)]
NQK = 2 * INNER // L
NPC = 3 * INNER // L
WT = P // WIN


def ffn_stage(nc, g, d, park):
    acc, xn, ident = g["acc"], g["xn"], g["ident"]
    with ExitStack() as ctx:
        s = Stage(nc, ctx, "ff")
        w_qkv = s.sb("w_qkv", [P, 3 * INNER])
        w_o = s.sb("w_o", [P, NCH, P])
        w_1 = s.sb("w_1", [P, 2 * FF])
        w_2 = s.sb("w_2", [P, len(FCH), P])
        par = s.sb("par", [P, 3 + 2 * len(FCH)])
        qk_s = s.sb("qk_s", [P, 4, DH])
        tab = s.sb("tab", [P, 4, NT, DH])
        mask_f = s.sb("mask_f", [P, 2, DH])
        mask = s.sb("mask", [P, 2, NCH, DH], BF16)
        ident_b = s.sb("ident_b", [P, P], BF16)
        xs = s.sb("xs", [P, L])
        xs1 = s.sb("xs1", [P, L])
        raw = s.sb("raw", [P, 2, NQK, L])
        sq = s.sb("sq", [P, NQK * L])
        n2 = s.sb("n2", [P, 2 * NHEAD])
        inv = s.sb("inv", [P, 2 * NHEAD])
        half = s.sb("half", [P, 2 * NHEAD])
        tmp = s.sb("tmp", [P, 2 * NHEAD])
        rc = s.sb("rc", [P, 2, NQK * L])
        qT = s.sb("qT", [P, 2, NCH, P])
        kT = s.sb("kT", [P, 2, 2, NCH, WIN + P])
        v = s.sb("v", [P, 2, INNER])
        v2 = s.sb("v2", [P, 2, WT, 2, NCH * DH])
        mx = s.sb("mx", [P, NHEAD])
        ssum = s.sb("ssum", [P, NHEAD])
        pr = s.sb("pr", [P, 2, NCH, 2, DH])
        pT = s.sb("pT", [P, NCH, P])
        ot = s.sb("ot", [P, INNER])
        oT = acc
        stats = s.sb("stats", [P, NT, 6])
        mv = s.sb("mv", [P, NT, 2])
        xh = s.sb("xh", [P, NT, P])
        x2 = s.sb("x2", [P, L])
        gg = s.sb("gg", [P, L])
        hh = s.sb("hh", [P, 2, L])
        QA = s.banks("QA", 2)
        TR = s.banks("TR", 2)
        S = s.banks("S", 2)
        O = s.banks("O", 2)
        q = s.sems("const x_in ff_in masks tabs padded xs_ready qa_fill qa_read0 qa_read1 raw_ready sq_ready "
                   "n2_done rs_ready rc_ready tr_fill tr_read0 tr_read1 qk_turned s_fill s_read p_exp p_sum p_ready "
                   "pt_ready o_fill o_read o_turned v_ready v2_in0 v2_in1 x1_ready xh_ready x2_ready g_ready "
                   "h_ready h_used ff_done wo_done xs1_ready parked back dch held")
        qa_read, tr_read, v2_in = ([q[f"{n}{k}"] for k in range(2)] for n in ("qa_read", "tr_read", "v2_in"))

        FFS = {2: [("Wo", 0, 1)], 3: [("tok", 0, 1), ("fea", 0, 1), ("W", 0, 1)]}
        TLINKS = {"X": 2 + RSQRT_LINKS + 3, "Y": 2, "Z": 2, "tok": 2 * NT + 1 + RSQRT_LINKS}

        ORDER = ("tok", "X", "T", "Wo", "fea", "Y", "V", "Z", "S", "PV", "W")

        def a_pass(steps):
            order = []
            for x, ff in steps:
                f = {k[0]: k for k in ff}
                names = {k[0]: k for k in x}
                for key in ORDER:
                    e = f.get(key) or names.get({"V": "X", "S": "Y", "PV": "Z"}.get(key, key))
                    order += [(key,) + e[1:]] if e else []
            qa, tr = [], []
            for kind, t, back in order:
                if kind == "X":
                    qa += [("X", t, pc) for pc in range(NQK)]
                if kind == "V":
                    qa += [("V", t, pc) for pc in range(NQK, NPC)]
                if kind == "Wo":
                    qa += [("Wo",)]
                if kind == "W":
                    qa += [("W1", c, j) for c in range(len(FCH)) for j in range(2)] + [("W2",)]
                tr += [(kind, t, j) for j in range({"Y": NQK, "Z": 2, "T": 2, "tok": 1, "fea": 1}.get(kind, 0))]
            links = sum(TLINKS.get(kind, 0) for kind, _, _ in order)
            return {"steps": steps, "order": order, "qa": {k: n for n, k in enumerate(qa)},
                    "tr": {k: n for n, k in enumerate(tr)}, "links": links}

        def steps_of(i, lo, hi):
            return [("XYZT"[lag], (i - lag) % NT, 0 if i >= lag else 1) for lag in range(4) if lo <= i - lag < hi]

        first = a_pass([(steps_of(i, 0, NT), []) for i in range(NT)])
        loop = a_pass([(steps_of(i, -NT, NT), FFS.get(i, [])) for i in range(NT)])
        last = a_pass([(steps_of(i, -NT, 0), FFS.get(i, [])) for i in range(NT)])
        QN, TN, LINKS = len(loop["qa"]), len(loop["tr"]), loop["links"]
        first["before"] = (0, 0, 0)
        loop["before"] = last["before"] = tuple(-len(x) if not isinstance(x, int) else -x
                                                for x in (last["qa"], last["tr"], last["links"]))
        assert all(len(p[r]) % 2 == 0 for p in (first, loop, last) for r in ("qa", "tr"))
        assert len(first["qa"]) + len(last["qa"]) == QN and len(first["tr"]) + len(last["tr"]) == TN
        X_LOADS = 3
        ff_loads = ((w_o, "f_w_o"), (w_1, "f_w_1"), (w_2, "f_w_2"), (par, "f_par"))

        def passes(eng, body):
            body(first, 0, 0, None, 0, None)
            with eng.Fori(0, NLAYER - 1) as l:
                with eng.Fori(1, NB) as b:
                    body(loop, l * NB + b, b, b - 1, None, l)
                body(loop, l * NB + NB, 0, NB - 1, l + 1, l)
            with eng.Fori(1, NB) as b:
                body(loop, b + (NLAYER - 1) * NB, b, b - 1, None, NLAYER - 1)
            body(last, NLAYER * NB, None, NB - 1, None, NLAYER - 1)

        def ff_weights(eng, l):
            eng.wait_ge(q["ff_in"], BASE + (l + 1) * (len(ff_loads) * 16))

        def ring(p, n, name, key):
            N, before, k = (QN, p["before"][0], p["qa"][key]) if name == "qa" else (TN, p["before"][1], p["tr"][key])
            return k % 2, n * (N // 2) + (before // 2 + k // 2), n * N + (before + k)

        def fill_qa(pe, p, n, key):
            k, bank_fills, _ = ring(p, n, "qa", key)
            pe.wait_ge(qa_read[k], BASE + bank_fills)
            return QA[:, k, :]

        def fill_tr(pe, p, n, key):
            k, bank_fills, _ = ring(p, n, "tr", key)
            pe.wait_ge(tr_read[k], BASE + bank_fills)
            return TR[:, k, :]

        def filled_qa(eng, p, n, key):
            k, _, fills = ring(p, n, "qa", key)
            eng.wait_ge(q["qa_fill"], BASE + 1 + fills)
            return QA[:, k, :], qa_read[k]

        def filled_tr(eng, p, n, key):
            k, _, fills = ring(p, n, "tr", key)
            eng.wait_ge(q["tr_fill"], BASE + 1 + fills)
            return TR[:, k, :], tr_read[k]

        def is_read(eng, p, n, name, key):
            k, bank_fills, _ = ring(p, n, name, key)
            eng.wait_ge((qa_read if name == "qa" else tr_read)[k], BASE + 1 + bank_fills)

        with nc.Block() as block:
            @block.sync
            def _(sp):
                sp.dma_start(mask_f[:], d["f_mask"]).then_inc(q["const"], 16)
                sp.dma_start(park, acc[:, :, :]).then_inc(q["parked"], 16)
                def lay_v(n):
                    for t in range(NT):
                        sp.wait_ge(q["v_ready"], BASE + n * NT + t + 1)
                        settle(sp, q["held"])
                        sp.wait_ge(q["o_fill"], BASE + n * NT + (t - 1))
                        settle(sp, q["held"])
                        for z in range(2):
                            for w in range(WT):
                                for old in range(2):
                                    r0 = 64 * z + WIN * (1 - old)
                                    k, w_v = (t % 2, w - old) if w >= old else ((t - 1) % 2, WT - 1)
                                    sp.dma_start(v2[r0:r0 + WIN, t % 2, w, z, :],
                                                 v[WIN * w_v:WIN * w_v + WIN, k, z * L:z * L + L]
                                                 ).then_inc(v2_in[t % 2], 16)

                with sp.Fori(0, NLAYER) as l:
                    sp.wait_ge(q["v_ready"], BASE + l * NB * NT)
                    settle(sp, q["held"])
                    sp.dma_start(w_qkv[:], d["f_w_qkv"][l]).then_inc(q["x_in"], 16)
                    sp.wait_ge(q["rc_ready"], BASE + l * NB * NT)
                    settle(sp, q["held"])
                    sp.dma_start(qk_s[:], d["f_qk_s"][l]).then_inc(q["x_in"], 16)
                    sp.dma_start(tab[:], d["f_ctab"]).then_inc(q["x_in"], 16)
                    lay_v(l * NB)
                    sp.wait_ge(q["ff_done"], BASE + l * NB)
                    settle(sp, q["held"])
                    for dst, src in ff_loads:
                        sp.dma_start(dst[:], d[src][l]).then_inc(q["ff_in"], 16)
                    with sp.Fori(1, NB) as b:
                        lay_v(l * NB + b)
                sp.wait_ge(q["wo_done"], BASE + NLAYER * NB)
                sp.dma_start(acc[:, :, :], park).then_inc(q["back"], 16)

            @block.gpsimd
            def _(pool):
                pool.memset(v2[:], 0.0)
                pool.memset(kT[:], 0.0)
                pool.memset(v[:, 1, :], 0.0)
                pool.memset(xs1[:, :], 0.0)
                pool.memset(xs[:, :], 0.0).then_inc(q["padded"], 1)
                pool.wait_ge(q["const"], BASE + 16)
                pool.tensor_copy(ident_b[:, :], ident[:, :])
                for j in range(2):
                    for c in range(NCH):
                        ins = pool.tensor_copy(mask[:, j, c, :], mask_f[:, j, :])
                ins.then_inc(q["masks"], 1)
                def scale_table(l):
                    pool.wait_ge(q["x_in"], BASE + (l + 1) * (X_LOADS * 16))
                    for k in range(4):
                        ins = pool.tensor_tensor(tab[:, k, :, :], tab[:, k, :, :],
                                                 qk_s[:, k:k + 1, :].broadcast_to([P, NT, DH]), ALU.mult)
                    ins.then_inc(q["tabs"], 1)
                    pool.wait_ge(q["tabs"], BASE + l + 1)
                    settle(pool, q["held"])

                def body(p, n, b, before, new, l):
                    def rotate(t):
                        pool.wait_ge(q["raw_ready"], BASE + n * NT + t + 1)
                        pool.wait_ge(q["n2_done"], BASE + n * NT + t + 1)
                        for k in range(2):
                            x = raw[:, t % 2, 2 * k:2 * k + 2, :].rearrange("p c (h z e) -> p (c h) z e", z=2, e=DH // 2)
                            y = sq[:, k * INNER:(k + 1) * INNER].rearrange("p (h z e) -> p h z e", z=2, e=DH // 2)
                            for z in range(2):
                                e0 = z * (DH // 2)
                                ins = pool.tensor_tensor(
                                    y[:, :, z, :], x[:, :, 1 - z, :],
                                    tab[:, 2 + k, t:t + 1, e0:e0 + DH // 2].broadcast_to([P, NHEAD, DH // 2]), ALU.mult)
                        ins.then_inc(q["rs_ready"], 1)

                    def norm_p(t, n):
                        pool.wait_ge(q["p_sum"], BASE + n * NT + t + 1)
                        x = pr[:, t % 2, :, :, :].rearrange("p c z e -> p (c z) e")
                        pool.tensor_tensor(x, x, ssum[:, :].unsqueeze(2).broadcast_to([P, NHEAD, DH]),
                                           ALU.mult).then_inc(q["p_ready"], 1)

                    for step, _ in p["steps"]:
                        x = {kind: (t, n - back) for kind, t, back in step}
                        if "Z" in x:
                            norm_p(*x["Z"])
                        if new is not None and "X" in x and x["X"][0] == 0:
                            scale_table(new)
                        if "X" in x:
                            rotate(x["X"][0])

                passes(pool, body)

            @block.scalar
            def _(act):
                act.wait_ge(q["padded"], BASE + 1)
                act.wait_ge(q["parked"], BASE + 16)
                def body(p, n, b, before, new, l):
                    def shift(dst, b, done):
                        settle(act, q["held"])
                        act.activation(dst[0:64, :], xn[0:64, b, :], ACT.Copy)
                        act.activation(dst[64:P, 1:L], xn[64:P, b, 0:L - 1], ACT.Copy).then_inc(done, 1)

                    def copy_qk(t, between):
                        act.wait_ge(q["rc_ready"], BASE + n * NT + (t - 1))
                        for pc in range(NQK):
                            bank, read = filled_qa(act, p, n, ("X", t, pc))
                            act.activation(raw[:, t % 2, pc, :], bank, ACT.Copy).then_inc(read, 1)
                            if pc == NQK - 1:
                                between()
                            if pc % 2 == 1:
                                is_read(act, p, n, "qa", ("X", t, pc - 1))
                                is_read(act, p, n, "qa", ("X", t, pc))
                                act.wait_ge(q["rc_ready"], BASE + n * NT + t)
                                ins = act.activation(sq[:, (pc - 1) * L:(pc + 1) * L], raw[:, t % 2, pc - 1:pc + 1, :],
                                                     ACT.Square)
                        ins.then_inc(q["sq_ready"], 1)
                        act.sem_inc(q["raw_ready"], 1)

                    def copy_v(t):
                        act.wait_ge(v2_in[t % 2], BASE + (2 * n + t // 2) * 256)
                        act.wait_ge(v2_in[(t - 1) % 2], BASE + (2 * n + ((t - 1) // 2 + 1)) * 256)
                        for pc in range(NQK, NPC):
                            bank, read = filled_qa(act, p, n, ("V", t, pc))
                            act.activation(v[:, t % 2, (pc - NQK) * L:(pc - NQK + 1) * L], bank, ACT.Copy).then_inc(read, 1)
                        for pc in range(NQK, NPC):
                            is_read(act, p, n, "qa", ("V", t, pc))
                        act.sem_inc(q["v_ready"], 1)

                    def turn_qk(t, m):
                        act.wait_ge(q["s_fill"], BASE + m * NT + t)
                        for j in range(NQK):
                            bank, read = filled_tr(act, p, n, ("Y", t, j))
                            src = bank.rearrange("p (c x) -> p c x", x=P)
                            c0 = 4 * (j % 2)
                            if j < NQK // 2:
                                act.activation(qT[:, t % 2, c0:c0 + 4, :], src, ACT.Copy).then_inc(read, 1)
                                continue
                            for z in range(2):
                                rows = slice(64 * z, 64 * z + 64)
                                act.activation(kT[rows, t % 2, z, c0:c0 + 4, WIN:], src[rows, :, :], ACT.Copy)
                                ins = act.activation(kT[rows, (t + 1) % 2, z, c0:c0 + 4, 0:WIN],
                                                     src[rows, :, P - WIN:P], ACT.Copy)
                            ins.then_inc(read, 1)
                        for j in (NQK - 2, NQK - 1):
                            is_read(act, p, n, "tr", ("Y", t, j))
                        act.sem_inc(q["qk_turned"], 1)

                    def turn_p(t, m):
                        act.wait_ge(q["o_fill"], BASE + m * NT + t)
                        for j in range(2):
                            bank, read = filled_tr(act, p, n, ("Z", t, j))
                            act.activation(pT[:, 4 * j:4 * j + 4, :], bank.rearrange("p (c x) -> p c x", x=P),
                                           ACT.Copy).then_inc(read, 1)
                        for j in range(2):
                            is_read(act, p, n, "tr", ("Z", t, j))
                        act.sem_inc(q["pt_ready"], 1)

                    def turn_o(t, m):
                        if t == 0:
                            act.wait_ge(q["wo_done"], BASE + m)
                        for j in range(2):
                            bank, read = filled_tr(act, p, n, ("T", t, j))
                            act.activation(oT[:, 4 * j:4 * j + 4, t * P:(t + 1) * P],
                                           bank.rearrange("p (c x) -> p c x", x=P), ACT.Copy).then_inc(read, 1)
                        for j in range(2):
                            is_read(act, p, n, "tr", ("T", t, j))
                        act.sem_inc(q["o_turned"], 1)

                    def exp_p(t, m):
                        act.wait_ge(q["s_read"], BASE + m * NT + t + 1)
                        act.activation(pr[:, t % 2, :, :, :], pr[:, t % 2, :, :, :], ACT.Exp,
                                       scale=8.0).then_inc(q["p_exp"], 1)

                    for step, ff in p["steps"]:
                        ff = {k for k, _, _ in ff}
                        x = {kind: (t, n - back) for kind, t, back in step}

                        def exp_z():
                            if "Z" in x:
                                exp_p(*x["Z"])

                        if "X" in x:
                            if x["X"][0] == 0:
                                act.wait_ge(q["ff_done"], BASE + n - (NB - 1))
                                shift(xs, b, q["xs_ready"])
                            copy_qk(x["X"][0], exp_z)
                        else:
                            exp_z()
                        if "T" in x:
                            turn_o(*x["T"])
                        if "fea" in ff:
                            ff_weights(act, l)
                            settle(act, q["held"])
                            bank, read = filled_tr(act, p, n, ("fea", 0, 0))
                            act.activation(x2[:, :], bank, ACT.Identity, scale=par[:, 0:1],
                                           bias=par[:, 1:2]).then_inc(read, 1)
                            is_read(act, p, n, "tr", ("fea", 0, 0))
                            act.sem_inc(q["x2_ready"], 1)
                        if "Y" in x:
                            turn_qk(*x["Y"])
                        if "Z" in x:
                            turn_p(*x["Z"])
                        if "X" in x:
                            copy_v(x["X"][0])
                        if "Wo" in ff:
                            act.wait_ge(q["x1_ready"], BASE + n)
                            shift(xs1, before, q["xs1_ready"])
                        if "W" in ff:
                            for c, (_, m) in enumerate(FCH):
                                bank, read = filled_qa(act, p, n, ("W1", c, 0))
                                act.wait_ge(q["h_ready"], BASE + (n - 1) * len(FCH) + c)
                                act.activation(gg[0:m, :], bank[0:m, :], ACT.Gelu, bias=par[0:m, 6 + c:7 + c]).then_inc(read, 1)
                                is_read(act, p, n, "qa", ("W1", c, 0))
                                act.sem_inc(q["g_ready"], 1)

                passes(act, body)

            @block.tensor
            def _(pe):
                pe.wait_ge(q["masks"], BASE + 1)
                def body(p, n, b, before, new, l):
                    def project(t, _):
                        if t == 0:
                            if new is not None:
                                pe.wait_ge(q["x_in"], BASE + (new + 1) * (X_LOADS * 16))
                                settle(pe, q["held"])
                            pe.wait_ge(q["xs_ready"], BASE + n + 1)
                        pieces("X", t, range(NQK))

                    def pieces(kind, t, pcs):
                        for pc in pcs:
                            bank = fill_qa(pe, p, n, (kind, t, pc))
                            pe.matmul(bank, xs[:, t * P:(t + 1) * P], w_qkv[:, pc * L:(pc + 1) * L],
                                      start=True, stop=True).then_inc(q["qa_fill"], 1)

                    def project_v(t, _):
                        pieces("V", t, range(NQK, NPC))

                    def turn_qk(t, m):
                        pe.wait_ge(q["rc_ready"], BASE + m * NT + t + 1)
                        for j in range(NQK):
                            bank = fill_tr(pe, p, n, ("Y", t, j))
                            for c in range(4):
                                mm = pe.transpose(bank[:, c * P:(c + 1) * P],
                                                  rc[:, t % 2, j * L + c * P:j * L + (c + 1) * P], ident[:, :])
                            mm.then_inc(q["tr_fill"], 1)

                    def scores(t, m):
                        pe.wait_ge(q["qk_turned"], BASE + m * NT + t + 1)
                        pe.wait_ge(q["s_read"], BASE + m * NT + t)
                        for k in range(2):
                            pe.matmul(S[:, k, :], ident_b[:, :], mask[:, 0 if t == 0 else 1, :, :], start=True,
                                      stop=False, skip_group_check=True)
                        for c in range(NCH):
                            for w in range(WT):
                                mm = pe.matmul(S[WIN * w:WIN * w + WIN, c // 4, (c % 4) * P:(c % 4 + 1) * P],
                                               qT[:, t % 2, c, WIN * w:WIN * w + WIN],
                                               kT[:, t % 2, :, c, WIN * w:WIN * w + 2 * WIN],
                                               start=False, stop=(c % 4 == 3), skip_group_check=True)
                        mm.then_inc(q["s_fill"], 1)

                    def turn_p(t, m):
                        pe.wait_ge(q["p_ready"], BASE + m * NT + t + 1)
                        for j in range(2):
                            bank = fill_tr(pe, p, n, ("Z", t, j))
                            for c in range(4):
                                mm = pe.transpose(bank[:, c * P:(c + 1) * P], pr[:, t % 2, 4 * j + c, :, :], ident[:, :])
                            mm.then_inc(q["tr_fill"], 1)

                    def attend(t, m):
                        pe.wait_ge(q["pt_ready"], BASE + m * NT + t + 1)
                        pe.wait_ge(v2_in[t % 2], BASE + (2 * m + (t // 2 + 1)) * 256)
                        pe.wait_ge(q["o_read"], BASE + m * NT + t)
                        settle(pe, q["held"])
                        for c in range(NCH):
                            for w in range(WT):
                                mm = pe.matmul(O[WIN * w:WIN * w + WIN, c // 4, (c % 4) * P:(c % 4 + 1) * P],
                                               pT[:, c, WIN * w:WIN * w + WIN],
                                               v2[:, t % 2, w, :, c * DH:(c + 1) * DH], start=True, stop=True,
                                               skip_group_check=True)
                        mm.then_inc(q["o_fill"], 1)

                    def turn_result(t, m):
                        pe.wait_ge(q["o_read"], BASE + m * NT + t + 1)
                        for j in range(2):
                            bank = fill_tr(pe, p, n, ("T", t, j))
                            for c in range(4):
                                mm = pe.transpose(bank[:, c * P:(c + 1) * P], ot[:, (4 * j + c) * P:(4 * j + c + 1) * P],
                                                  ident[:, :])
                            mm.then_inc(q["tr_fill"], 1)

                    def output(_, m):
                        ff_weights(pe, l)
                        settle(pe, q["held"])
                        pe.wait_ge(q["o_turned"], BASE + (m + 1) * NT)
                        bank = fill_qa(pe, p, n, ("Wo",))
                        for c in range(NCH):
                            mm = pe.matmul(bank, w_o[:, c, :], oT[:, c, :], start=(c == 0), stop=(c == NCH - 1))
                        mm.then_inc(q["qa_fill"], 1)
                        pe.wait_ge(q["qa_fill"], BASE + 1 + ring(p, n, "qa", ("Wo",))[2])
                        pe.sem_inc(q["wo_done"], 1)

                    def token_major(_, m):
                        pe.wait_ge(q["xs1_ready"], BASE + m + 1)
                        bank = fill_tr(pe, p, n, ("tok", 0, 0))
                        for t in range(NT):
                            mm = pe.transpose(bank[:, t * P:(t + 1) * P], xs1[:, t * P:(t + 1) * P], ident[:, :])
                        mm.then_inc(q["tr_fill"], 1)

                    def feature_major(_, m):
                        pe.wait_ge(q["xh_ready"], BASE + m + 1)
                        bank = fill_tr(pe, p, n, ("fea", 0, 0))
                        for t in range(NT):
                            mm = pe.transpose(bank[:, t * P:(t + 1) * P], xh[:, t, :], ident[:, :])
                        mm.then_inc(q["tr_fill"], 1)

                    def feed_forward(_, m):
                        pe.wait_ge(q["x2_ready"], BASE + m + 1)
                        for c, (f0, f) in enumerate(FCH):
                            for j in range(2):
                                bank = fill_qa(pe, p, n, ("W1", c, j))
                                c0 = f0 + (1 - j) * FF
                                pe.matmul(bank[0:f, :], w_1[:, c0:c0 + f], x2[:, :], start=True,
                                          stop=True).then_inc(q["qa_fill"], 1)
                        bank = fill_qa(pe, p, n, ("W2",))
                        for c, (_, f) in enumerate(FCH):
                            pe.wait_ge(q["h_ready"], BASE + m * len(FCH) + c + 1)
                            mm = pe.matmul(bank, w_2[0:f, c, :], hh[0:f, c % 2, :], start=(c == 0), stop=(c == len(FCH) - 1))
                            if c < len(FCH) - 1:
                                mm.then_inc(q["h_used"], 1)
                        mm.then_inc(q["qa_fill"], 1)

                    run = {"X": project, "V": project_v, "Y": turn_qk, "S": scores, "Z": turn_p, "PV": attend, "T": turn_result, "Wo": output, "tok": token_major,
                           "fea": feature_major, "W": feed_forward}
                    for kind, t, back in p["order"]:
                        run[kind](t, n - back)

                passes(pe, body)

            @block.vector
            def _(dve):
                def body(p, n, b, before, new, l):
                    ch = Chain(dve, q["dch"], p["links"])
                    ch.base = BASE + n * LINKS + p["before"][2]

                    def rotate(t):
                        dve.wait_ge(q["sq_ready"], BASE + n * NT + t + 1)
                        ch.link(dve.tensor_reduce(n2[:, :], sq[:, :].rearrange("p (h e) -> p h e", e=DH), AX, ALU.add))
                        dve.sem_inc(q["n2_done"], 1)
                        ch.link(dve.tensor_scalar(n2[:, :], n2[:, :], 1e-24, None, ALU.max))
                        rsqrt(dve, ch, inv[:, :], n2[:, :], half[:, :], tmp[:, :])
                        dve.wait_ge(q["s_fill"], BASE + n * NT + (t - 1))
                        for k in range(2):
                            x = raw[:, t % 2, 2 * k:2 * k + 2, :].rearrange("p c (h e) -> p (c h) e", e=DH)
                            y = rc[:, t % 2, k * INNER:(k + 1) * INNER].rearrange("p (h e) -> p h e", e=DH)
                            ins = dve.tensor_tensor(y, x, tab[:, k, t:t + 1, :].broadcast_to([P, NHEAD, DH]), ALU.mult)
                        ch.link(ins)
                        dve.wait_ge(q["rs_ready"], BASE + n * NT + t + 1)
                        ch.link(dve.tensor_tensor(rc[:, t % 2, :], rc[:, t % 2, :], sq[:, :], ALU.add))
                        y = rc[:, t % 2, :].rearrange("p (h e) -> p h e", e=DH)
                        ch.link(dve.tensor_tensor(y, y, inv[:, :].unsqueeze(2).broadcast_to([P, 2 * NHEAD, DH]), ALU.mult))
                        dve.sem_inc(q["rc_ready"], 1)

                    def copy_o(t, m):
                        dve.wait_ge(q["o_fill"], BASE + m * NT + t + 1)
                        dve.wait_ge(q["o_turned"], BASE + m * NT + t)
                        dve.tensor_copy(ot[:, :], O[:, :, :].rearrange("p k x -> p (k x)")).then_inc(q["o_read"], 1)

                    def subtract_top(t, m):
                        tile = m * NT + t
                        dve.wait_ge(q["s_fill"], BASE + tile + 1)
                        x = S[:, :, :].rearrange("p k (h e) -> p (k h) e", e=DH)
                        ch.link(dve.tensor_reduce(mx[:, :], x, AX, ALU.max))
                        dve.wait_ge(q["o_fill"], BASE + tile - 1)
                        ch.link(dve.tensor_tensor(pr[:, t % 2, :, :, :].rearrange("p c z e -> p (c z) e"), x,
                                                  mx[:, :].unsqueeze(2).broadcast_to([P, NHEAD, DH]), ALU.subtract))
                        dve.sem_inc(q["s_read"], 1)

                    def sum_p(t, m):
                        tile = m * NT + t
                        dve.wait_ge(q["p_exp"], BASE + tile + 1)
                        dve.wait_ge(q["p_ready"], BASE + tile)
                        ch.link(dve.tensor_reduce(ssum[:, :], pr[:, t % 2, :, :, :].rearrange("p c z e -> p (c z) e"),
                                                  AX, ALU.add))
                        ch.link(dve.reciprocal(ssum[:, :], ssum[:, :]))
                        dve.sem_inc(q["p_sum"], 1)

                    def add_attention():
                        bank, read = filled_qa(dve, p, n, ("Wo",))
                        dve.tensor_tensor(xn[:, before, :], xn[:, before, :], bank, ALU.add).then_inc(read, 1)
                        is_read(dve, p, n, "qa", ("Wo",))
                        dve.sem_inc(q["x1_ready"], 1)

                    def normalise():
                        bank, read = filled_tr(dve, p, n, ("tok", 0, 0))
                        for t in range(NT):
                            ch.tick(dve.bn_stats(stats[:, t, :], bank[:, t * P:(t + 1) * P]))
                        ch.wait()
                        dve.memset(tmp[:, :], 0.0)
                        for t in range(NT):
                            ch.tick(dve.bn_aggr(mv[:, t, :], stats[:, t, :]))
                        ch.wait()
                        ch.link(dve.tensor_scalar(mv[:, :, 1], mv[:, :, 1], EPS, None, ALU.add))
                        rsqrt(dve, ch, inv[:, 0:NT], mv[:, :, 1], half[:, 0:NT], tmp[:, 0:NT])
                        dve.wait_ge(q["x2_ready"], BASE + n - 1)
                        for t in range(NT):
                            ins = dve.tensor_scalar(xh[:, t, :], bank[:, t * P:(t + 1) * P], mv[:, t, 0:1],
                                                    inv[:, t:t + 1], ALU.subtract, ALU.mult)
                        ins.then_inc(read, 1)
                        is_read(dve, p, n, "tr", ("tok", 0, 0))
                        dve.sem_inc(q["xh_ready"], 1)

                    def feed_forward():
                        ff_weights(dve, l)
                        settle(dve, q["held"])
                        for c, (_, m) in enumerate(FCH):
                            bank, read = filled_qa(dve, p, n, ("W1", c, 1))
                            dve.wait_ge(q["g_ready"], BASE + (n - 1) * len(FCH) + c + 1)
                            if c >= 2:
                                dve.wait_ge(q["h_used"], BASE + (n - 1) * (len(FCH) - 1) + c - 1)
                            dve.scalar_tensor_tensor(out=hh[0:m, c % 2, :], in0=bank[0:m, :], scalar=par[0:m, 3 + c:4 + c],
                                                     in1=gg[0:m, :], op0=ALU.add, op1=ALU.mult).then_inc(read, 1)
                            is_read(dve, p, n, "qa", ("W1", c, 1))
                            dve.sem_inc(q["h_ready"], 1)
                        bank, read = filled_qa(dve, p, n, ("W2",))
                        dve.scalar_tensor_tensor(out=xn[:, before, :], in0=bank, scalar=par[:, 2:3], in1=xn[:, before, :],
                                                 op0=ALU.add, op1=ALU.add).then_inc(read, 1)
                        is_read(dve, p, n, "qa", ("W2",))
                        dve.sem_inc(q["ff_done"], 1)

                    for step, ff in p["steps"]:
                        ff = {k for k, _, _ in ff}
                        if "tok" in ff:
                            normalise()
                        x = {kind: (t, n - back) for kind, t, back in step}
                        if "Z" in x:
                            sum_p(*x["Z"])
                        if new is not None and "X" in x and x["X"][0] == 0:
                            dve.wait_ge(q["tabs"], BASE + new + 1)
                            settle(dve, q["held"])
                        if "X" in x:
                            rotate(x["X"][0])
                        if "Wo" in ff:
                            add_attention()
                        if "Y" in x:
                            subtract_top(*x["Y"])
                        if "Z" in x:
                            copy_o(*x["Z"])
                        if "W" in ff:
                            feed_forward()
                    ch.end()

                passes(dve, body)
                dve.wait_ge(q["back"], BASE + 16)
                for b in range(NB):
                    dve.tensor_tensor(acc[:, b, :], acc[:, b, :], xn[:, b, :], ALU.add)


BH, BD, HOR = 16, 16, 64
HS = P // BH
NG = BH // 4
NQ = HOR // 4
DB, GR = 3, 4
PITCH = HOR + P
ZROW = 1544
DAMAGE = 10.0


def attn_stage(nc, g, d, skew):
    acc, xn, ident = g["acc"], g["xn"], g["ident"]
    with ExitStack() as ctx:
        s = Stage(nc, ctx, "at")
        w_disp = s.sb("w_disp", [P, 2 * P])
        w_val = s.sb("w_val", [P, P])
        w_proj = s.sb("w_proj", [P, P])
        w_fused = s.sb("w_fused", [P, P])
        w_red = s.sb("w_red", [P, NG, 32])
        w_pos = s.sb("w_pos", [BD, P])
        rel = s.sb("rel", [BD, HOR])
        bias = s.sb("bias", [P, 2])
        mask = s.sb("mask", [P, HOR])
        pos = s.sb("pos", [P, HOR])
        xp = s.sb("xp", [P, HOR + L + 1])
        disp = s.sb("disp", [P, 2, L])
        fp = s.sb("fp", [P, NG, HOR + L])
        df = s.sb("df", [P, DB, NG, L])
        ge = s.sb("ge", [P, GR, NG, L])
        lt = s.sb("lt", [P, 2, L])
        th = s.sb("th", [P, NT, 4, BH])
        lg = s.sb("lg", [P, NT, BH, HOR])
        pn = s.sb("pn", [P, NT, BH, HOR])
        mx = s.sb("mx", [P, NT, BH])
        rsum = s.sb("rsum", [P, NT, BH])
        va = s.sb("va", [P, NT, 4, 4, 32])
        vb = s.sb("vb", [HOR, NT, 4, 4, 32])
        band = s.sb("band", [P, 2, BH, PITCH])
        ba = s.sb("ba", [P, BH, P])
        bb = s.sb("bb", [HOR, BH, P])
        oT = s.sb("oT", [P, L])
        zero = band[:, 0, :, :].rearrange("p h c -> p (h c)")[:, 0:ZROW]
        LT = s.banks("LT", 2)
        TK = s.banks("TK", 2)
        TB = s.banks("TB", 2)
        O = s.banks("O", 1)
        X = s.banks("X", 1)
        q = s.sems("loaded zeroed cleared pos_fill pos_ready dbias xp_ready tb_fill tb_read0 tb_read1 disp_ready f_ready "
                   "d_ready g_ready red_done lt_ready tk_fill th_ready lg_part sub_done exp_done sum_done norm_done band_free pv_ready "
                   "pv_done ot_ready pr_fill acc_done dch held wr0 wr1 wr2 wr3 rd0 rd1 rd2 rd3 v_ready")
        tb_read = [q["tb_read0"], q["tb_read1"]]
        wr, rd = ([q[f"{n}{t}"] for t in range(NT)] for n in ("wr", "rd"))

        def a_pass(own, tail):
            keys = [("disp", k) for k in range(2)] + [("F", k) for k in range(NG)] if own else []
            keys += [(k, t, j) for t in range(NT) for j in range(4) for k in ("A", "B")] if tail else []
            keys += [("V", k) for k in range(2)] if own else []
            return {"own": own, "tail": tail, "tb": {key: n for n, key in enumerate(keys)}, "before": 0}

        first, loop, last = a_pass(True, False), a_pass(True, True), a_pass(False, True)
        TN = len(loop["tb"])
        loop["before"] = last["before"] = -len(last["tb"])

        def batches(eng, body):
            body(first, 0)
            with eng.Fori(1, NB) as b:
                body(loop, b)
            body(last, NB)

        def fill(pe, p, b, key):
            k = p["tb"][key]
            pe.wait_ge(tb_read[k % 2], BASE + b * (TN // 2) + (p["before"] // 2 + k // 2))
            if key[0] == "B":
                settle(pe, q["held"])
            return TB[:, k % 2, :]

        def filled(eng, p, b, key):
            k = p["tb"][key]
            eng.wait_ge(q["tb_fill"], BASE + b * TN + (p["before"] + k + 1))
            return TB[:, k % 2, :], tb_read[k % 2]

        def read(eng, p, b, keys):
            for key in keys:
                k = p["tb"][key]
                eng.wait_ge(tb_read[k % 2], BASE + b * (TN // 2) + (p["before"] // 2 + k // 2 + 1))

        TURN = {12 + 12 * t + 2 * j: (t, j) for t in range(NT) for j in range(4)}
        PV = {12 + 12 * t + 12: t for t in range(NT)}
        SUB, EXP, SUM = {0: 2, 2: 3}, 4, {5 + 2 * t: t for t in range(NT)}

        loads = ((w_disp, "a_w_disp"), (w_val, "a_w_val"), (w_proj, "a_w_proj"), (w_fused, "a_w_fused"),
                 (w_red, "a_w_red"), (w_pos, "a_w_pos"), (rel, "a_rel"), (bias, "a_bias"), (mask, "a_mask"))
        flat = skew.rearrange("t h (a n) -> (t h a) n", n=ZROW)
        with nc.Block() as block:
            @block.sync
            def _(sp):
                for dst, src in loads:
                    sp.dma_start(dst[:], d[src]).then_inc(q["loaded"], 16)
                sp.wait_ge(q["zeroed"], BASE + 1)
                for k in range(flat.shape[0] // P):
                    sp.dma_start(flat[k * P:(k + 1) * P, :], zero).then_inc(q["cleared"], 16)
                sp.wait_ge(q["cleared"], BASE + 16 * (flat.shape[0] // P))
                with sp.Fori(0, NB) as b:
                    for t in range(NT):
                        sp.wait_ge(rd[t], BASE + b * 16)
                        settle(sp, q["held"])
                        sp.wait_ge(q["norm_done"], BASE + b * NT + t + 1)
                        settle(sp, q["held"])
                        sp.dma_start(skew[t].rearrange("h (t c) -> t h c", c=PITCH + 1)[:, :, 0:HOR],
                                     pn[:, t, :, :]).then_inc(wr[t], 16)
                        sp.wait_ge(wr[t], BASE + (b + 1) * 16)
                        settle(sp, q["held"])
                        sp.wait_ge(q["band_free"], BASE + b * NT + t - 1)
                        sp.dma_start(band[:, t % 2, :, :],
                                     skew[t][:, 0:P * PITCH].rearrange("h (t c) -> t h c", c=PITCH)).then_inc(rd[t], 16)

            @block.gpsimd
            def _(pool):
                pool.memset(xp[:, :], 0.0)
                pool.memset(va[:], 0.0)
                pool.memset(vb[:], 0.0)
                pool.memset(fp[:, :, 0:HOR], 0.0)
                pool.memset(zero, 0.0).then_inc(q["zeroed"], 1)
                pool.wait_ge(q["loaded"], BASE + 16 * len(loads))
                pool.tensor_scalar(bias[:, 1:2], bias[:, 1:2], 0.5, None, ALU.mult).then_inc(q["dbias"], 1)
                with pool.Fori(0, NB) as b:
                    for t in range(NT):
                        pool.wait_ge(q["sum_done"], BASE + b * NT + t + 1)
                        pool.tensor_tensor(pn[:, t, :, :], pn[:, t, :, :],
                                           rsum[:, t, :].unsqueeze(2).broadcast_to([P, BH, HOR]), ALU.mult).then_inc(q["norm_done"], 1)

            @block.scalar
            def _(act):
                act.wait_ge(q["pos_fill"], BASE + 1)
                act.activation(pos[:, :], X[:, 0, 0:HOR], ACT.Identity, bias=bias[:, 0:1]).then_inc(q["pos_ready"], 1)
                act.wait_ge(q["pos_ready"], BASE + 1)
                act.wait_ge(q["dbias"], BASE + 1)
                act.wait_ge(q["zeroed"], BASE + 1)

                def body(p, b):
                    m = b - 1
                    own, tail = p["own"], p["tail"]

                    def project():
                        for k in range(2):
                            bank, r = filled(act, p, b, ("disp", k))
                            act.activation(disp[:, k, :], bank, ACT.Copy).then_inc(r, 1)
                        read(act, p, b, [("disp", 0), ("disp", 1)])
                        act.sem_inc(q["disp_ready"], 1)
                        for k in range(NG):
                            bank, r = filled(act, p, b, ("F", k))
                            act.activation(fp[:, k, HOR:], bank, ACT.Copy).then_inc(r, 1)
                        read(act, p, b, [("F", NG - 2), ("F", NG - 1)])
                        act.sem_inc(q["f_ready"], 1)

                    def values():
                        act.wait_ge(q["pv_done"], BASE + b * NT)
                        for k, dst in enumerate((va, vb)):
                            bank, r = filled(act, p, b, ("V", k))
                            for i in range(4):
                                ins = act.activation(dst[:, :, :, i, HS * i:HS * (i + 1)],
                                                     bank[0:dst.shape[0], :].rearrange("p (t h m e) -> p t h m e", t=NT, m=4, e=HS)[:, :, :, i, :],
                                                     ACT.Copy)
                            ins.then_inc(r, 1)
                        read(act, p, b, [("V", 0), ("V", 1)])
                        act.sem_inc(q["v_ready"], 1)

                    def keep(n, c):
                        act.wait_ge(q["red_done"], BASE + n * (HOR // 2) + 2 * (c + 1))
                        act.wait_ge(q["tk_fill"], BASE + n * NQ + (c - 1))
                        act.activation(lt[:, c % 2, :], LT[:, c % 2, :], ACT.Copy).then_inc(q["lt_ready"], 1)

                    def damage(n, c):
                        act.wait_ge(q["tk_fill"], BASE + n * NQ + c + 1)
                        act.wait_ge(q["lg_part"], BASE + n * NQ + c)
                        act.activation(th[:].rearrange("p t w (g h) -> p (t w g) h", h=4),
                                       TK[:, c % 2, :].rearrange("p (n y h) -> p n y h", y=2, h=4)[:, :, 1, :],
                                       ACT.Tanh, scale=0.5, bias=bias[:, 1:2]).then_inc(q["th_ready"], 1)

                    def turned(k, t, j):
                        if (k, j) == ("A", 0):
                            act.wait_ge(q["pv_done"], BASE + m * NT + t)
                        dst = ba if k == "A" else bb
                        bank, r = filled(act, p, b, (k, t, j))
                        act.activation(dst[:, 4 * j:4 * j + 4, :],
                                       bank[0:dst.shape[0], :].rearrange("p (h x) -> p h x", x=P), ACT.Copy).then_inc(r, 1)
                        if (k, j) == ("B", 3):
                            read(act, p, b, [("A", t, 3), ("B", t, 3)])
                            act.sem_inc(q["pv_ready"], 1)

                    if tail:
                        keep(m, NQ - 1)
                    if own:
                        act.wait_ge(q["v_ready"], BASE + b)
                        settle(act, q["held"])
                        act.activation(xp[:, HOR:HOR + L], xn[:, b, :], ACT.Copy).then_inc(q["xp_ready"], 1)
                    if tail:
                        damage(m, NQ - 2)
                        damage(m, NQ - 1)
                    if own:
                        project()
                    for w in range(HOR):
                        if own:
                            act.wait_ge(q["d_ready"], BASE + b * HOR + w + 1)
                            act.wait_ge(q["red_done"], BASE + b * (HOR // 2) + (w // 2 - 1))
                            act.activation(ge[:, w % GR, :, :], df[:, w % DB, :, :], ACT.Gelu,
                                           bias=pos[:, w:w + 1]).then_inc(q["g_ready"], 1)
                            if w >= 4 and w % 4 == 1:
                                keep(b, w // 4 - 1)
                            if w >= 8 and w % 4 == 0:
                                damage(b, w // 4 - 2)
                        if tail and w == EXP:
                            for t in range(NT):
                                act.wait_ge(q["sub_done"], BASE + m * NT + t + 1)
                                act.wait_ge(wr[t], BASE + m * 16)
                                act.activation(pn[:, t, :, :], lg[:, t, :, :], ACT.Exp).then_inc(q["exp_done"], 1)
                        for lag, k in ((2, "A"), (3, "B")):
                            if tail and w - lag in TURN:
                                turned(k, *TURN[w - lag])
                        if tail and w == HOR - 3:
                            act.wait_ge(q["pv_done"], BASE + (m + 1) * NT)
                            act.wait_ge(q["pr_fill"], BASE + m)
                            act.activation(oT[:, :], O[:, 0, :], ACT.Copy).then_inc(q["ot_ready"], 1)
                    if own:
                        values()

                batches(act, body)

            @block.tensor
            def _(pe):
                pe.wait_ge(q["loaded"], BASE + 16 * len(loads))
                pe.matmul(X[:, 0, 0:HOR], w_pos[:, :], rel[:, :], start=True, stop=True).then_inc(q["pos_fill"], 1)

                def body(p, b):
                    m = b - 1
                    own, tail = p["own"], p["tail"]

                    def project():
                        pe.wait_ge(q["xp_ready"], BASE + b + 1)
                        for k in range(2):
                            bank = fill(pe, p, b, ("disp", k))
                            pe.matmul(bank, w_disp[:, k * P:(k + 1) * P], xp[:, HOR:HOR + L], start=True,
                                      stop=True).then_inc(q["tb_fill"], 1)
                        pe.wait_ge(q["disp_ready"], BASE + b + 1)
                        for k in range(NG):
                            bank = fill(pe, p, b, ("F", k))
                            rows = slice(64 * (k % 2), 64 * (k % 2) + 64)
                            pe.matmul(bank, w_fused[rows, :], disp[rows, k // 2, :], start=True,
                                      stop=True).then_inc(q["tb_fill"], 1)

                    def values():
                        for k, rows in enumerate((P, HOR)):
                            bank = fill(pe, p, b, ("V", k))
                            for t in range(NT):
                                c0 = t * P + 1 + k * P
                                mm = pe.matmul(bank[0:rows, t * P:(t + 1) * P], xp[:, c0:c0 + rows], w_val[:, :],
                                               start=True, stop=True)
                            mm.then_inc(q["tb_fill"], 1)

                    def turn(n, c):
                        pe.wait_ge(q["lt_ready"], BASE + n * NQ + c + 1)
                        pe.wait_ge(q["lg_part"], BASE + n * NQ + (c - 1))
                        for t in range(NT):
                            mm = pe.transpose(TK[:, c % 2, t * P:(t + 1) * P], lt[:, c % 2, t * P:(t + 1) * P], ident[:, :])
                        mm.then_inc(q["tk_fill"], 1)

                    def turn_band(t, j):
                        if j == 0:
                            pe.wait_ge(rd[t], BASE + (m + 1) * 16)
                        for k, rows in (("A", P), ("B", HOR)):
                            bank = fill(pe, p, b, (k, t, j))
                            c0 = 0 if k == "A" else P
                            for i in range(4):
                                mm = pe.transpose(bank[0:rows, i * P:(i + 1) * P], band[:, t % 2, 4 * j + i, c0:c0 + rows], ident[:, :])
                            mm.then_inc(q["tb_fill"], 1)
                        if j == 3:
                            pe.wait_ge(q["tb_fill"], BASE + b * TN + (p["before"] + p["tb"][("B", t, 3)] + 1))
                            pe.sem_inc(q["band_free"], 1)

                    def attend(t):
                        pe.wait_ge(q["v_ready"], BASE + m + 1)
                        pe.wait_ge(q["pv_ready"], BASE + m * NT + t + 1)
                        settle(pe, q["held"])
                        for i in range(4):
                            for k, (val, bnd) in enumerate(((va, ba), (vb, bb))):
                                for h in range(4):
                                    mm = pe.matmul(O[32 * h:32 * h + 32, 0, t * P:(t + 1) * P], val[:, t, h, i, :],
                                                   bnd[:, 4 * h + i, :], start=(i == 0 and k == 0),
                                                   stop=(i == 3 and k == 1), skip_group_check=True)
                        mm.then_inc(q["pv_done"], 1)

                    if tail:
                        turn(m, NQ - 1)
                    if own:
                        project()
                    for w in range(0, HOR, 2):
                        c = w // 4
                        if own and w >= 4 and w % 4 == 2:
                            turn(b, c - 1)
                        if tail and w in TURN:
                            turn_band(*TURN[w])
                        if tail and w in PV:
                            attend(PV[w])
                        if tail and w == HOR - 2:
                            pe.wait_ge(q["ot_ready"], BASE + m + 1)
                            pe.wait_ge(q["acc_done"], BASE + m)
                            pe.matmul(X[:, 0, :], w_proj[:, :], oT[:, :], start=True, stop=True).then_inc(q["pr_fill"], 1)
                        if own:
                            pe.wait_ge(q["lt_ready"], BASE + b * NQ + (c - 1))
                            pe.wait_ge(q["g_ready"], BASE + b * HOR + w + 2)
                            for k in range(NG):
                                for i in (w, w + 1):
                                    r0 = 32 * (i % 4)
                                    mm = pe.matmul(LT[r0:r0 + 32, c % 2, :], w_red[:, k, :], ge[:, i % GR, k, :],
                                                   start=(k == 0), stop=(k == NG - 1), skip_group_check=True)
                            mm.then_inc(q["red_done"], 1)
                    if own:
                        values()

                batches(pe, body)

            @block.vector
            def _(dve):
                dve.wait_ge(q["loaded"], BASE + 16 * len(loads))

                def body(p, b):
                    m = b - 1
                    own, tail = p["own"], p["tail"]
                    ch = Chain(dve, q["dch"], 1 + 4 * NT)
                    if tail:
                        ch.start(m)

                    def logits(n, c):
                        dve.wait_ge(q["th_ready"], BASE + n * NQ + c + 1)
                        dve.wait_ge(q["exp_done"], BASE + n * NT)
                        for t in range(NT):
                            ins = dve.scalar_tensor_tensor(
                                out=lg[:, t, :, 4 * c:4 * c + 4].rearrange("p (g h) w -> p w g h", h=4),
                                in0=th[:, t, :, :].rearrange("p w (g h) -> p w g h", h=4), scalar=-DAMAGE / 2,
                                in1=TK[:, c % 2, t * P:(t + 1) * P].rearrange("p (w g y h) -> p w g y h", w=4, y=2, h=4)[:, :, :, 0, :],
                                op0=ALU.mult, op1=ALU.add)
                        ins.then_inc(q["lg_part"], 1)

                    def subtract_top(t):
                        if t == 0:
                            dve.wait_ge(q["lg_part"], BASE + (m + 1) * NQ)
                            ch.link(dve.tensor_tensor(lg[:, 0, :, :], lg[:, 0, :, :],
                                                      mask[:, :].unsqueeze(1).broadcast_to([P, BH, HOR]), ALU.add))
                        ch.link(dve.tensor_reduce(mx[:, t, :], lg[:, t, :, :], AX, ALU.max))
                        ch.link(dve.tensor_tensor(lg[:, t, :, :], lg[:, t, :, :],
                                                  mx[:, t, :].unsqueeze(2).broadcast_to([P, BH, HOR]), ALU.subtract))
                        dve.sem_inc(q["sub_done"], 1)

                    def sums(t):
                        dve.wait_ge(q["exp_done"], BASE + m * NT + t + 1)
                        dve.wait_ge(q["norm_done"], BASE + m * NT + (t + 1 - NT))
                        ch.link(dve.tensor_reduce(rsum[:, t, :], pn[:, t, :, :], AX, ALU.add))
                        ch.link(dve.reciprocal(rsum[:, t, :], rsum[:, t, :]))
                        dve.sem_inc(q["sum_done"], 1)

                    if tail:
                        logits(m, NQ - 2)
                        logits(m, NQ - 1)
                        subtract_top(0)
                        subtract_top(1)
                    if own:
                        dve.wait_ge(q["f_ready"], BASE + b + 1)
                    for w in range(HOR):
                        if own:
                            dve.wait_ge(q["g_ready"], BASE + b * HOR + max(w - DB + 1, 0))
                            dve.tensor_tensor(df[:, w % DB, :, :], fp[:, :, w + 1:w + 1 + L], fp[:, :, HOR:],
                                              ALU.subtract).then_inc(q["d_ready"], 1)
                            if w >= 8 and w % 4 == 3:
                                logits(b, w // 4 - 2)
                        if tail and w in SUB:
                            subtract_top(SUB[w])
                        if tail and w in SUM:
                            sums(SUM[w])
                    if tail:
                        dve.wait_ge(q["pr_fill"], BASE + m + 1)
                        dve.tensor_tensor(acc[:, m, :], acc[:, m, :], X[:, 0, :], ALU.add).then_inc(q["acc_done"], 1)
                        ch.end()

                batches(dve, body)


NE, NI, NTOP, GROUPS, GTOP = 64, 64, 6, 8, 4
NCK = NE * NI // P
EH = NE // 2
LOW, TAKEN = -1e30, 3e30


def moe_stage(nc, g, d, out):
    acc, xn, ident = g["acc"], g["xn"], g["ident"]
    with ExitStack() as ctx:
        s = Stage(nc, ctx, "mo")
        w_g = s.sb("w_g", [P, NCK + 1, P])
        w_u = s.sb("w_u", [P, NCK + 1, P])
        w_d = s.sb("w_d", [P, NCK + 1, P])
        w_r = s.sb("w_r", [P, NE])
        gb = s.sb("gb", [P, NE])
        comb_t = s.sb("comb_t", [3 * EH, 2, NB, L], BF16)
        pick = s.sb("pick", [3 * EH, EH, NI], BF16)
        ident_b = s.sb("ident_b", [P, P], BF16)
        parts = s.sb("parts", [P, NT, 2, 3, EH], BF16)
        rest = s.sb("rest", [P, NT, NE])
        xc = s.sb("xc", [P, L])
        sc = s.sb("sc", [P, NT, NE])
        gv = s.sb("gv", [P, NT, 2 * GROUPS])
        ev = s.sb("ev", [P, NT, NE + 8])
        gsel = s.sb("gsel", [P, NT, 2 * GROUPS])
        esel = s.sb("esel", [P, NT, NE + 8])
        top = s.sb("top", [P, NT, 8])
        comb = s.sb("comb", [P, NT, NE])
        wsum = s.sb("wsum", [P, NT])
        sg = s.sb("sg", [P, 2, L])
        h1 = s.sb("h1", [P, L])
        h2 = s.sb("h2", [P, 2, L])
        G = s.banks("G", 2)
        U = s.banks("U", 2)
        C = s.banks("C", 2)
        R = s.banks("R", 1)
        X = s.banks("X", 1)
        q = s.sems("loaded w_in x_ready lo_fill sc_ready picked lows comb_ready ct_fill ct_ready g_fill uc_fill sg_ready "
                   "h1_ready h_ready d_done saved stored dch held rch")
        TURN = [19, 22]
        with nc.Block() as block:
            @block.sync
            def _(sp):
                for dst, src in ((w_r, "e_w_r"), (gb, "e_gb")):
                    sp.dma_start(dst[:], d[src]).then_inc(q["loaded"], 16)
                for dst, src in ((w_g, "e_w_g"), (w_u, "e_w_u"), (w_d, "e_w_d")):
                    sp.dma_start(dst[:], d[src]).then_inc(q["w_in"], 16)
                with sp.Fori(0, NB) as b:
                    sp.wait_ge(q["saved"], BASE + b + 1)
                    settle(sp, q["held"])
                    sp.dma_start(out[:, b, :], acc[:, b, :]).then_inc(q["stored"], 16)
                sp.wait_ge(q["stored"], BASE + 16 * NB)

            @block.gpsimd
            def _(pool):
                pool.tensor_copy(ident_b[:, :], ident[:, :])
                pool.memset(gv[:], LOW)
                pool.memset(ev[:], LOW).then_inc(q["lows"], 1)
                pool.wait_ge(q["lows"], BASE + 1)
                for k in range(3):
                    rows = slice(k * EH, (k + 1) * EH)
                    pool.tensor_copy(pick[rows, :, :], ident[rows, rows].unsqueeze(2).broadcast_to([EH, EH, NI])
                                     ).then_inc(q["picked"], 1)
                    pool.wait_ge(q["picked"], BASE + k + 1)

            def batches(eng, route, experts):
                for c in range(NCK + 1):
                    route(0, c)
                with eng.Fori(0, NB - 1) as b:
                    experts(b, route)
                experts(NB - 1, lambda b, c: None)

            @block.scalar
            def _(act):
                def route(b, c):
                    if c == 1:
                        act.wait_ge(q["lo_fill"], BASE + b)
                        settle(act, q["held"])
                        act.activation(xc[:, :], xn[:, b, :], ACT.Copy).then_inc(q["x_ready"], 1)
                    if c == 5:
                        act.wait_ge(q["lo_fill"], BASE + b + 1)
                        act.wait_ge(q["comb_ready"], BASE + b)
                        act.activation(sc[:], X[:, 0, 0:NT * NE].rearrange("p (t e) -> p t e", e=NE),
                                       ACT.Sigmoid).then_inc(q["sc_ready"], 1)
                    if c in TURN:
                        k = TURN.index(c)
                        act.wait_ge(q["ct_fill"], BASE + b * 2 + k + 1)
                        settle(act, q["held"])
                        act.activation(comb_t[:, k, b, :], X[0:3 * EH, 0, :], ACT.Copy).then_inc(q["ct_ready"], 1)

                def experts(b, route):
                    for c in range(NCK + 1):
                        n = b * (NCK + 1) + c
                        act.wait_ge(q["g_fill"], BASE + n + 1)
                        act.wait_ge(q["h1_ready"], BASE + n - 1)
                        act.activation(sg[:, c % 2, :], G[:, c % 2, :], ACT.Silu).then_inc(q["sg_ready"], 1)
                        route(b + 1, c)
                    act.wait_ge(q["h1_ready"], BASE + (b + 1) * (NCK + 1))

                batches(act, route, experts)

            @block.tensor
            def _(pe):
                pe.wait_ge(q["loaded"], BASE + 32)

                def route(b, c):
                    if c == 3:
                        pe.wait_ge(q["x_ready"], BASE + b + 1)
                        pe.wait_ge(q["ct_ready"], BASE + b * 2)
                        for t in range(NT):
                            mm = pe.matmul(X[:, 0, t * NE:(t + 1) * NE], xc[:, t * P:(t + 1) * P], w_r[:, :], start=True, stop=True)
                        mm.then_inc(q["lo_fill"], 1)
                    if c + 2 in TURN:
                        k = TURN.index(c + 2)
                        pe.wait_ge(q["comb_ready"], BASE + b + 1)
                        pe.wait_ge(q["ct_ready"], BASE + b * 2 + k)
                        settle(pe, q["held"])
                        for t in range(NT):
                            mm = pe.matmul(X[0:3 * EH, 0, t * P:(t + 1) * P],
                                           parts[:, t, k, :, :].rearrange("p k e -> p (k e)"), ident_b[:, :],
                                           start=True, stop=True)
                        mm.then_inc(q["ct_fill"], 1)

                def experts(b, route):
                    def up(c):
                        n = b * (NCK + 1) + c
                        pe.wait_ge(q["sg_ready"], BASE + n - 1)
                        pe.matmul(G[:, c % 2, :], w_g[:, c, :], xn[:, b, :], start=True, stop=True).then_inc(q["g_fill"], 1)
                        pe.wait_ge(q["h_ready"], BASE + n - 1)
                        mm = pe.matmul(U[:, c % 2, :], w_u[:, c, :], xn[:, b, :], start=True, stop=True)
                        if c < NCK:
                            e0 = 2 * c % EH
                            mm = pe.matmul(C[:, c % 2, :], pick[:, e0:e0 + 2, :].rearrange("k e i -> k (e i)"),
                                           comb_t[:, 2 * c // EH, b, :], start=True, stop=True)
                        mm.then_inc(q["uc_fill"], 1)

                    def down(c):
                        n = b * (NCK + 1) + c
                        pe.wait_ge(q["h_ready"], BASE + n + 1)
                        if c == 0:
                            pe.wait_ge(q["saved"], BASE + b)
                        pe.matmul(R[:, 0, :], w_d[:, c, :], h2[:, c % 2, :], start=(c == 0),
                                  stop=(c == NCK)).then_inc(q["d_done"], 1)

                    pe.wait_ge(q["h_ready"], BASE + b * (NCK + 1))
                    pe.wait_ge(q["ct_ready"], BASE + b * 2 + 2)
                    settle(pe, q["held"])
                    for c in range(NCK + 1):
                        up(c)
                        if c >= 1:
                            down(c - 1)
                        route(b + 1, c)
                    down(NCK)

                def weights(b, c):
                    route(b, c)
                    if isinstance(b, int) and c == NCK:
                        pe.wait_ge(q["w_in"], BASE + 48)
                        pe.wait_ge(q["picked"], BASE + 3)

                batches(pe, weights, experts)

            @block.vector
            def _(dve):
                ch = Chain(dve, q["rch"], 16)
                dve.wait_ge(q["loaded"], BASE + 32)
                dve.wait_ge(q["lows"], BASE + 1)

                def first_of(values, sel, n):
                    settle(dve, q["held"])
                    for t in range(NT):
                        ins = dve.max(top[:, t, :], values[:, t, :])
                    ch.link(ins)
                    ch.link(dve.memset(top[:, :, n:8], LOW))
                    settle(dve, q["held"])
                    for t in range(NT):
                        ins = dve.match_replace(sel[:, t, :], top[:, t, :], values[:, t, :], TAKEN)
                    ch.link(ins)

                def route(b, c):
                    if c == 6:
                        ch.start(b)
                        dve.wait_ge(q["sc_ready"], BASE + b + 1)
                        ch.link(dve.tensor_tensor(sc[:], sc[:], gb[:, :].unsqueeze(1).broadcast_to([P, NT, NE]), ALU.add))
                        ch.link(dve.tensor_reduce(gv[:, :, 0:GROUPS], sc[:].rearrange("p t (g e) -> p t g e", g=GROUPS), AX, ALU.max))
                    if c == 8:
                        first_of(gv, gsel, GTOP)
                    if c == 9:
                        ch.link(dve.tensor_scalar(gsel[:], gsel[:], -LOW, None, ALU.is_ge))
                        for t in range(NT):
                            ins = dve.tensor_tensor(ev[:, t, 0:NE].rearrange("p (g e) -> p g e", g=GROUPS),
                                                    sc[:, t, :].rearrange("p (g e) -> p g e", g=GROUPS),
                                                    gsel[:, t, 0:GROUPS].unsqueeze(2).broadcast_to([P, GROUPS, NE // GROUPS]), ALU.mult)
                        ch.link(ins)
                    if c == 11:
                        first_of(ev, esel, NTOP)
                    if c == 12:
                        ins = dve.scalar_tensor_tensor(out=comb[:], in0=esel[:, :, 0:NE], scalar=-LOW, in1=ev[:, :, 0:NE],
                                                       op0=ALU.is_ge, op1=ALU.mult)
                        ch.link(ins)
                    if c == 13:
                        dve.tensor_reduce(wsum[:, :], comb[:], AX, ALU.add).then_inc(q["dch"], 1)
                        dve.wait_ge(q["dch"], BASE + 3 * b + 1)
                        dve.tensor_scalar(wsum[:, :], wsum[:, :], 1e-8, None, ALU.add).then_inc(q["dch"], 1)
                        dve.wait_ge(q["dch"], BASE + 3 * b + 2)
                        dve.reciprocal(wsum[:, :], wsum[:, :]).then_inc(q["dch"], 1)
                        dve.wait_ge(q["dch"], BASE + 3 * b + 3)
                        ch.link(dve.tensor_tensor(comb[:], comb[:], wsum[:, :].unsqueeze(2).broadcast_to([P, NT, NE]), ALU.mult))
                    halves = lambda x: x.rearrange("p t (k e) -> p t k e", e=EH)
                    if c == 14:
                        dve.wait_ge(q["ct_fill"], BASE + b * 2)
                        ch.link(dve.tensor_copy(parts[:, :, :, 0, :], halves(comb[:])))
                        ch.link(dve.tensor_tensor(halves(rest[:]), halves(comb[:]), parts[:, :, :, 0, :], ALU.subtract))
                    if c == 15:
                        ch.link(dve.tensor_copy(parts[:, :, :, 1, :], halves(rest[:])))
                        ch.link(dve.tensor_tensor(parts[:, :, :, 2, :], halves(rest[:]), parts[:, :, :, 1, :], ALU.subtract))
                        dve.sem_inc(q["comb_ready"], 1)
                        ch.end()

                def experts(b, route):
                    for c in range(NCK + 1):
                        n = b * (NCK + 1) + c
                        dve.wait_ge(q["sg_ready"], BASE + n + 1)
                        dve.wait_ge(q["uc_fill"], BASE + n + 1)
                        dve.wait_ge(q["d_done"], BASE + n - 1)
                        if c < NCK:
                            dve.tensor_tensor(h1[:, :], sg[:, c % 2, :], U[:, c % 2, :], ALU.mult).then_inc(q["h1_ready"], 1)
                            dve.wait_ge(q["h1_ready"], BASE + n + 1)
                            dve.tensor_tensor(h2[:, c % 2, :], h1[:, :], C[:, c % 2, :], ALU.mult).then_inc(q["h_ready"], 1)
                            dve.wait_ge(q["h_ready"], BASE + n + 1)
                        else:
                            dve.tensor_tensor(h2[:, c % 2, :], sg[:, c % 2, :], U[:, c % 2, :], ALU.mult).then_inc(q["h1_ready"], 1)
                            dve.wait_ge(q["h1_ready"], BASE + n + 1)
                            dve.sem_inc(q["h_ready"], 1)
                        route(b + 1, c)
                    dve.wait_ge(q["d_done"], BASE + (b + 1) * (NCK + 1))
                    settle(dve, q["held"])
                    dve.tensor_tensor(acc[:, b, :], acc[:, b, :], R[:, 0, :], ALU.add).then_inc(q["saved"], 1)

                batches(dve, route, experts)


def rotary_tables():
    f = np.float32
    half = np.arange(0, DH, 2, dtype=f)
    freqs = np.arange(L, dtype=f)[:, None] * (f(1) / f(10000) ** (half / f(DH)))[None, :]
    power = (np.arange(L, dtype=f) - f(L // 2)) / f(WIN // 2)
    scale = ((half + f(0.4 * DH)) / f(1.4 * DH))[None, :] ** power[:, None]
    cos, sin = np.cos(freqs), np.sin(freqs)
    pair = lambda lo, hi: np.concatenate([lo, hi], axis=1)
    k = f(1) / scale
    t = np.stack([pair(cos * scale, cos * scale), pair(cos * k, cos * k),
                  pair(-sin * scale, sin * scale), pair(-sin * k, sin * k)])
    return np.ascontiguousarray(t.reshape(4, NT, P, DH).transpose(2, 0, 1, 3).astype(f))


def window_masks():
    a, key = (np.arange(P) % WIN)[:, None], np.arange(2 * WIN)[None, :]
    seen = (key >= a) & (key <= a + WIN)
    first = seen & ~((np.arange(P)[:, None] < WIN) & (key < WIN))
    return np.ascontiguousarray(np.where(np.stack([first, seen], axis=1), 0.0, -1e30).astype(np.float32))


def program(nc, d, out):
    with ExitStack() as ctx:
        g = {}
        g["acc"] = ctx.enter_context(nc.sbuf_tensor("acc", [P, NB, L], F32))
        g["xn"] = ctx.enter_context(nc.sbuf_tensor("xn", [P, NB, L], F32))
        g["ident"] = ctx.enter_context(nc.sbuf_tensor("ident", [P, P], F32))
        loaded = ctx.enter_context(nc.semaphore("x_loaded"))
        with nc.Block() as block:
            @block.sync
            def _(sp):
                sp.dma_start(g["ident"][:, :], d["ident"]).then_inc(loaded, 16)
                sp.dma_start(g["acc"][:, :, :], d["x"]).then_inc(loaded, 16)
                sp.wait_ge(loaded, 32)
        layernorm_stage(nc, g, "ln0")
        mamba_stage(nc, g, d)
        ffn_stage(nc, g, d, nc.dram_tensor("park", (P, NB, L), F32).ap())
        layernorm_stage(nc, g, "ln1")
        attn_stage(nc, g, d, nc.dram_tensor("skew", (NT, BH, P * (PITCH + 1)), F32).ap())
        moe_stage(nc, g, d, out)


def layouts(i):
    T = np.ascontiguousarray
    a = {}
    a["ident"] = np.eye(P, dtype=np.float32)
    a["x"] = T(i["L0_attn_x"].reshape(NB, L, P).transpose(2, 0, 1))
    halves = lambda w: T(w.reshape(2, P, -1).transpose(1, 0, 2))
    a["m_w_in"] = T(i["L0_attn_W_in"].T)
    a["m_w_x"] = halves(T(np.roll(i["L0_attn_W_x"], -DR, axis=0).T))
    a["m_w_dt"] = T(i["L0_attn_W_dt"].T)
    a["m_w_out"] = halves(T(i["L0_attn_W_out"].T))
    a["m_par"] = halves(np.concatenate([i["L0_attn_conv_w"], i["L0_attn_conv_b"][:, None],
                                        i["L0_attn_b_dt"][:, None], i["L0_attn_D"][:, None]], axis=1))
    a["m_alog"] = halves(i["L0_attn_A_log"])
    a["f_w_qkv"] = i["L0_ffn_Wqkv"].copy()
    a["f_w_qkv"][:, :, 2 * INNER:] = (i["L0_ffn_Wqkv"][:, :, 2 * INNER:].reshape(NLAYER, P, NCH, 2, DH)
                                      .transpose(0, 1, 3, 2, 4).reshape(NLAYER, P, INNER))
    a["f_w_o"] = T(i["L0_ffn_Wo"].reshape(NLAYER, NCH, P, P).transpose(0, 2, 1, 3))
    a["f_w_1"] = i["L0_ffn_W1"]
    a["f_w_2"] = np.zeros((NLAYER, P, len(FCH), P), np.float32)
    a["f_par"] = np.zeros((NLAYER, P, 3 + 2 * len(FCH)), np.float32)
    for k, name in enumerate(("ln_g", "ln_b", "b2")):
        a["f_par"][:, :, k] = i[f"L0_ffn_{name}"]
    for c, (f0, m) in enumerate(FCH):
        a["f_w_2"][:, 0:m, c, :] = i["L0_ffn_W2"][:, f0:f0 + m, :]
        a["f_par"][:, 0:m, 3 + c] = i["L0_ffn_b1"][:, f0:f0 + m]
        a["f_par"][:, 0:m, 6 + c] = i["L0_ffn_b1"][:, FF + f0:FF + f0 + m]
    qs, ks = i["L0_ffn_q_scale"], i["L0_ffn_k_scale"]
    swap = lambda w: np.concatenate([w[:, DH // 2:], w[:, :DH // 2]], axis=1)
    a["f_qk_s"] = T(np.broadcast_to(np.stack([qs, ks, swap(qs), swap(ks)], axis=1)[:, None], (NLAYER, P, 4, DH)))
    a["f_ctab"], a["f_mask"] = rotary_tables(), window_masks()
    a["a_w_disp"] = T(i["L1_attn_W_disp"].T)
    a["a_w_val"] = T(i["L1_attn_W_val"].T)
    a["a_w_proj"] = T(i["L1_attn_c_proj_w"].T)
    a["a_w_fused"] = np.zeros((2, 4, BD, 4, 2 * BD), np.float32)
    a["a_w_red"] = np.zeros((4, 2, BD, NG, NG, 2, 4), np.float32)
    a["a_w_pos"] = np.zeros((BD, 4, 2, BD), np.float32)
    for h in range(4):
        a["a_w_fused"][:, h, :, h, :] = i["L1_attn_strain_fused_w"].T
        for k in range(NG):
            a["a_w_red"][h, 0, :, k, k, 0, h] = i["L1_attn_bond_out_w"][0]
            a["a_w_red"][h, 1, :, k, k, 1, h] = i["L1_attn_damage_out_w"][0]
        a["a_w_pos"][:, h, 0, :] = i["L1_attn_pos_proj_w"].T
    a["a_w_fused"] = a["a_w_fused"].reshape(P, P)
    a["a_w_red"] = a["a_w_red"].reshape(P, NG, 32)
    a["a_w_pos"] = a["a_w_pos"].reshape(BD, P)
    a["a_rel"] = T(i["L1_attn_rel_pos_emb"].T)
    a["a_bias"] = T(np.stack([np.tile(i["L1_attn_strain_fused_b"], 4),
                              np.tile(i["L1_attn_damage_out_b"], P)], axis=1))
    t, w = np.arange(P)[:, None], np.arange(HOR)[None, :]
    a["a_mask"] = np.where(t + w >= HOR - 1, 0.0, -1e30).astype(np.float32)
    chunks = lambda w, sh: T(np.concatenate([w.reshape(NE * NI, P), sh]).reshape(NCK + 1, P, P))
    a["e_w_g"] = T(chunks(i["L1_ffn_eg_w"], i["L1_ffn_sg_w"]).transpose(2, 0, 1))
    a["e_w_u"] = T(chunks(i["L1_ffn_eu_w"], i["L1_ffn_su_w"]).transpose(2, 0, 1))
    a["e_w_d"] = T(chunks(T(i["L1_ffn_ed_w"].transpose(0, 2, 1)), i["L1_ffn_sd_w"].T).transpose(1, 0, 2))
    a["e_w_r"] = T(i["L1_ffn_gate_w"].T)
    a["e_gb"] = T(np.broadcast_to(i["L1_ffn_gate_bias"], (P, NE)))
    return a


def kernel(**inputs):
    import concourse.bacc as _bacc
    from concourse.bass_utils import run_bass_kernel_spmd as _run

    nc = _bacc.Bacc("TRN2", target_bir_lowering=False, num_devices=1)
    arrays, d = {}, {}
    for name, a in layouts({k: np.asarray(v) for k, v in inputs.items()}).items():
        arrays[f"in_{name}_dram"] = a
        d[name] = nc.dram_tensor(f"in_{name}_dram", a.shape, mybir.dt.from_np(a.dtype), kind="ExternalInput").ap()
    out = nc.dram_tensor("out_0_dram", (P, NB, L), F32, kind="ExternalOutput").ap()
    program(nc, d, out)
    r = _run(nc, [arrays], core_ids=[0])
    return np.ascontiguousarray(r.results[0]["out_0_dram"].transpose(1, 2, 0))
```
